# Optimizing a Trainium2 kernel written in Bass

```python
import numpy as np
import jax
import jax.numpy as jnp

def _softmax(x, axis=-1):
    return jax.nn.softmax(x, axis=axis)

def _gelu(x):
    return jax.nn.gelu(x, approximate=True)

def _silu(x):
    return jax.nn.silu(x)

def _sigmoid(x):
    return jax.nn.sigmoid(x)

def _layernorm(x, axis=-1, eps=1e-05):
    m = jnp.mean(x, axis=axis, keepdims=True)
    v = jnp.var(x, axis=axis, keepdims=True)
    return (x - m) / jnp.sqrt(v + eps)

def _scatter_add(tgt, idx, src, axis=0):
    return tgt.at[idx].add(src)

def _segment_sum(src, seg, n):
    return jax.ops.segment_sum(src, seg, n)
kernel_name = 'mk_decoder_postln_d1_seqx_r8_78e86b'

def setup_inputs(seed: int=0):
    np.random.seed(seed)
    _w = jnp.asarray

    def _rec_inputs():
        import jax
        import jax.numpy as jnp
        _rk = jax.random.key(seed)
        x = -0.0003929 + 0.9999 * jax.random.normal(jax.random.fold_in(_rk, 1), (16, 56, 256), jnp.float32)
        _lenS = 56 - jax.random.randint(jax.random.fold_in(_rk, 7), (16,), 0, max(1, 56 // 4) + 1, jnp.int32)
        _lenS2 = 1500 - jax.random.randint(jax.random.fold_in(_rk, 8), (16,), 0, max(1, 1500 // 4) + 1, jnp.int32)
        _ctx_2048P = jax.random.normal(jax.random.fold_in(_rk, 11), (16, 16, 256), jnp.float32)
        _ctx_2048c = jax.random.dirichlet(jax.random.fold_in(_rk, 511), 0.3 * jnp.ones((16,), jnp.float32), (16, 1500))
        _ctx_2048t = jnp.einsum('bsk,bkd->bsd', _ctx_2048c, _ctx_2048P)
        _ctx_2048t = _ctx_2048t * jax.lax.rsqrt(jnp.mean(jnp.square(_ctx_2048t)) + 1e-12) * 0.953939
        ctx_2048 = -0.000514642 + 1.00011 * (_ctx_2048t + 0.3 * jax.random.normal(jax.random.fold_in(_rk, 611), (16, 1500, 256), jnp.float32))
        _validS = jnp.arange(56)[None, :] < _lenS[:, None]
        _validS2 = jnp.arange(1500)[None, :] < _lenS2[:, None]
        _causal = jnp.tril(jnp.ones((56, 56), dtype=bool))
        mask_BxSxS2_ff0 = jnp.where(jnp.ones((16, 56, 1500), dtype=bool), 0.0, -1000000000.0).astype(jnp.float32)
        return (x, ctx_2048, mask_BxSxS2_ff0)
    x, ctx_2048, mask_BxSxS2_ff0 = _rec_inputs()

    def _L0_attn_setup():
        import jax, jax.numpy as jnp
        import numpy as np
        D_MODEL = 256
        N_HEADS = 16
        HEAD_DIM = D_MODEL // N_HEADS
        SCALE = HEAD_DIM ** (-0.5)
        key = jax.random.key(seed)
        ks = jax.random.split(key, 9)
        B, L, D = (4, 512, D_MODEL)
        s = 1.0 / np.sqrt(D)
        inp = {'x': jax.random.normal(ks[0], (B, L, D), dtype=jnp.float32)}
        inp['Wq'] = jax.random.normal(ks[1], (D, D), dtype=jnp.float32) * s
        inp['bq'] = jnp.zeros((D,), dtype=jnp.float32)
        inp['Wk'] = jax.random.normal(ks[2], (D, D), dtype=jnp.float32) * s
        inp['bk'] = jnp.zeros((D,), dtype=jnp.float32)
        inp['Wv'] = jax.random.normal(ks[3], (D, D), dtype=jnp.float32) * s
        inp['bv'] = jnp.zeros((D,), dtype=jnp.float32)
        inp['Wo'] = jax.random.normal(ks[4], (D, D), dtype=jnp.float32) * s
        inp['bo'] = jnp.zeros((D,), dtype=jnp.float32)
        return inp
    _L0_attn_all = _L0_attn_setup()
    _L0_attn_in = {k: v for k, v in _L0_attn_all.items() if k in ('Wq', 'bq', 'Wk', 'bk', 'Wv', 'bv', 'Wo', 'bo')}
    del _L0_attn_all

    def _L0_xattn_setup():
        import jax, jax.numpy as jnp
        import numpy as np
        NUM_HEADS = 16
        EPS = 1e-08

        def _dyn_quant(x):
            s = jnp.maximum(jnp.max(jnp.abs(x), axis=-1, keepdims=True) / 127.0, EPS)
            q = jnp.clip(jnp.round(x / s), -127.0, 127.0)
            return (q, s)

        def _quant_weight(w):
            s = jnp.maximum(jnp.max(jnp.abs(w), axis=1, keepdims=True) / 127.0, EPS)
            q = jnp.clip(jnp.round(w / s), -127.0, 127.0)
            return (q, s)

        def _w8a8_linear(x, w, b):
            qx, sx = _dyn_quant(x)
            qw, sw = _quant_weight(w)
            y = jnp.einsum('bnc,oc->bno', qx, qw) * (sx * sw[:, 0])
            return y + b
        key = jax.random.key(seed)
        ks = jax.random.split(key, 9)
        B, N, L, C = (2, 512, 64, 256)
        sc = 0.02
        return {'x': jax.random.normal(ks[0], (B, N, C), jnp.float32), 'cond': jax.random.normal(ks[1], (B, L, C), jnp.float32), 'mask': jnp.zeros((B, N, L), jnp.float32), 'wq': jax.random.normal(ks[2], (C, C), jnp.float32) * sc, 'bq': jnp.zeros((C,), jnp.float32), 'wk': jax.random.normal(ks[3], (C, C), jnp.float32) * sc, 'bk': jnp.zeros((C,), jnp.float32), 'wv': jax.random.normal(ks[4], (C, C), jnp.float32) * sc, 'bv': jnp.zeros((C,), jnp.float32), 'wo': jax.random.normal(ks[5], (C, C), jnp.float32) * sc, 'bo': jnp.zeros((C,), jnp.float32)}
    _L0_xattn_all = _L0_xattn_setup()
    _L0_xattn_in = {k: v for k, v in _L0_xattn_all.items() if k in ('wq', 'bq', 'wk', 'bk', 'wv', 'bv', 'wo', 'bo')}
    del _L0_xattn_all

    def _L0_ffn_setup():
        import jax, jax.numpy as jnp
        import numpy as np
        TOP_K = 2
        key = jax.random.key(seed)
        ks = jax.random.split(key, 7)
        B, S, H = (2, 256, 256)
        E, A, NS = (8, 64, 2048)
        x = jax.random.normal(ks[0], (B, S, H), jnp.float32)
        gate_w = jax.random.normal(ks[1], (E, H), jnp.float32) * 0.01
        W = jax.random.normal(ks[2], (H, H), jnp.float32) * 0.02
        atoms = jax.random.normal(ks[3], (A, NS), jnp.float32) * 0.02
        expert_atom_weights = jax.random.normal(ks[4], (E, A), jnp.float32) * 0.1
        importance = jax.random.normal(ks[5], (E, NS), jnp.float32) * 0.1
        mask_idx = jax.random.randint(ks[6], (NS,), 0, H * H, jnp.int32)
        return dict(x=x, gate_w=gate_w, W=W, atoms=atoms, expert_atom_weights=expert_atom_weights, importance=importance, mask_idx=mask_idx)
    _L0_ffn_all = _L0_ffn_setup()
    _L0_ffn_in = {k: v for k, v in _L0_ffn_all.items() if k in ('gate_w', 'W', 'atoms', 'expert_atom_weights', 'importance', 'mask_idx')}
    del _L0_ffn_all
    return {'x': x, 'ctx_2048': ctx_2048, 'mask_BxSxS2_ff0': mask_BxSxS2_ff0, 'L0_attn_Wq': _L0_attn_in['Wq'], 'L0_attn_bq': _L0_attn_in['bq'], 'L0_attn_Wk': _L0_attn_in['Wk'], 'L0_attn_bk': _L0_attn_in['bk'], 'L0_attn_Wv': _L0_attn_in['Wv'], 'L0_attn_bv': _L0_attn_in['bv'], 'L0_attn_Wo': _L0_attn_in['Wo'], 'L0_attn_bo': _L0_attn_in['bo'], 'L0_xattn_wq': _L0_xattn_in['wq'], 'L0_xattn_bq': _L0_xattn_in['bq'], 'L0_xattn_wk': _L0_xattn_in['wk'], 'L0_xattn_bk': _L0_xattn_in['bk'], 'L0_xattn_wv': _L0_xattn_in['wv'], 'L0_xattn_bv': _L0_xattn_in['bv'], 'L0_xattn_wo': _L0_xattn_in['wo'], 'L0_xattn_bo': _L0_xattn_in['bo'], 'L0_ffn_gate_w': _L0_ffn_in['gate_w'], 'L0_ffn_W': _L0_ffn_in['W'], 'L0_ffn_atoms': _L0_ffn_in['atoms'], 'L0_ffn_expert_atom_weights': _L0_ffn_in['expert_atom_weights'], 'L0_ffn_importance': _L0_ffn_in['importance'], 'L0_ffn_mask_idx': _L0_ffn_in['mask_idx']}

def reference(x, ctx_2048, mask_BxSxS2_ff0, L0_attn_Wq, L0_attn_bq, L0_attn_Wk, L0_attn_bk, L0_attn_Wv, L0_attn_bv, L0_attn_Wo, L0_attn_bo, L0_xattn_wq, L0_xattn_bq, L0_xattn_wk, L0_xattn_bk, L0_xattn_wv, L0_xattn_bv, L0_xattn_wo, L0_xattn_bo, L0_ffn_gate_w, L0_ffn_W, L0_ffn_atoms, L0_ffn_expert_atom_weights, L0_ffn_importance, L0_ffn_mask_idx):
    import jax
    import jax.numpy as jnp

    def _L0_attn_ref(x, Wq, bq, Wk, bk, Wv, bv, Wo, bo):
        import jax, jax.numpy as jnp
        import numpy as np
        D_MODEL = 256
        N_HEADS = 16
        HEAD_DIM = D_MODEL // N_HEADS
        SCALE = HEAD_DIM ** (-0.5)
        B, L, D = x.shape
        H, Hd = (N_HEADS, HEAD_DIM)
        q = jnp.einsum('bld,ed->ble', x, Wq) + bq
        k = jnp.einsum('bld,ed->ble', x, Wk) + bk
        v = jnp.einsum('bld,ed->ble', x, Wv) + bv
        phi_q = jax.nn.elu(q) + 1.0
        phi_k = jax.nn.elu(k) + 1.0
        phi_q = phi_q.reshape(B, L, H, Hd)
        phi_k = phi_k.reshape(B, L, H, Hd)
        v = v.reshape(B, L, H, Hd)
        kv_sum = jnp.cumsum(phi_k * v, axis=1)
        context = (phi_q * kv_sum).reshape(B, L, D) * SCALE
        return jnp.einsum('bld,ed->ble', context, Wo) + bo

    def _L0_xattn_ref(x, cond, mask, wq, bq, wk, bk, wv, bv, wo, bo):
        import jax, jax.numpy as jnp
        import numpy as np
        NUM_HEADS = 16
        EPS = 1e-08

        def _dyn_quant(x):
            s = jnp.maximum(jnp.max(jnp.abs(x), axis=-1, keepdims=True) / 127.0, EPS)
            q = jnp.clip(jnp.round(x / s), -127.0, 127.0)
            return (q, s)

        def _quant_weight(w):
            s = jnp.maximum(jnp.max(jnp.abs(w), axis=1, keepdims=True) / 127.0, EPS)
            q = jnp.clip(jnp.round(w / s), -127.0, 127.0)
            return (q, s)

        def _w8a8_linear(x, w, b):
            qx, sx = _dyn_quant(x)
            qw, sw = _quant_weight(w)
            y = jnp.einsum('bnc,oc->bno', qx, qw) * (sx * sw[:, 0])
            return y + b
        B, N, C = x.shape
        L = cond.shape[1]
        H = NUM_HEADS
        D = C // H
        inv_sqrt_d = np.float32(1.0 / np.sqrt(D))
        q = _w8a8_linear(x, wq, bq).reshape(B, N, H, D).transpose(0, 2, 1, 3)
        k = (cond @ wk.T + bk).reshape(B, L, H, D).transpose(0, 2, 1, 3)
        v = (cond @ wv.T + bv).reshape(B, L, H, D).transpose(0, 2, 1, 3)
        scores = jnp.einsum('bhnd,bhld->bhnl', q, k) * inv_sqrt_d + mask[:, None]
        attn = jax.nn.softmax(scores, axis=-1)
        o = jnp.einsum('bhnl,bhld->bhnd', attn, v)
        o = o.transpose(0, 2, 1, 3).reshape(B, N, C)
        return _w8a8_linear(o, wo, bo)

    def _L0_ffn_ref(x, gate_w, W, atoms, expert_atom_weights, importance, mask_idx):
        import jax, jax.numpy as jnp
        import numpy as np
        TOP_K = 2
        B, S, H = x.shape
        xt = x.reshape(-1, H)
        logits = jnp.clip(xt @ gate_w.T, -50.0, 50.0)
        top_w, top_idx = jax.lax.top_k(logits, TOP_K)
        rw = jax.nn.softmax(top_w, axis=-1)
        deltas = jax.nn.softmax(expert_atom_weights, axis=-1) @ atoms
        weighted = deltas * jax.nn.sigmoid(importance)
        rows = mask_idx // H
        cols = mask_idx % H
        vals = jnp.einsum('tk,tks->ts', rw, weighted[top_idx])
        xg = xt[:, cols]
        contrib = jax.ops.segment_sum((xg * vals).T, rows, num_segments=H)
        out = xt @ W.T + contrib.T
        return out.reshape(B, S, H)
    x = _layernorm(x + _L0_attn_ref(x, L0_attn_Wq, L0_attn_bq, L0_attn_Wk, L0_attn_bk, L0_attn_Wv, L0_attn_bv, L0_attn_Wo, L0_attn_bo), axis=-1)
    x = _layernorm(x + _L0_xattn_ref(x, ctx_2048, mask_BxSxS2_ff0, L0_xattn_wq, L0_xattn_bq, L0_xattn_wk, L0_xattn_bk, L0_xattn_wv, L0_xattn_bv, L0_xattn_wo, L0_xattn_bo), axis=-1)
    x = _layernorm(x + _L0_ffn_ref(x, L0_ffn_gate_w, L0_ffn_W, L0_ffn_atoms, L0_ffn_expert_atom_weights, L0_ffn_importance, L0_ffn_mask_idx), axis=-1)
    return x

_drawn_inputs = setup_inputs


def setup_inputs(seed=0):
    import zlib

    import numpy as np

    out = dict(_drawn_inputs(seed))
    spreads = {'L0_attn_bq': (0.0, 0.1),
     'L0_attn_bk': (0.0, 0.1),
     'L0_attn_bv': (0.0, 0.1),
     'L0_attn_bo': (0.0, 0.1),
     'L0_xattn_bq': (0.0, 0.8),
     'L0_xattn_bk': (0.0, 2.0),
     'L0_xattn_bv': (0.0, 0.1),
     'L0_xattn_bo': (0.0, 0.1)}
    factors = {'L0_xattn_wq': 8.0,
     'L0_xattn_wk': 8.0,
     'L0_ffn_gate_w': 22.036,
     'L0_ffn_atoms': 8.0,
     'L0_ffn_expert_atom_weights': 8.0,
     'L0_ffn_importance': 44.954}
    for name, (base, spread) in spreads.items():
        noise = np.random.default_rng([zlib.crc32(name.encode()), seed]).standard_normal(out[name].shape)
        drawn = base * np.exp(spread * noise) if base else spread * noise
        out[name] = jnp.asarray(drawn.astype(out[name].dtype))
    for name, factor in factors.items():
        out[name] = (out[name] * factor).astype(out[name].dtype)
    return out
```

```python
import concourse.bass as bass
from concourse import mybir
from contextlib import ExitStack

F32 = mybir.dt.float32
F32R = mybir.dt.float32r
BF16 = mybir.dt.bfloat16
I32 = mybir.dt.int32
U32 = mybir.dt.uint32
ALU = mybir.AluOpType
ACT = mybir.ActivationFunctionType
AX = mybir.AxisListType

B, S, D = 16, 56, 256
H, DH = 16, 16
L = 1500
P = 128
KT = D // P
T = B * S
TT = 2 * S
NT = T // TT
HALF = T // 2
HT = HALF // TT
LT = 125
LC = 500
NC = L // LC
TC = LC // LT
NL = L // LT
NP = H // 2
PD = 2 * DH
PN = 2 * S
GP = P // PD
SCALE = DH ** -0.5
QMAX = 127.0
QEPS = 1e-8
LN_EPS = 1e-5
ROUND = 1.5 * 2.0 ** 23
BIG = 3.0e38


def split(ap, n):
    return ap.rearrange("p (a b) -> p a b", a=n)


def self_attention_phase(nc, io, keep):
    ctx = ExitStack()
    with ctx:
        sb = lambda n, s, d=F32: ctx.enter_context(nc.sbuf_tensor(n, s, d))
        sem = lambda n: ctx.enter_context(nc.semaphore(n))
        WK, WV, WQ, WO, XK, XV, XQ = range(7)
        names = ["L0_attn_Wk", "L0_attn_Wv", "L0_attn_Wq", "L0_attn_Wo",
                 "L0_xattn_wk", "L0_xattn_wv", "L0_xattn_wq"]
        w_raw = sb("w_raw", [P, 7, KT, D])
        wT = sb("wT", [P, 4, KT, D])
        x_sb = sb("x_sb", [TT, NT, D])
        xT = sb("xT", [P, KT, T])
        qkv_bias = sb("qkv_bias", [P, 3, KT])
        neg_bias = sb("neg_bias", [P, 3, KT])
        bo_row = sb("bo_row", [TT, D])
        xbq_row = sb("xbq_row", [TT, D])
        relu_pos = sb("relu_pos", [P, 4, 2, HALF])
        relu_neg = sb("relu_neg", [P, 4, 2, HALF])
        phi = sb("phi", [P, 4, 2, HALF])
        kv = sb("kv", [P, 4, HALF])
        kv_sum = sb("kv_sum", [P, 4, HALF])
        context = sb("context", [P, KT, T])
        keep_going = sb("keep_going", [P, HALF])
        def tokens_in(buf):
            return buf[0:TT].rearrange("p u n c -> p (u n c)")[:, 0:NT * D].rearrange("p (i d) -> p i d", i=NT)
        resid = tokens_in(relu_neg)
        stats = sb("stats", [TT, NT, 6])
        mv = sb("mv", [TT, NT, 2])
        var_eps = sb("var_eps", [TT, NT])
        minus_half = sb("minus_half", [TT, NT])
        rstd = sb("rstd", [TT, NT])
        wq_scale = sb("wq_scale", [P, KT])
        wq_inv = sb("wq_inv", [P, KT])
        wq_tmp = sb("wq_tmp", [P, KT, D])
        wq_int = sb("wq_int", [P, KT, D], BF16)
        wq_intT = sb("wq_intT", [P, KT, D], BF16)
        diag = sb("diag", [P, KT, P])
        ones = sb("ones", [P, TT])
        wq_scale_row = sb("wq_scale_row", [TT, D])
        x_scale = sb("x_scale", [TT, NT])
        x_inv = sb("x_inv", [TT, NT])
        x_tmp = tokens_in(phi)
        x_int = sb("x_int", [TT, NT, D], BF16)
        x_intT = sb("x_intT", [P, KT, T], BF16)
        head_of = sb("head_of", [P, 2 * GP])
        head_mask = sb("head_mask", [P, 2])
        query = sb("query", [TT, NT, D])
        q_scaled = sb("q_scaled", [TT, NT, D])
        qbd = relu_pos[:].rearrange("p u n c -> p (u n c)").rearrange("p (m b e s) -> p m b e s", m=KT, b=B, e=2)
        qbd_hi = sb("qbd_hi", [P, KT, B, 2, S], F32R)
        qbd_lo = sb("qbd_lo", [P, KT, B, 2, S], F32R)
        ps = ctx.enter_context(nc.psum_tensor("psA", [P, 8, 512], F32))
        psb = ps[:, :, :].bitcast(BF16)

        x_in = sem("x_in")
        w_in = [sem(f"w_in{k}") for k in range(7)]
        bias_in = sem("bias_in")
        row_in = sem("row_in")
        const_set = sem("const_set")
        dve_const = sem("dve_const")
        ident_ready = sem("ident_ready")
        identb_ready = sem("identb_ready")
        sel_ready = sem("sel_ready")
        head_of_ready = sem("head_of_ready")
        mask_ready = sem("mask_ready")
        xT_in_psum = sem("xT_in_psum")
        xT_dve = sem("xT_dve")
        xT_act = sem("xT_act")
        wT_in_psum = sem("wT_in_psum")
        wT_act = sem("wT_act")
        wT_lo = sem("wT_lo")
        qkv_in_psum = sem("qkv_in_psum")
        relus = sem("relus")
        exps = sem("exps")
        phis = sem("phis")
        v_used = sem("v_used")
        scanned = sem("scanned")
        context_ready = sem("context_ready")
        attn_in_psum = sem("attn_in_psum")
        xbo_ready = sem("xbo_ready")
        resid_ready = sem("resid_ready")
        stats_ready = sem("stats_ready")
        mv_ready = sem("mv_ready")
        var_ready = sem("var_ready")
        rstd_ready = sem("rstd_ready")
        x1_ready = sem("x1_ready")
        wq_steps = sem("wq_steps")
        wq_int_ready = sem("wq_int_ready")
        diag_ready = sem("diag_ready")
        wqT_in_psum = sem("wqT_in_psum")
        wqT_ready = sem("wqT_ready")
        row_in_psum = sem("row_in_psum")
        row_ready = sem("row_ready")
        x_steps = sem("x_steps")
        x_int_ready = sem("x_int_ready")
        x_intT_in_psum = sem("x_intT_in_psum")
        x_intT_ready = sem("x_intT_ready")
        q_in_psum = sem("q_in_psum")
        q_scaled_ready = sem("q_scaled_ready")
        query_ready = sem("query_ready")
        qT_in_psum = sem("qT_in_psum")
        qbd_ready = sem("qbd_ready")
        qbd_hi_ready = sem("qbd_hi_ready")
        qbd_lo_ready = sem("qbd_lo_ready")
        q_stored = sem("q_stored")

        def column(ap):
            return ap.rearrange("(k p) -> p k", k=KT)

        def row(ap, n):
            return ap.unsqueeze(0).broadcast_to([n, D])

        with nc.Block() as block:

            @block.sync
            def _(sp):
                sp.dma_start(x_sb[:], io["x"].rearrange("b s d -> (b s) d").rearrange("(i p) d -> p i d", p=TT)
                             ).then_inc(x_in, 16)
                for k in range(7):
                    sp.dma_start(w_raw[:, k], io[names[k]].rearrange("(k p) d -> p k d", p=P)).then_inc(w_in[k], 16)
                for h in range(2):
                    for m in range(KT):
                        bs = slice(h * B // 2, (h + 1) * B // 2)
                        sp.wait_ge(qbd_hi_ready, 2 * h + m + 1)
                        sp.dma_start(io["q_hi"][m, :, bs], qbd_hi[:, m, bs].bitcast(F32).rearrange("p b e n -> p b (e n)")).then_inc(q_stored, 16)
                        sp.wait_ge(qbd_lo_ready, 2 * h + m + 1)
                        sp.dma_start(io["q_lo"][m, :, bs], qbd_lo[:, m, bs].bitcast(F32).rearrange("p b e n -> p b (e n)")).then_inc(q_stored, 16)
                sp.wait_ge(q_stored, 16 * 4 * KT)

            @block.gpsimd
            def _(pool):
                nc.gpsimd.memset(keep["ident"][:], 0.0).then_inc(const_set, 1)
                nc.gpsimd.memset(keep["sel"][:], 0.0).then_inc(const_set, 1)
                nc.gpsimd.memset(head_of[:], 1.0).then_inc(const_set, 1)
                nc.gpsimd.memset(minus_half[:], -0.5).then_inc(const_set, 1)
                pool.wait_ge(const_set, 4)
                nc.gpsimd.affine_select(out=keep["ident"][:], in_=keep["ident"][:], compare_op=ALU.not_equal,
                                        fill=1.0, base=0, pattern=[[-1, P]], channel_multiplier=1).then_inc(ident_ready, 1)
                for e in range(2):
                    for a in range(2):
                        v = keep["sel"][:, 2 * e + a, a * S:(a + 1) * S]
                        nc.gpsimd.affine_select(out=v, in_=v, compare_op=ALU.not_equal, fill=1.0, base=-e * S,
                                                pattern=[[-1, S]], channel_multiplier=1).then_inc(sel_ready, 1)
                nc.gpsimd.affine_select(out=head_of[:], in_=head_of[:], compare_op=ALU.is_ge, fill=0.0, base=0,
                                        pattern=[[-DH, 2 * GP]], channel_multiplier=1).then_inc(head_of_ready, 1)
                pool.wait_ge(head_of_ready, 1)
                nc.gpsimd.affine_select(out=head_of[:], in_=head_of[:], compare_op=ALU.is_ge, fill=0.0, base=DH - 1,
                                        pattern=[[DH, 2 * GP]], channel_multiplier=-1).then_inc(head_of_ready, 1)
                pool.wait_ge(sel_ready, 4)
                for h in range(2):
                    g = slice(h * HT, (h + 1) * HT)
                    pool.wait_ge(var_ready, h + 1)
                    nc.gpsimd.tensor_tensor(rstd[:, g], var_eps[:, g], minus_half[:, g], ALU.pow).then_inc(rstd_ready, 1)

            @block.tensor
            def _(pe):
                pe.wait_ge(ident_ready, 1)
                pe.wait_ge(x_in, 16)
                for m in range(KT):
                    for h in range(2):
                        for j in range(HT):
                            last = nc.tensor.transpose(ps[:, 2 * m + h, j * TT:(j + 1) * TT],
                                                       x_sb[:, h * HT + j, m * P:(m + 1) * P], keep["ident"][0:TT, 0:TT])
                        last.then_inc(xT_in_psum, 1)

                def weight_transpose(k):
                    pe.wait_ge(w_in[k], 16)
                    if k >= 2:
                        pe.wait_ge(wT_act, k - 1)
                    if k >= 6:
                        pe.wait_ge(wT_lo, k - 5)
                    for m in range(KT):
                        for e in range(KT):
                            last = nc.tensor.transpose(ps[:, 6 + k % 2, m * D + e * P:m * D + (e + 1) * P],
                                                       w_raw[:, k, e, m * P:(m + 1) * P], keep["ident"][:])
                    last.then_inc(wT_in_psum, 1)

                for k in (WK, WV, WQ):
                    weight_transpose(k)
                pe.wait_ge(xT_dve, 2)
                pe.wait_ge(xT_act, 2)
                pe.wait_ge(wT_act, 3)
                for u in range(4):
                    h, e = divmod(u, KT)
                    bank = 3 * (u % 2)
                    if u >= 2:
                        pe.wait_ge(relus, 4 * (u - 1))
                        pe.wait_ge(v_used, u - 1)
                    for n, k in enumerate((WK, WQ, WV)):
                        for m in range(KT):
                            last = nc.tensor.matmul(ps[:, bank + n, 0:HALF], wT[:, k, m, e * P:(e + 1) * P],
                                                    xT[:, m, h * HALF:(h + 1) * HALF], start=m == 0, stop=m == KT - 1)
                        last.then_inc(qkv_in_psum, 1)
                    if u == 0:
                        weight_transpose(WO)
                        weight_transpose(XK)
                    if u == 1:
                        weight_transpose(XV)
                pe.wait_ge(identb_ready, 1)
                pe.wait_ge(wq_int_ready, 1)
                pe.wait_ge(wT_lo, 1)
                for m in range(KT):
                    for e in range(KT):
                        last = nc.tensor.transpose(psb[:, 6, m * D + e * P:m * D + (e + 1) * P],
                                                   wq_int[:, e, m * P:(m + 1) * P], keep["ident_b"][:])
                last.then_inc(wqT_in_psum, 1)
                pe.wait_ge(diag_ready, KT)
                pe.wait_ge(dve_const, 2)
                pe.wait_ge(wT_lo, 2)
                for e in range(KT):
                    last = nc.tensor.matmul(ps[0:TT, 7, e * P:(e + 1) * P], ones[:], diag[:, e], start=True, stop=True)
                last.then_inc(row_in_psum, 1)
                for h in range(2):
                    pe.wait_ge(context_ready, KT * (h + 1))
                    if h == 0:
                        pe.wait_ge(relus, 16)
                        pe.wait_ge(v_used, 4)
                    for i in range(h * HT, (h + 1) * HT):
                        for m in range(KT):
                            last = nc.tensor.matmul(ps[0:TT, i // 2, (i % 2) * D:(i % 2 + 1) * D],
                                                    context[:, m, i * TT:(i + 1) * TT], wT[:, WO, m], start=m == 0, stop=m == KT - 1)
                        if i % 2:
                            last.then_inc(attn_in_psum, 1)
                for h in range(2):
                    for j in range(HT):
                        i = h * HT + j
                        pe.wait_ge(x_int_ready, i + 1)
                        for m in range(KT):
                            last = nc.tensor.transpose(psb[:, 4 + h, m * HALF + j * TT:m * HALF + (j + 1) * TT],
                                                       x_int[:, i, m * P:(m + 1) * P], keep["ident_b"][0:TT, 0:TT])
                    last.then_inc(x_intT_in_psum, 1)
                    pe.wait_ge(wqT_ready, 1)
                    pe.wait_ge(x_intT_ready, h + 1)
                    for i in range(h * HT, (h + 1) * HT):
                        if i % 2 == 0:
                            pe.wait_ge(resid_ready, i + 2)
                        for m in range(KT):
                            last = nc.tensor.matmul(ps[0:TT, i // 2, (i % 2) * D:(i % 2 + 1) * D],
                                                    x_intT[:, m, i * TT:(i + 1) * TT], wq_intT[:, m], start=m == 0, stop=m == KT - 1)
                        if i % 2:
                            last.then_inc(q_in_psum, 1)
                pe.wait_ge(row_ready, 1)
                pe.wait_ge(x_intT_ready, 2)
                for h in range(2):
                    pe.wait_ge(query_ready, (h + 1) * HT)
                    for m in range(KT):
                        for j in range(HT):
                            last = nc.tensor.transpose(ps[:, 4 + 2 * m + h, j * TT:(j + 1) * TT],
                                                       query[:, h * HT + j, m * P:(m + 1) * P], keep["ident"][0:TT, 0:TT])
                        last.then_inc(qT_in_psum, 1)

            @block.scalar
            def _(act):
                for n, name in enumerate(["L0_attn_bk", "L0_attn_bq", "L0_attn_bv"]):
                    act.dma_start(qkv_bias[:, n], column(io[name]), allow_slow_non_contiguous=True).then_inc(bias_in, 16)
                act.dma_start(keep["xbk"][:], column(io["L0_xattn_bk"]), allow_slow_non_contiguous=True).then_inc(bias_in, 16)
                act.dma_start(bo_row[:], row(io["L0_attn_bo"], TT)).then_inc(row_in, 16)
                act.dma_start(xbq_row[:], row(io["L0_xattn_bq"], TT)).then_inc(row_in, 16)
                act.wait_ge(bias_in, 64)
                act.wait_ge(row_in, 32)
                act.wait_ge(ident_ready, 1)
                nc.scalar.activation(keep["ident_b"][:], keep["ident"][:], ACT.Copy).then_inc(identb_ready, 1)
                nc.scalar.activation(neg_bias[:], qkv_bias[:], ACT.Copy, scale=-1.0).then_inc(identb_ready, 1)
                for n in (1, 3):
                    act.wait_ge(xT_in_psum, n + 1)
                    nc.scalar.activation(xT[:, n // 2, HALF:T], ps[:, n, 0:HALF], ACT.Copy).then_inc(xT_act, 1)

                def weight_out(k):
                    act.wait_ge(wT_in_psum, k + 1)
                    src = ps[:, 6 + k % 2]
                    if k < XK:
                        dst = wT[:, k]
                    else:
                        dst = keep["wkT_hi" if k == XK else "wvT_hi"][:]
                    nc.scalar.activation(dst, split(src, KT), ACT.Copy).then_inc(wT_act, 1)

                for k in (WK, WV, WQ):
                    weight_out(k)
                act.wait_ge(identb_ready, 2)
                for u in range(4):
                    h, e = divmod(u, KT)
                    for n in range(2):
                        act.wait_ge(qkv_in_psum, 3 * u + n + 1)
                        src = ps[:, 3 * (u % 2) + n, 0:HALF]
                        nc.scalar.activation(relu_neg[:, u, n], src, ACT.Relu, scale=-1.0,
                                             bias=neg_bias[:, n, e:e + 1]).then_inc(relus, 1)
                        nc.scalar.activation(relu_pos[:, u, n], src, ACT.Relu,
                                             bias=qkv_bias[:, n, e:e + 1]).then_inc(relus, 1)
                    act.wait_ge(relus, 4 * u + 4)
                    nc.scalar.activation(relu_neg[:, u], relu_neg[:, u], ACT.Exp, scale=-1.0).then_inc(exps, 1)
                    if u == 0:
                        weight_out(WO)
                        weight_out(XK)
                    if u == 1:
                        weight_out(XV)
                act.wait_ge(wqT_in_psum, 1)
                nc.scalar.activation(wq_intT[:], split(psb[:, 6, 0:KT * D], KT), ACT.Copy).then_inc(wqT_ready, 1)
                act.wait_ge(row_in_psum, 1)
                nc.scalar.activation(wq_scale_row[:], ps[0:TT, 7, 0:D], ACT.Copy, scale=SCALE).then_inc(row_ready, 1)
                for n in range(4):
                    m, h = n % 2, n // 2
                    act.wait_ge(qbd_ready, 2 * n + 2)
                    bs = slice(h * B // 2, (h + 1) * B // 2)
                    nc.scalar.activation(qbd_hi[:, m, bs], qbd[:, m, bs], ACT.Copy).then_inc(qbd_hi_ready, 1)

            @block.vector
            def _(dve):
                nc.vector.memset(keep_going[:], 1.0).then_inc(dve_const, 1)
                nc.vector.memset(ones[:], 1.0).then_inc(dve_const, 1)
                dve.wait_ge(dve_const, 1)
                nc.vector.memset(keep_going[:].rearrange("p (b s) -> p b s", s=S)[:, :, 0:1], 0.0).then_inc(dve_const, 1)
                dve.wait_ge(head_of_ready, 2)
                nc.vector.tensor_reduce(head_mask[:], head_of[:].rearrange("p (k e) -> p e k", e=2), AX.X, ALU.add).then_inc(mask_ready, 1)
                for n in (0, 2):
                    dve.wait_ge(xT_in_psum, n + 1)
                    nc.vector.tensor_copy(xT[:, n // 2, 0:HALF], ps[:, n, 0:HALF]).then_inc(xT_dve, 1)
                dve.wait_ge(w_in[XQ], 16)
                nc.vector.tensor_reduce(wq_scale[:], w_raw[:, XQ], AX.X, ALU.max, apply_absolute_value=True).then_inc(wq_steps, 1)
                dve.wait_ge(wq_steps, 1)
                nc.vector.tensor_scalar(wq_scale[:], wq_scale[:], 1.0 / QMAX, QEPS, ALU.mult, ALU.max).then_inc(wq_steps, 1)
                dve.wait_ge(wq_steps, 2)
                nc.vector.reciprocal(wq_inv[:], wq_scale[:]).then_inc(wq_steps, 1)
                dve.wait_ge(ident_ready, 1)
                for e in range(KT):
                    nc.vector.tensor_scalar(diag[:, e], keep["ident"][:], wq_scale[:, e:e + 1], None, ALU.mult).then_inc(diag_ready, 1)
                dve.wait_ge(wq_steps, 3)
                for e in range(KT):
                    nc.vector.tensor_scalar(wq_tmp[:, e], w_raw[:, XQ, e], wq_inv[:, e:e + 1], ROUND, ALU.mult, ALU.add).then_inc(wq_steps, 1)
                dve.wait_ge(wq_steps, 5)
                nc.vector.tensor_scalar(wq_tmp[:], wq_tmp[:], ROUND, QMAX, ALU.subtract, ALU.min).then_inc(wq_steps, 1)
                dve.wait_ge(wq_steps, 6)
                nc.vector.tensor_scalar(wq_int[:], wq_tmp[:], -QMAX, None, ALU.max).then_inc(wq_int_ready, 1)
                dve.wait_ge(bias_in, 64)
                dve.wait_ge(row_in, 32)
                dve.wait_ge(dve_const, 3)
                dve.wait_ge(xT_in_psum, 4)
                nc.vector.tensor_tensor(x_sb[:], x_sb[:], bo_row[:].unsqueeze(1).broadcast_to([TT, NT, D]), ALU.add).then_inc(xbo_ready, 1)
                nc.vector.tensor_scalar(xbq_row[:], xbq_row[:], SCALE, None, ALU.mult).then_inc(xbo_ready, 1)

                def weight_lo(k):
                    dve.wait_ge(wT_act, k + 1)
                    hi = keep["wkT_hi" if k == XK else "wvT_hi"]
                    lo = keep["wkT_lo" if k == XK else "wvT_lo"]
                    nc.vector.tensor_tensor(lo[:], split(ps[:, 6 + k % 2], KT), hi[:].bitcast(F32), ALU.subtract).then_inc(wT_lo, 1)

                for u in range(4):
                    h, e = divmod(u, KT)
                    dve.wait_ge(exps, u + 1)
                    nc.vector.tensor_tensor(phi[:, u], relu_pos[:, u], relu_neg[:, u], ALU.add).then_inc(phis, 1)
                    dve.wait_ge(phis, u + 1)
                    dve.wait_ge(qkv_in_psum, 3 * u + 3)
                    nc.vector.scalar_tensor_tensor(out=kv[:, u], in0=ps[:, 3 * (u % 2) + 2, 0:HALF], scalar=qkv_bias[:, 2, e:e + 1],
                                                   in1=phi[:, u, 0], op0=ALU.add, op1=ALU.mult).then_inc(v_used, 1)
                    dve.wait_ge(v_used, u + 1)
                    nc.vector.tensor_tensor_scan(kv_sum[:, u], keep_going[:], kv[:, u], 0.0, ALU.mult, ALU.add).then_inc(scanned, 1)
                    dve.wait_ge(scanned, u + 1)
                    nc.vector.scalar_tensor_tensor(out=context[:, e, h * HALF:(h + 1) * HALF], in0=kv_sum[:, u], scalar=SCALE,
                                                   in1=phi[:, u, 1], op0=ALU.mult, op1=ALU.mult).then_inc(context_ready, 1)
                    if u == 1:
                        weight_lo(XK)
                    if u == 2:
                        weight_lo(XV)
                dve.wait_ge(xbo_ready, 2)
                for h in range(2):
                    for i in range(h * HT, (h + 1) * HT):
                        if i % 2 == 0:
                            dve.wait_ge(attn_in_psum, i // 2 + 1)
                        nc.vector.tensor_tensor(resid[:, i], ps[0:TT, i // 2, (i % 2) * D:(i % 2 + 1) * D], x_sb[:, i], ALU.add).then_inc(resid_ready, 1)
                    for i in range(h * HT, (h + 1) * HT):
                        dve.wait_ge(resid_ready, i + 1)
                        nc.vector.bn_stats(stats[:, i], resid[:, i]).then_inc(stats_ready, 1)
                    for i in range(h * HT, (h + 1) * HT):
                        dve.wait_ge(stats_ready, i + 1)
                        nc.vector.bn_aggr(mv[:, i], stats[:, i]).then_inc(mv_ready, 1)
                    g = slice(h * HT, (h + 1) * HT)
                    dve.wait_ge(mv_ready, (h + 1) * HT)
                    nc.vector.tensor_scalar(var_eps[:, g], mv[:, g, 1], LN_EPS, None, ALU.add).then_inc(var_ready, 1)
                for h in range(2):
                    dve.wait_ge(rstd_ready, h + 1)
                    for i in range(h * HT, (h + 1) * HT):
                        nc.vector.tensor_scalar(keep["x1"][:, i], resid[:, i], mv[:, i, 0:1], rstd[:, i:i + 1],
                                                ALU.subtract, ALU.mult).then_inc(x1_ready, 1)
                    g = slice(h * HT, (h + 1) * HT)
                    dve.wait_ge(x1_ready, (h + 1) * HT)
                    nc.vector.tensor_reduce(x_scale[:, g], keep["x1"][:, g], AX.X, ALU.max, apply_absolute_value=True).then_inc(x_steps, 1)
                    dve.wait_ge(x_steps, 4 * h + 1)
                    nc.vector.tensor_scalar(x_scale[:, g], x_scale[:, g], 1.0 / QMAX, QEPS, ALU.mult, ALU.max).then_inc(x_steps, 1)
                    dve.wait_ge(x_steps, 4 * h + 2)
                    nc.vector.reciprocal(x_inv[:, g], x_scale[:, g]).then_inc(x_steps, 1)
                    dve.wait_ge(x_steps, 4 * h + 3)
                    for i in range(h * HT, (h + 1) * HT):
                        ins = nc.vector.tensor_scalar(x_tmp[:, i], keep["x1"][:, i], x_inv[:, i:i + 1], ROUND, ALU.mult, ALU.add)
                    ins.then_inc(x_steps, 1)
                    dve.wait_ge(x_steps, 4 * h + 4)
                    for i in range(h * HT, (h + 1) * HT):
                        nc.vector.tensor_scalar(x_int[:, i], x_tmp[:, i], ROUND, QMAX, ALU.subtract, ALU.min).then_inc(x_int_ready, 1)
                    dve.wait_ge(x_intT_in_psum, h + 1)
                    nc.vector.tensor_scalar(x_intT[:, :, h * HALF:(h + 1) * HALF], split(psb[:, 4 + h, 0:KT * HALF], KT),
                                            -QMAX, None, ALU.max).then_inc(x_intT_ready, 1)
                dve.wait_ge(row_ready, 1)
                for i in range(NT):
                    if i % 2 == 0:
                        dve.wait_ge(q_in_psum, i // 2 + 1)
                    nc.vector.scalar_tensor_tensor(out=q_scaled[:, i], in0=ps[0:TT, i // 2, (i % 2) * D:(i % 2 + 1) * D],
                                                   scalar=x_scale[:, i:i + 1], in1=wq_scale_row[:], op0=ALU.mult, op1=ALU.mult).then_inc(q_scaled_ready, 1)
                for h in range(2):
                    g = slice(h * HT, (h + 1) * HT)
                    dve.wait_ge(q_scaled_ready, (h + 1) * HT)
                    nc.vector.tensor_tensor(query[:, g], q_scaled[:, g], xbq_row[:].unsqueeze(1).broadcast_to([TT, HT, D]), ALU.add).then_inc(query_ready, HT)
                dve.wait_ge(mask_ready, 1)
                for n in range(4):
                    m, h = n % 2, n // 2
                    dve.wait_ge(qT_in_psum, n + 1)
                    src = ps[:, 4 + 2 * m + h, 0:HALF].rearrange("p (b s) -> p b s", s=S)
                    bs = slice(h * B // 2, (h + 1) * B // 2)
                    for e in range(2):
                        nc.vector.tensor_scalar(qbd[:, m, bs, e], src, head_mask[:, e:e + 1], None, ALU.mult).then_inc(qbd_ready, 1)
                for n in range(4):
                    m, h = n % 2, n // 2
                    bs = slice(h * B // 2, (h + 1) * B // 2)
                    dve.wait_ge(qbd_hi_ready, n + 1)
                    nc.vector.tensor_tensor(qbd_lo[:, m, bs], qbd[:, m, bs], qbd_hi[:, m, bs].bitcast(F32), ALU.subtract).then_inc(qbd_lo_ready, 1)


UNITS = [
    ([("X", 0, 0)], [("X", 0, 1)]),
    ([("X", 1, 0), ("X", 1, 1)], [("V", 0, 0)]),
    ([("X", 2, 0), ("X", 2, 1)], [("K", 0, 0)]),
    ([("K", 0, 1)], [("K", 0, 2)]),
    ([("V", 1, 0)], [("V", 2, 0)]),
    ([("V", 3, 0)], [("V", 4, 0)]),
    ([("K", 1, 0)], [("K", 1, 1)]),
    ([("K", 1, 2)], [("V", 5, 0)]),
]
ORDER = [u for before, after in UNITS for u in before + after]
NU = len(ORDER)
AT = {u: n for n, u in enumerate(ORDER)}
HI = [u for u in ORDER if u[0] != "V"]
HI_AT = {u: n for n, u in enumerate(HI)}
NHI = len(HI)
TB = 3
STACK = 3


def cross_attention_phase(nc, io, keep):
    ctx = ExitStack()
    with ctx:
        sb = lambda n, s, d=F32: ctx.enter_context(nc.sbuf_tensor(n, s, d))
        sem = lambda n: ctx.enter_context(nc.semaphore(n))
        context = sb("ctx_rows", [LT, NL, D])
        cT_hi = sb("cT_hi", [P, KT, L], F32R)
        cT_lo = sb("cT_lo", [P, KT, L], F32R)
        k_hi = sb("k_hi", [P, L], F32R)
        k_lo = sb("k_lo", [P, L], F32R)
        k_stack = sb("k_stack", [STACK * PD, NP, L], F32R)
        q_stack = sb("q_stack", [STACK * PD, 2, NP, PN], F32R)
        v_sb = sb("v_sb", [LT, 2, NL, D])
        mask_sb = sb("mask_sb", [PN, 2, L])
        scores = sb("scores", [PN, 2, L])
        shift = sb("shift", [PN, 2])
        gate_cell = sb("gate_cell", [PN, 1])
        probsT = sb("probsT", [LT, 2, NL, PN])
        ps_scores = ctx.enter_context(nc.psum_tensor("ps_scores", [P, NC, 512], F32))
        ps_T = ctx.enter_context(nc.psum_tensor("ps_T", [P, 2, 512], F32))
        ps_proj = ctx.enter_context(nc.psum_tensor("ps_proj", [P, 2, 512], F32))
        ps_out = ctx.enter_context(nc.psum_tensor("ps_out", [P, 512], F32))

        ctx_in = [sem(f"ctx_in{c}") for c in range(NC)]
        mask_in = [sem(f"mask_in{a}") for a in range(2)]
        q_in = [sem(f"q_in{a}") for a in range(2)]
        k_in = [sem(f"k_in{p}") for p in range(NP)]
        unit_in_psum = sem("unit_in_psum")
        hi_ready = sem("hi_ready")
        unit_out = sem("unit_out")
        scores_in_psum = sem("scores_in_psum")
        scores_ready = sem("scores_ready")
        gate = sem("gate")
        probs_ready = sem("probs_ready")
        probsT_in_psum = sem("probsT_in_psum")
        probsT_dve = sem("probsT_dve")
        probsT_act = sem("probsT_act")
        values_done = sem("values_done")
        out_copied = sem("out_copied")

        def q_rows(src, b):
            return src[:, :, b].rearrange("m (k r) n -> r (m k) n", r=PD)

        with nc.Block() as block:

            @block.sync
            def _(sp):
                def load_chunk(b, c):
                    sp.dma_start(context[:, c * TC:(c + 1) * TC],
                                 io["ctx"][b, c * LC:(c + 1) * LC].rearrange("(j p) d -> p j d", p=LT)).then_inc(ctx_in[c], 16)

                def load_mask(b, a):
                    for e in range(2):
                        sp.dma_start(mask_sb[e * S:(e + 1) * S, a], io["mask"][b]).then_inc(mask_in[a], 16)

                def load_q(b, a):
                    for g, src in enumerate(("q_hi", "q_lo", "q_hi")):
                        sp.dma_start(q_stack[g * PD:(g + 1) * PD, a].bitcast(F32), q_rows(io[src], b)).then_inc(q_in[a], 16)

                def k_out(n, m):
                    return n * NU + AT[("K", m, NC - 1)] + 1 + 2

                def stack_k(n, m):
                    for k in range(GP):
                        rows = slice(k * PD, (k + 1) * PD)
                        for g, src in enumerate((k_hi, k_hi, k_lo)):
                            sp.dma_start(k_stack[g * PD:(g + 1) * PD, m * GP + k].bitcast(F32), src[rows].bitcast(F32)).then_inc(k_in[m * GP + k], 16)

                def batch(b, a, project, load):
                    if project:
                        n = b + 1
                        for c in range(NC):
                            if load:
                                sp.wait_ge(unit_in_psum, n * NU + AT[("X", c, 1)] + 1)
                                load_chunk(b + 2, c)
                        sp.wait_ge(unit_out, k_out(n, 0))
                        stack_k(n, 0)
                        if load:
                            sp.wait_ge(scores_ready, (b + 1) * NP)
                            load_mask(b + 2, a)
                            load_q(b + 2, a)
                        sp.wait_ge(unit_out, k_out(n, 1))
                        stack_k(n, 1)

                for c in range(NC):
                    load_chunk(0, c)
                for a in range(2):
                    load_q(a, a)
                    load_mask(a, a)
                for c in range(NC):
                    sp.wait_ge(unit_in_psum, AT[("X", c, 1)] + 1)
                    load_chunk(1, c)
                for m in range(KT):
                    sp.wait_ge(unit_out, k_out(0, m))
                    stack_k(0, m)
                with sp.Fori(0, B // 2 - 1) as i:
                    for a in range(2):
                        batch(2 * i + a, a, True, True)
                batch(B - 2, 0, True, False)

            @block.tensor
            def _(pe):
                def terms(w_hi, w_lo, x_hi, x_lo):
                    return ((w_hi, x_hi), (w_hi, x_lo), (w_lo, x_hi))

                def unit(n, u, a, first=False):
                    kind, p, q = u
                    bank = AT[u] % 2
                    pe.wait_ge(unit_out, n * NU + AT[u] + 1)
                    if kind == "X":
                        if q == 0:
                            pe.wait_ge(ctx_in[p], 16 * (n + 1))
                        for j in range(TC):
                            last = nc.tensor.transpose(ps_proj[:, bank, j * LT:(j + 1) * LT],
                                                       context[:, p * TC + j, q * P:(q + 1) * P], keep["ident"][0:LT, 0:LT])
                    elif kind == "K":
                        pe.wait_ge(unit_out, n * NU + AT[("X", q, 1)] + 1 + 2)
                        c, e = slice(q * LC, (q + 1) * LC), slice(p * P, (p + 1) * P)
                        mm = [t for m in range(KT) for t in terms(keep["wkT_hi"][:, m, e], keep["wkT_lo"][:, m, e],
                                                                  cT_hi[:, m, c], cT_lo[:, m, c])]
                        for i, (w, x) in enumerate(mm):
                            last = nc.tensor.matmul(ps_proj[:, bank, 0:LC], w, x, start=i == 0, stop=i == len(mm) - 1)
                    else:
                        pe.wait_ge(unit_out, n * NU + AT[("X", (2 * p + 1) // TC, 1)] + 1 + 2)
                        for j in range(2):
                            c = slice((2 * p + j) * LT, (2 * p + j + 1) * LT)
                            mm = [t for m in range(KT) for t in terms(cT_hi[:, m, c], cT_lo[:, m, c],
                                                                      keep["wvT_hi"][:, m], keep["wvT_lo"][:, m])]
                            for i, (w, x) in enumerate(mm):
                                last = nc.tensor.matmul(ps_proj[0:LT, bank, j * D:(j + 1) * D], w, x, start=i == 0, stop=i == len(mm) - 1)
                    last.then_inc(unit_in_psum, 1)


                def scores_of(b, half, a, t, before):
                    if t == 0:
                        pe.wait_ge(q_in[a], 16 * STACK * (half + 1))
                    pe.wait_ge(k_in[t], 16 * STACK * (b + 1))
                    if before:
                        pe.wait_ge(scores_ready, b * NP + t)
                    for c in range(NC):
                        last = nc.tensor.matmul(ps_scores[0:PN, c, 0:LC], q_stack[:, a, t], k_stack[:, t, c * LC:(c + 1) * LC],
                                                start=True, stop=True)
                        if c == 0 and not before:
                            last.then_inc(values_done, 2)
                    last.then_inc(scores_in_psum, 1)

                def transposes(b, t, k):
                    if k == 0:
                        pe.wait_ge(probs_ready, b * NP + t + 1)
                    if k < 2:
                        pe.wait_ge(probsT_act, 2 * (b * NP + t) + k + 1)
                    else:
                        pe.wait_ge(probsT_dve, b * NP + t + 1)
                    for j in range(TC):
                        last = nc.tensor.transpose(ps_T[0:LT, (TB * t + k) % 2, j * PN:(j + 1) * PN],
                                                   scores[:, t % 2, (k * TC + j) * LT:(k * TC + j + 1) * LT], keep["ident"][0:PN, 0:PN])
                    last.then_inc(probsT_in_psum, 1)

                def values(b, a, t, tiles):
                    g, k = divmod(t, GP)
                    for j in tiles:
                        if j == 0:
                            pe.wait_ge(probsT_dve, b * NP + t + 1)
                            if t == 0:
                                pe.wait_ge(out_copied, b + 1)
                                pe.wait_ge(unit_out, b * NU + NU + 2)
                        if j == TC:
                            pe.wait_ge(probsT_act, 2 * (b * NP + t) + 1 + 2)
                        if j == 2 * TC:
                            pe.wait_ge(probsT_act, 2 * (b * NP + t) + 2 + 2)
                        last = nc.tensor.matmul(ps_out[k * PD:(k + 1) * PD, g * PN:(g + 1) * PN], v_sb[:, a, j, t * PD:(t + 1) * PD],
                                                probsT[:, t % 2, j], start=j == 0, stop=j == NL - 1)
                    if j == NL - 1:
                        last.then_inc(values_done, 1)

                def batch(b, half, a, project):
                    for t in range(NP):
                        transposes(b, t, 0)
                        transposes(b, t, 1)
                        if t + 2 < NP:
                            scores_of(b, half, a, t + 2, True)
                        elif project:
                            scores_of(b + 1, half + a, 1 - a, t + 2 - NP, True)
                        transposes(b, t, 2)
                        before, after = UNITS[t] if project else ([], [])
                        for u in before:
                            unit(b + 1, u, 1 - a)
                        values(b, a, t, range(0, 2 * TC))
                        for u in after:
                            unit(b + 1, u, 1 - a)
                        values(b, a, t, range(2 * TC, NL))

                for u in ORDER:
                    unit(0, u, 0)
                scores_of(0, 0, 0, 0, False)
                scores_of(0, 0, 0, 1, True)
                with pe.Fori(0, B // 2 - 1) as i:
                    for a in range(2):
                        batch(2 * i + a, i, a, True)
                batch(B - 2, B // 2 - 1, 0, True)
                batch(B - 1, B // 2 - 1, 1, False)

            @block.scalar
            def _(act):
                def unit_hi(n, u):
                    kind, p, q = u
                    if kind == "V":
                        return
                    act.wait_ge(unit_in_psum, n * NU + AT[u] + 1)
                    src = ps_proj[:, AT[u] % 2, 0:LC]
                    if kind == "X":
                        nc.scalar.activation(cT_hi[:, q, p * LC:(p + 1) * LC], src, ACT.Copy).then_inc(hi_ready, 1)
                    else:
                        if q == 0:
                            for k in range(GP):
                                done = n * 16 * STACK if p == 0 else (n + 1) * 16 * STACK
                                other = (1 - p) * GP + k
                                if p == 1 or not isinstance(n, int) or n > 0:
                                    act.wait_ge(k_in[other], done)
                        nc.scalar.activation(k_hi[:, q * LC:(q + 1) * LC], src, ACT.Identity,
                                             bias=keep["xbk"][:, p:p + 1]).then_inc(hi_ready, 1)

                def exponentials(b, t):
                    act.wait_ge(scores_ready, b * NP + t + 1)
                    nc.scalar.activation(scores[:, t % 2], scores[:, t % 2], ACT.Exp, scale=-1.0, bias=shift[:, t % 2:t % 2 + 1],
                                         accum_out=keep["sums"][:, b, t:t + 1]).then_inc(probs_ready, 1)

                def batch(b, project):
                    for t in range(NP):
                        act.wait_ge(values_done, b * NP + t + 1)
                        for k in (1, 2):
                            act.wait_ge(probsT_in_psum, TB * (b * NP + t) + k + 1)
                            nc.scalar.activation(probsT[:, t % 2, k * TC:(k + 1) * TC],
                                                 ps_T[0:LT, (TB * t + k) % 2, 0:TC * PN].rearrange("p (j n) -> p j n", j=TC),
                                                 ACT.Copy).then_inc(probsT_act, 1)
                        if project:
                            for u in UNITS[t][0] + UNITS[t][1]:
                                unit_hi(b + 1, u)
                        if t + 2 < NP:
                            exponentials(b, t + 2)
                        elif project:
                            exponentials(b + 1, t + 2 - NP)
                    act.wait_ge(values_done, (b + 1) * NP + 2)
                    nc.scalar.activation(keep["outT"][:, b], ps_out[:, 0:2 * PN], ACT.Copy).then_inc(out_copied, 1)

                nc.scalar.activation(keep["credit"][:, 1:2], keep["ident"][:, 0:1], ACT.Copy).then_inc(probsT_act, 2)
                nc.scalar.activation(keep["credit"][:, 2:3], keep["ident"][:, 0:1], ACT.Copy).then_inc(out_copied, 1)
                for u in ORDER:
                    unit_hi(0, u)
                exponentials(0, 0)
                exponentials(0, 1)
                with act.Fori(0, B // 2 - 1) as i:
                    for a in range(2):
                        batch(2 * i + a, True)
                batch(B - 2, True)
                batch(B - 1, False)

            @block.vector
            def _(dve):
                def unit_rest(n, u, a):
                    kind, p, q = u
                    bank = AT[u] % 2
                    if kind == "V":
                        dve.wait_ge(unit_in_psum, n * NU + AT[u] + 1)
                        nc.vector.tensor_copy(v_sb[:, a, 2 * p:2 * p + 2], split(ps_proj[0:LT, bank], 2)).then_inc(unit_out, 1)
                        return
                    dve.wait_ge(hi_ready, n * NHI + HI_AT[u] + 1)
                    if kind == "X":
                        c = slice(p * LC, (p + 1) * LC)
                        nc.vector.tensor_tensor(cT_lo[:, q, c], ps_proj[:, bank, 0:LC], cT_hi[:, q, c].bitcast(F32),
                                                ALU.subtract).then_inc(unit_out, 1)
                    else:
                        c = slice(q * LC, (q + 1) * LC)
                        nc.vector.scalar_tensor_tensor(out=k_lo[:, c], in0=ps_proj[:, bank, 0:LC], scalar=keep["xbk"][:, p:p + 1],
                                                       in1=k_hi[:, c].bitcast(F32), op0=ALU.add, op1=ALU.subtract).then_inc(unit_out, 1)

                def masked_scores(b, half, a, t, before):
                    if t == 0:
                        dve.wait_ge(mask_in[a], 32 * (half + 1))
                    if before:
                        dve.wait_ge(probsT_in_psum, TB * (b * NP + t - 1))
                    if before:
                        dve.wait_ge(gate, b * NP + t)
                    dve.wait_ge(scores_in_psum, b * NP + t + 1)
                    nc.vector.memset(gate_cell[:], 0.0).then_inc(gate, 1)
                    nc.vector.tensor_tensor_reduce(out=split(scores[:, t % 2], NC), in0=ps_scores[0:PN, :, 0:LC],
                                                   in1=split(mask_sb[:, a], NC), scale=-1.0, scalar=BIG, op0=ALU.add, op1=ALU.min,
                                                   accum_out=shift[:, t % 2:t % 2 + 1]).then_inc(scores_ready, 1)

                def batch(b, half, a, project):
                    for t in range(NP):
                        dve.wait_ge(values_done, b * NP + t + 1)
                        dve.wait_ge(probsT_in_psum, TB * (b * NP + t) + 1)
                        nc.vector.tensor_copy(probsT[:, t % 2, 0:TC],
                                              ps_T[0:LT, (TB * t) % 2, 0:TC * PN].rearrange("p (j n) -> p j n", j=TC)).then_inc(probsT_dve, 1)
                        if t + 2 < NP:
                            masked_scores(b, half, a, t + 2, True)
                        elif project:
                            masked_scores(b + 1, half + a, 1 - a, t + 2 - NP, True)
                        if project:
                            for u in UNITS[t][0] + UNITS[t][1]:
                                unit_rest(b + 1, u, 1 - a)

                nc.vector.memset(keep["credit"][:, 0:1], 0.0).then_inc(unit_out, 2)
                for u in ORDER:
                    unit_rest(0, u, 0)
                masked_scores(0, 0, 0, 0, False)
                masked_scores(0, 0, 0, 1, False)
                with dve.Fori(0, B // 2 - 1) as i:
                    for a in range(2):
                        batch(2 * i + a, i, a, True)
                batch(B - 2, B // 2 - 1, 0, True)
                batch(B - 1, B // 2 - 1, 1, False)


def kept(nc, ctx):
    sb = lambda n, s, d=F32: ctx.enter_context(nc.sbuf_tensor(n, s, d))
    return {
        "ident": sb("ident", [P, P]),
        "ident_b": sb("ident_b", [P, P], BF16),
        "sel": sb("sel", [PN, 4, TT]),
        "x1": sb("x1", [TT, NT, D]),
        "outT": sb("outT", [P, B, 2 * PN]),
        "sums": sb("sums", [PN, B, NP]),
        "wkT_hi": sb("wkT_hi", [P, KT, D], F32R),
        "wkT_lo": sb("wkT_lo", [P, KT, D], F32R),
        "wvT_hi": sb("wvT_hi", [P, KT, D], F32R),
        "wvT_lo": sb("wvT_lo", [P, KT, D], F32R),
        "xbk": sb("xbk", [P, KT]),
        "credit": sb("credit", [P, 4]),
    }


E, A_ATOMS, NS = 8, 64, 2048
NST = NS // P
CLIP = 50.0
EST = 3


def feed_forward_phase(nc, io, keep):
    ctx = ExitStack()
    with ctx:
        sb = lambda n, s, d=F32: ctx.enter_context(nc.sbuf_tensor(n, s, d))
        sem = lambda n: ctx.enter_context(nc.semaphore(n))
        w_raw = sb("wf_raw", [P, KT, D])
        wT_hi = sb("wfT_hi", [P, KT, D], F32R)
        wT_lo = sb("wfT_lo", [P, KT, D], F32R)
        wo_raw = sb("wo_raw", [P, KT, D])
        wo_scale = sb("wo_scale", [P, KT])
        wo_inv = sb("wo_inv", [P, KT])
        wo_tmp = sb("wo_tmp", [P, KT, D])
        wo_int = sb("wo_int", [P, KT, D], BF16)
        wo_intT = sb("wo_intT", [P, KT, D], BF16)
        diag = sb("diag_o", [P, KT, P])
        ones = sb("ones_o", [P, TT])
        wo_scale_row = sb("wo_scale_row", [TT, D])
        bo_row = sb("xbo_row", [TT, D])
        bv_row = sb("xbv_row", [TT, D])
        x1_bo = keep["x1"]
        gate_raw = sb("gate_raw", [E, D])
        gateT = sb("gateT", [P, KT, E])
        atom_w = sb("atom_w", [E, A_ATOMS])
        atom_shift = sb("atom_shift", [E, 1])
        atom_sum = sb("atom_sum", [E, 1])
        atom_rsum = sb("atom_rsum", [E, 1])
        atom_p = sb("atom_p", [E, A_ATOMS])
        atom_pn = sb("atom_pn", [E, A_ATOMS])
        atom_pT = sb("atom_pT", [A_ATOMS, E])
        atoms = sb("atoms", [A_ATOMS, NS])
        gate_imp = sb("gate_imp", [P, E * NS // P])
        gate_sig = sb("gate_sig", [P, E * NS // P])
        sig8 = sb("sig8", [E, NS])
        w8 = sig8
        w_stack = sb("w_stack", [EST * E, NS], F32R)
        w8_lo = sb("w8_lo", [E, NS], F32R)
        idx_row = sb("idx_row", [P, NS], I32)
        idx_col = sb("idx_col", [P, NST], I32)
        col_i = idx_row
        row_i = sb("row_i", [P, NST], I32)
        row_f = sb("row_f", [P, NST])
        channel = sb("channel", [P, KT])
        channel_row = sb("channel_row", [P, D])
        expert_row = sb("expert_row", [TT, E])
        pick_c = sb("pick_c", [P, KT, NS], F32R)
        pick_r = sb("pick_r", [P, NST, D], F32R)
        rsums = sb("rsums", [PN, B, NP])
        o_norm = sb("o_norm", [PN, 2, 2 * NP, PD])
        o_sb = sb("o_sb", [TT, NT, D])
        o_scale = sb("o_scale", [TT, NT])
        o_inv = sb("o_inv", [TT, NT])
        tmp = sb("tmp_t", [TT, NT, D])
        o_int = sb("o_int", [TT, NT, D], BF16)
        o_intT = sb("o_intT", [P, KT, T], BF16)
        resid = sb("resid2", [TT, NT, D])
        stats = sb("stats2", [TT, 2, NT, 6])
        mv = sb("mv2", [TT, 2, NT, 2])
        var_eps = sb("var_eps2", [TT, 2, NT])
        minus_half = sb("minus_half2", [TT, NT])
        rstd = sb("rstd2", [TT, 2, NT])
        x2 = resid
        x2T_hi = sb("x2T_hi", [P, KT, T], F32R)
        x2T_lo = sb("x2T_lo", [P, KT, T], F32R)
        logits = sb("logits", [TT, NT, E])
        top = sb("top", [TT, NT, 8])
        top_i = sb("top_i", [TT, NT, 8], U32)
        top_f = sb("top_f", [TT, NT, 8])
        gap = sb("gap", [TT, NT])
        egap = sb("egap", [TT, NT])
        den = sb("den", [TT, NT])
        route = sb("route", [TT, 2, NT])
        hit = sb("hit", [TT, 2, NT, E])
        hit_w = sb("hit_w", [TT, 2, NT, E])
        comb = sb("comb", [TT, NT, E])
        c_stack = sb("c_stack", [EST * E, T], F32R)
        c_lo = sb("c_lo", [E, T], F32R)
        xg_sb = sb("xg_sb", [P, 2, HALF])
        free_rows = keep["outT"][:].rearrange("p b n -> p (b n)")
        prod = free_rows[:, 0:3 * HALF].rearrange("p (n t) -> p n t", n=3)
        prod_hi = sb("prod_hi", [P, 3, HALF], F32R)
        prod_lo = sb("prod_lo", [P, 3, HALF], F32R)
        ffT = free_rows[:, 3 * HALF:3 * HALF + KT * T].rearrange("p (m t) -> p m t", m=KT)
        resid3 = y_sb = tmp
        ps = ctx.enter_context(nc.psum_tensor("psC", [P, 8, 512], F32))
        psb = ps[:, :, :].bitcast(BF16)

        load = {n: sem(f"in_{n}") for n in ("wo", "w", "gate", "atom_w", "atoms", "imp", "idx_row", "idx_col", "rows")}
        consts = sem("consts")
        channels = sem("channels")
        wo_steps = sem("wo_steps")
        wo_int_ready = sem("wo_int_ready")
        diag_ready = sem("diag_o_ready")
        W_T, GATE_T, WO_T, SCALE_ROW, ATOM_T, DELTAS = range(1, 7)
        prepared_in_psum = sem("prepared_in_psum")
        prepared_out = sem("prepared_out")
        wT_lo_ready = sem("wfT_lo_ready")
        atom_steps = sem("atom_steps")
        atom_exp = sem("atom_exp")
        sig_exp = sem("sig_exp")
        sig_steps = sem("sig_steps")
        sig_stored = sem("sig_stored")
        sig_in = sem("sig_in")
        w8_ready = sem("w8_ready")
        w8_hi_ready = sem("w8_hi_ready")
        w8_lo_ready = sem("w8_lo_ready")
        w_stacked = sem("w_stacked")
        idx_steps = sem("idx_steps")
        rsums_ready = sem("rsums_ready")
        x1_bo_ready = sem("x1_bo_ready")
        o_in_psum = sem("o_in_psum")
        o_normed = sem("o_normed")
        o_moved = sem("o_moved")
        o_ready = sem("o_ready")
        o_steps = sem("o_steps")
        o_int_ready = sem("o_int_ready")
        o_intT_in_psum = sem("o_intT_in_psum")
        o_intT_ready = sem("o_intT_ready")
        y_in_psum = sem("y_in_psum")
        y_scaled = sem("y_scaled")
        resid_ready = sem("resid2_ready")
        stats_ready = sem("stats2_ready")
        mv_ready = sem("mv2_ready")
        var_ready = sem("var2_ready")
        rstd_ready = sem("rstd2_ready")
        x2_ready = sem("x2_ready")
        x2T_in_psum = sem("x2T_in_psum")
        x2T_hi_ready = sem("x2T_hi_ready")
        x2T_lo_ready = sem("x2T_lo_ready")
        logits_in_psum = sem("logits_in_psum")
        route_steps = sem("route_steps")
        egap_ready = sem("egap_ready")
        combT_in_psum = sem("combT_in_psum")
        c_hi_ready = sem("c_hi_ready")
        c_lo_ready = sem("c_lo_ready")
        c_stacked = [sem(f"c_stacked{h}") for h in range(2)]
        xg_in_psum = sem("xg_in_psum")
        xg_copied = sem("xg_copied")
        vals_in_psum = sem("vals_in_psum")
        prod_ready = sem("prod_ready")
        prod_hi_ready = sem("prod_hi_ready")
        prod_lo_ready = sem("prod_lo_ready")
        contributed = sem("contributed")
        ff_copied = sem("ff_copied")
        ff_in_psum = sem("ff_in_psum")
        resid3_ready = sem("resid3_ready")
        y_ready = sem("y_ready")
        stored = sem("stored")

        def row(ap, n, width=D):
            return ap.unsqueeze(0).broadcast_to([n, width])

        def half(h):
            return slice(h * HALF, (h + 1) * HALF)

        def tiles(h):
            return range(h * HT, (h + 1) * HT)

        UNIT = [(h, j) for h in range(2) for j in range(NST)]
        LAG = 2

        with nc.Block() as block:

            @block.sync
            def _(sp):
                rows = lambda a: a.rearrange("(k p) d -> p k d", p=P)
                sp.dma_start(wo_raw[:], rows(io["L0_xattn_wo"])).then_inc(load["wo"], 16)
                sp.dma_start(bo_row[:], row(io["L0_xattn_bo"], TT)).then_inc(load["rows"], 16)
                sp.dma_start(bv_row[:], row(io["L0_xattn_bv"], TT)).then_inc(load["rows"], 16)
                sp.dma_start(w_raw[:], rows(io["L0_ffn_W"])).then_inc(load["w"], 16)
                sp.dma_start(gate_raw[:], io["L0_ffn_gate_w"]).then_inc(load["gate"], 16)
                sp.dma_start(atom_w[:], io["L0_ffn_expert_atom_weights"]).then_inc(load["atom_w"], 16)
                sp.dma_start(gate_imp[:], io["L0_ffn_importance"].rearrange("e (a c) -> (e a) c", c=E * NS // P)).then_inc(load["imp"], 16)
                sp.dma_start(atoms[:], io["L0_ffn_atoms"]).then_inc(load["atoms"], 16)
                sp.dma_start(idx_col[:], io["L0_ffn_mask_idx"].rearrange("(j p) -> p j", p=P),
                             allow_slow_non_contiguous=True).then_inc(load["idx_col"], 16)
                sp.dma_start(idx_row[:], row(io["L0_ffn_mask_idx"], P, NS)).then_inc(load["idx_row"], 16)
                sp.wait_ge(sig_steps, 2)
                sp.dma_start(io["sig"].rearrange("e (a c) -> (e a) c", c=E * NS // P), gate_sig[:]).then_inc(sig_stored, 16)
                sp.wait_ge(sig_stored, 16)
                sp.dma_start(sig8[:], io["sig"]).then_inc(sig_in, 16)
                sp.wait_ge(w8_lo_ready, 1)
                sp.dma_start(w_stack[E:2 * E].bitcast(F32), w8_lo[:].bitcast(F32)).then_inc(w_stacked, 16)
                sp.dma_start(w_stack[2 * E:3 * E].bitcast(F32), w_stack[0:E].bitcast(F32)).then_inc(w_stacked, 16)
                for h in range(2):
                    sp.wait_ge(c_hi_ready, h + 1)
                    sp.dma_start(c_stack[E:2 * E, half(h)].bitcast(F32), c_stack[0:E, half(h)].bitcast(F32)).then_inc(c_stacked[h], 16)
                    sp.wait_ge(c_lo_ready, h + 1)
                    sp.dma_start(c_stack[2 * E:3 * E, half(h)].bitcast(F32), c_lo[:, half(h)].bitcast(F32)).then_inc(c_stacked[h], 16)
                for h in range(2):
                    sp.wait_ge(y_ready, (h + 1) * HT)
                    sp.dma_start(io["out"].rearrange("b s d -> (b s) d").rearrange("(i p) d -> p i d", p=TT)[:, h * HT:(h + 1) * HT],
                                 y_sb[:, h * HT:(h + 1) * HT]).then_inc(stored, 16)
                sp.wait_ge(stored, 32)

            @block.gpsimd
            def _(pool):
                nc.gpsimd.iota(channel[:], pattern=[[P, KT]], base=0, channel_multiplier=1,
                               allow_small_or_imprecise_dtypes=True).then_inc(channels, 1)
                nc.gpsimd.iota(channel_row[:], pattern=[[1, D]], base=0, channel_multiplier=0,
                               allow_small_or_imprecise_dtypes=True).then_inc(channels, 1)
                nc.gpsimd.iota(expert_row[:], pattern=[[1, E]], base=0, channel_multiplier=0,
                               allow_small_or_imprecise_dtypes=True).then_inc(channels, 1)
                nc.gpsimd.memset(minus_half[:], -0.5).then_inc(channels, 1)
                pool.wait_ge(channels, 4)
                for h in range(2):
                    g = slice(h * HT, (h + 1) * HT)
                    pool.wait_ge(var_ready, h + 1)
                    nc.gpsimd.tensor_tensor(rstd[:, 0, g], var_eps[:, 0, g], minus_half[:, g], ALU.pow).then_inc(rstd_ready, 1)
                for n, (h, j) in enumerate(UNIT):
                    pool.wait_ge(prod_hi_ready, n + 1)
                    nc.gpsimd.tensor_tensor(prod_lo[:, n % 3], prod[:, n % 3], prod_hi[:, n % 3].bitcast(F32), ALU.subtract).then_inc(prod_lo_ready, 1)
                for h in range(2):
                    g = slice(h * HT, (h + 1) * HT)
                    pool.wait_ge(var_ready, 2 + h + 1)
                    nc.gpsimd.tensor_tensor(rstd[:, 1, g], var_eps[:, 1, g], minus_half[:, g], ALU.pow).then_inc(rstd_ready, 1)

            @block.tensor
            def _(pe):
                pe.wait_ge(load["w"], 16)
                for m in range(KT):
                    for e in range(KT):
                        last = nc.tensor.transpose(ps[:, 0, m * D + e * P:m * D + (e + 1) * P], w_raw[:, e, m * P:(m + 1) * P], keep["ident"][:])
                last.then_inc(prepared_in_psum, 1)
                pe.wait_ge(load["gate"], 16)
                for m in range(KT):
                    last = nc.tensor.transpose(ps[:, 3, m * E:(m + 1) * E], gate_raw[:, m * P:(m + 1) * P], keep["ident"][0:E, 0:E])
                last.then_inc(prepared_in_psum, 1)
                pe.wait_ge(wo_int_ready, 1)
                for m in range(KT):
                    for e in range(KT):
                        last = nc.tensor.transpose(psb[:, 1, m * D + e * P:m * D + (e + 1) * P], wo_int[:, e, m * P:(m + 1) * P], keep["ident_b"][:])
                last.then_inc(prepared_in_psum, 1)
                pe.wait_ge(consts, 1)
                pe.wait_ge(diag_ready, KT)
                for e in range(KT):
                    last = nc.tensor.matmul(ps[0:TT, 2, e * P:(e + 1) * P], ones[:], diag[:, e], start=True, stop=True)
                last.then_inc(prepared_in_psum, 1)
                pe.wait_ge(atom_steps, 5)
                pe.wait_ge(prepared_out, GATE_T)
                nc.tensor.transpose(ps[0:A_ATOMS, 3, 0:E], atom_pn[:], keep["ident"][0:E, 0:E]).then_inc(prepared_in_psum, 1)
                pe.wait_ge(prepared_out, ATOM_T)
                pe.wait_ge(load["atoms"], 16)
                for n in range(4):
                    last = nc.tensor.matmul(ps[0:E, 4 + n, :], atom_pT[:], atoms[:, n * 512:(n + 1) * 512], start=True, stop=True)
                last.then_inc(prepared_in_psum, 1)

                pe.wait_ge(wT_lo_ready, 1)
                pe.wait_ge(prepared_out, WO_T)
                pe.wait_ge(prepared_out, SCALE_ROW)

                def out_transpose(i):
                    if i >= 2:
                        pe.wait_ge(o_normed, i - 1)
                    for b in range(2):
                        for g in range(2):
                            last = nc.tensor.transpose(ps[0:PN, i % 2, b * D + g * P:b * D + (g + 1) * P],
                                                       keep["outT"][:, 2 * i + b, g * PN:(g + 1) * PN], keep["ident"][:])
                    last.then_inc(o_in_psum, 1)

                out_transpose(0)
                out_transpose(1)
                for i in range(NT):
                    if i % 2 == 0 and i >= 4:
                        pe.wait_ge(o_ready, i - 2)
                    pe.wait_ge(o_normed, i + 1)
                    for e in range(2):
                        dst = ps[0:TT, 2 + i // 2 % 2, (i % 2) * D:(i % 2 + 1) * D].rearrange("p (k e d) -> p k e d", k=NP, e=2)[:, :, e]
                        for a in range(2):
                            last = nc.tensor.matmul(dst, keep["sel"][:, 2 * e + a], o_norm[:, i % 2, a * NP:(a + 1) * NP, e * DH:(e + 1) * DH],
                                                    start=a == 0, stop=a == 1)
                    last.then_inc(o_moved, 1)
                    if i + 2 < NT:
                        out_transpose(i + 2)
                pe.wait_ge(w8_ready, 1)
                for h in range(2):
                    for j, i in enumerate(tiles(h)):
                        pe.wait_ge(o_int_ready, i + 1)
                        for m in range(KT):
                            last = nc.tensor.transpose(psb[:, 4 + h, m * HALF + j * TT:m * HALF + (j + 1) * TT],
                                                       o_int[:, i, m * P:(m + 1) * P], keep["ident_b"][0:TT, 0:TT])
                    last.then_inc(o_intT_in_psum, 1)
                    pe.wait_ge(o_intT_ready, h + 1)
                    for i in tiles(h):
                        if i % 2 == 0 and i >= 4:
                            pe.wait_ge(y_scaled, i - 2)
                        for m in range(KT):
                            last = nc.tensor.matmul(ps[0:TT, 6 + i // 2 % 2, (i % 2) * D:(i % 2 + 1) * D],
                                                    o_intT[:, m, i * TT:(i + 1) * TT], wo_intT[:, m], start=m == 0, stop=m == KT - 1)
                        last.then_inc(y_in_psum, 1)
                pe.wait_ge(o_ready, NT)
                for h in range(2):
                    pe.wait_ge(x2_ready, (h + 1) * HT)
                    for m in range(KT):
                        for j, i in enumerate(tiles(h)):
                            last = nc.tensor.transpose(ps[:, 2 * h + m, j * TT:(j + 1) * TT], x2[:, i, m * P:(m + 1) * P], keep["ident"][0:TT, 0:TT])
                        last.then_inc(x2T_in_psum, 1)
                pe.wait_ge(y_scaled, NT)
                for h in range(2):
                    pe.wait_ge(x2T_lo_ready, KT * (h + 1))
                    for i in tiles(h):
                        mm = [(part[:, m, i * TT:(i + 1) * TT].bitcast(F32), gateT[:, m]) for m in range(KT) for part in (x2T_hi, x2T_lo)]
                        for n, (x, g) in enumerate(mm):
                            last = nc.tensor.matmul(ps[0:TT, 6, i * E:(i + 1) * E], x, g, start=n == 0, stop=n == len(mm) - 1)
                last.then_inc(logits_in_psum, 1)
                def dense(h):
                    for m in range(KT):
                        e = slice(m * P, (m + 1) * P)
                        mm = [t for k in range(KT) for t in ((wT_hi[:, k, e], x2T_hi[:, k, half(h)]), (wT_hi[:, k, e], x2T_lo[:, k, half(h)]),
                                                             (wT_lo[:, k, e], x2T_hi[:, k, half(h)]))]
                        for n, (w, x) in enumerate(mm):
                            nc.tensor.matmul(ps[:, 4 + 2 * h + m, 0:HALF], w, x, start=n == 0, stop=False)

                pe.wait_ge(o_intT_ready, 2)
                dense(0)

                def gather(n):
                    h, j = UNIT[n]
                    if n >= 2:
                        pe.wait_ge(xg_copied, n - 1)
                    mm = [(pick_c[:, m, j * P:(j + 1) * P], part[:, m, half(h)]) for m in range(KT) for part in (x2T_hi, x2T_lo)]
                    for k, (w, x) in enumerate(mm):
                        last = nc.tensor.matmul(ps[:, n % 2, 0:HALF], w, x, start=k == 0, stop=k == len(mm) - 1)
                    last.then_inc(xg_in_psum, 1)

                def values(n):
                    h, j = UNIT[n]
                    if n >= 2:
                        pe.wait_ge(prod_ready, n - 1)
                    if j == 0:
                        pe.wait_ge(c_stacked[h], 32)
                    nc.tensor.matmul(ps[:, 2 + n % 2, 0:HALF], w_stack[:, j * P:(j + 1) * P], c_stack[:, half(h)],
                                     start=True, stop=True).then_inc(vals_in_psum, 1)

                def scatter(n):
                    h, j = UNIT[n]
                    pe.wait_ge(prod_lo_ready, n + 1)
                    for m in range(KT):
                        for part in (prod_hi, prod_lo):
                            last = nc.tensor.matmul(ps[:, 4 + 2 * h + m, 0:HALF], pick_r[:, j, m * P:(m + 1) * P], part[:, n % 3],
                                                    start=False, stop=j == NST - 1 and part is prod_lo)
                    last.then_inc(contributed, 1)

                def back(h):
                    pe.wait_ge(ff_copied, KT * (h + 1))
                    for j, i in enumerate(tiles(h)):
                        for m in range(KT):
                            last = nc.tensor.transpose(ps[0:TT, 4 + 2 * h + j // 2, (j % 2) * D + m * P:(j % 2) * D + (m + 1) * P],
                                                       ffT[:, m, i * TT:(i + 1) * TT], keep["ident"][:])
                        if j % 2:
                            last.then_inc(ff_in_psum, 1)

                pe.wait_ge(idx_steps, 4 + KT + NST)
                gather(0)
                gather(1)
                pe.wait_ge(route_steps, ROUTE_STEPS)
                for h in range(2):
                    if h == 1:
                        pe.wait_ge(c_lo_ready, 1)
                    for j, i in enumerate(tiles(h)):
                        last = nc.tensor.transpose(ps[0:E, 7, j * TT:(j + 1) * TT], comb[:, i], keep["ident"][0:TT, 0:TT])
                    last.then_inc(combT_in_psum, 1)
                pe.wait_ge(w_stacked, 32)
                pe.wait_ge(c_lo_ready, 2)
                for n, (h, j) in enumerate(UNIT):
                    if n >= 2:
                        gather(n)
                    values(n)
                    if n >= LAG:
                        scatter(n - LAG)
                    if (h, j) == (0, 8):
                        dense(1)
                    if (h, j) == (1, 6):
                        back(0)
                scatter(len(UNIT) - 2)
                scatter(len(UNIT) - 1)
                back(1)

            @block.scalar
            def _(act):
                act.wait_ge(prepared_in_psum, W_T)
                nc.scalar.activation(wT_hi[:], split(ps[:, 0], KT), ACT.Copy).then_inc(prepared_out, 1)
                act.wait_ge(prepared_in_psum, GATE_T)
                nc.scalar.activation(gateT[:], split(ps[:, 3, 0:KT * E], KT), ACT.Copy).then_inc(prepared_out, 1)
                act.wait_ge(load["imp"], 16)
                nc.scalar.activation(gate_sig[:], gate_imp[:], ACT.Exp, scale=-1.0).then_inc(sig_exp, 1)
                act.wait_ge(atom_steps, 1)
                nc.scalar.activation(atom_p[:], atom_w[:], ACT.Exp, bias=atom_shift[:, 0:1], accum_out=atom_sum[:, 0:1]).then_inc(atom_exp, 1)
                act.wait_ge(prepared_in_psum, WO_T)
                nc.scalar.activation(wo_intT[:], split(psb[:, 1, 0:KT * D], KT), ACT.Copy).then_inc(prepared_out, 1)
                act.wait_ge(prepared_in_psum, SCALE_ROW)
                nc.scalar.activation(wo_scale_row[:], ps[0:TT, 2, 0:D], ACT.Copy).then_inc(prepared_out, 1)
                act.wait_ge(prepared_in_psum, ATOM_T)
                nc.scalar.activation(atom_pT[:], ps[0:A_ATOMS, 3, 0:E], ACT.Copy).then_inc(prepared_out, 1)
                act.wait_ge(w8_ready, 1)
                nc.scalar.activation(w_stack[0:E], w8[:], ACT.Copy).then_inc(w8_hi_ready, 1)
                for h in range(2):
                    for m in range(KT):
                        act.wait_ge(x2T_in_psum, KT * h + m + 1)
                        nc.scalar.activation(x2T_hi[:, m, half(h)], ps[:, 2 * h + m, 0:HALF], ACT.Copy).then_inc(x2T_hi_ready, 1)
                act.wait_ge(route_steps, NT + 2)
                nc.scalar.activation(egap[:], gap[:], ACT.Exp).then_inc(egap_ready, 1)
                def routing_hi(h):
                    act.wait_ge(combT_in_psum, h + 1)
                    nc.scalar.activation(c_stack[0:E, half(h)], ps[0:E, 7, 0:HALF], ACT.Copy).then_inc(c_hi_ready, 1)

                def gathered(n):
                    act.wait_ge(xg_in_psum, n + 1)
                    if n >= 2:
                        act.wait_ge(prod_ready, n - 1)
                    nc.scalar.activation(xg_sb[:, n % 2], ps[:, n % 2, 0:HALF], ACT.Copy).then_inc(xg_copied, 1)

                gathered(0)
                routing_hi(0)
                routing_hi(1)
                gathered(1)
                for n, (h, j) in enumerate(UNIT):
                    act.wait_ge(prod_ready, n + 1)
                    if n >= 3:
                        act.wait_ge(contributed, n - 2)
                    nc.scalar.activation(prod_hi[:, n % 3], prod[:, n % 3], ACT.Copy).then_inc(prod_hi_ready, 1)
                    if n + 2 < len(UNIT):
                        gathered(n + 2)
                    if (h, j) == (1, 3):
                        act.wait_ge(contributed, NST)
                        for m in range(KT):
                            nc.scalar.activation(ffT[:, m, half(0)], ps[:, 4 + m, 0:HALF], ACT.Copy).then_inc(ff_copied, 1)
                act.wait_ge(contributed, 2 * NST)
                for m in range(KT):
                    nc.scalar.activation(ffT[:, m, half(1)], ps[:, 6 + m, 0:HALF], ACT.Copy).then_inc(ff_copied, 1)

            @block.vector
            def _(dve):
                nc.vector.memset(ones[:], 1.0).then_inc(consts, 1)
                nc.vector.reciprocal(rsums[:], keep["sums"][:]).then_inc(rsums_ready, 1)
                dve.wait_ge(load["wo"], 16)
                nc.vector.tensor_reduce(wo_scale[:], wo_raw[:], AX.X, ALU.max, apply_absolute_value=True).then_inc(wo_steps, 1)
                dve.wait_ge(wo_steps, 1)
                nc.vector.tensor_scalar(wo_scale[:], wo_scale[:], 1.0 / QMAX, QEPS, ALU.mult, ALU.max).then_inc(wo_steps, 1)
                dve.wait_ge(wo_steps, 2)
                nc.vector.reciprocal(wo_inv[:], wo_scale[:]).then_inc(wo_steps, 1)
                for e in range(KT):
                    nc.vector.tensor_scalar(diag[:, e], keep["ident"][:], wo_scale[:, e:e + 1], None, ALU.mult).then_inc(diag_ready, 1)
                dve.wait_ge(wo_steps, 3)
                for e in range(KT):
                    nc.vector.tensor_scalar(wo_tmp[:, e], wo_raw[:, e], wo_inv[:, e:e + 1], ROUND, ALU.mult, ALU.add).then_inc(wo_steps, 1)
                dve.wait_ge(wo_steps, 5)
                nc.vector.tensor_scalar(wo_tmp[:], wo_tmp[:], ROUND, QMAX, ALU.subtract, ALU.min).then_inc(wo_steps, 1)
                dve.wait_ge(wo_steps, 6)
                nc.vector.tensor_scalar(wo_int[:], wo_tmp[:], -QMAX, None, ALU.max).then_inc(wo_int_ready, 1)
                dve.wait_ge(load["rows"], 32)
                nc.vector.tensor_tensor(x1_bo[:], keep["x1"][:], bo_row[:].unsqueeze(1).broadcast_to([TT, NT, D]), ALU.add).then_inc(x1_bo_ready, 1)
                dve.wait_ge(load["atom_w"], 16)
                nc.vector.tensor_reduce(atom_shift[:], atom_w[:], AX.X, ALU.max, negate=True).then_inc(atom_steps, 1)
                dve.wait_ge(prepared_out, W_T)
                nc.vector.tensor_tensor(wT_lo[:], split(ps[:, 0], KT), wT_hi[:].bitcast(F32), ALU.subtract).then_inc(wT_lo_ready, 1)
                dve.wait_ge(atom_exp, 1)
                nc.vector.reciprocal(atom_rsum[:], atom_sum[:]).then_inc(atom_steps, 1)
                dve.wait_ge(atom_steps, 2)
                nc.vector.tensor_scalar(atom_pn[:], atom_p[:], atom_rsum[:, 0:1], None, ALU.mult).then_inc(atom_steps, 3)
                dve.wait_ge(sig_exp, 1)
                nc.vector.tensor_scalar(gate_sig[:], gate_sig[:], 1.0, None, ALU.add).then_inc(sig_steps, 1)
                dve.wait_ge(sig_steps, 1)
                nc.vector.reciprocal(gate_sig[:], gate_sig[:]).then_inc(sig_steps, 1)

                def moved_pair(i):
                    dve.wait_ge(o_moved, i + 2)
                    nc.vector.tensor_tensor(o_sb[:, i:i + 2], split(ps[0:TT, 2 + i // 2 % 2], 2), bv_row[:].unsqueeze(1).broadcast_to([TT, 2, D]),
                                            ALU.add).then_inc(o_ready, 2)

                dve.wait_ge(rsums_ready, 1)
                for i in range(NT):
                    dve.wait_ge(o_in_psum, i + 1)
                    if i >= 2:
                        dve.wait_ge(o_moved, i - 1)
                    nc.vector.tensor_tensor(o_norm[:, i % 2], ps[0:PN, i % 2].rearrange("p (k d) -> p k d", d=PD),
                                            rsums[:, 2 * i:2 * i + 2].rearrange("p b k -> p (b k)").unsqueeze(2).broadcast_to([PN, 2 * NP, PD]),
                                            ALU.mult).then_inc(o_normed, 1)
                    if i % 2 == 0 and i >= 2:
                        moved_pair(i - 2)
                    if i == 1:
                        dve.wait_ge(prepared_in_psum, DELTAS)
                        dve.wait_ge(sig_in, 16)
                        nc.vector.tensor_tensor(w8[:].rearrange("p (a b) -> p a b", a=4), ps[0:E, 4:8], sig8[:].rearrange("p (a b) -> p a b", a=4), ALU.mult).then_inc(w8_ready, 1)
                    if i == 3:
                        dve.wait_ge(w8_hi_ready, 1)
                        nc.vector.tensor_tensor(w8_lo[:], w8[:], w_stack[0:E].bitcast(F32), ALU.subtract).then_inc(w8_lo_ready, 1)
                moved_pair(NT - 2)

                for h in range(2):
                    g = slice(h * HT, (h + 1) * HT)
                    dve.wait_ge(o_ready, (h + 1) * HT)
                    nc.vector.tensor_reduce(o_scale[:, g], o_sb[:, g], AX.X, ALU.max, apply_absolute_value=True).then_inc(o_steps, 1)
                    dve.wait_ge(o_steps, 4 * h + 1)
                    nc.vector.tensor_scalar(o_scale[:, g], o_scale[:, g], 1.0 / QMAX, QEPS, ALU.mult, ALU.max).then_inc(o_steps, 1)
                    dve.wait_ge(o_steps, 4 * h + 2)
                    nc.vector.reciprocal(o_inv[:, g], o_scale[:, g]).then_inc(o_steps, 1)
                    dve.wait_ge(o_steps, 4 * h + 3)
                    for i in tiles(h):
                        ins = nc.vector.tensor_scalar(tmp[:, i], o_sb[:, i], o_inv[:, i:i + 1], ROUND, ALU.mult, ALU.add)
                    ins.then_inc(o_steps, 1)
                    dve.wait_ge(o_steps, 4 * h + 4)
                    for i in tiles(h):
                        nc.vector.tensor_scalar(o_int[:, i], tmp[:, i], ROUND, QMAX, ALU.subtract, ALU.min).then_inc(o_int_ready, 1)
                    dve.wait_ge(o_intT_in_psum, h + 1)
                    nc.vector.tensor_scalar(o_intT[:, :, half(h)], split(psb[:, 4 + h, 0:KT * HALF], KT), -QMAX, None, ALU.max).then_inc(o_intT_ready, 1)

                def normalise(n, h, src, dst, done, base):
                    g = slice(h * HT, (h + 1) * HT)
                    for i in tiles(h):
                        nc.vector.bn_stats(stats[:, n, i], src[:, i]).then_inc(stats_ready, 1)
                    for i in tiles(h):
                        dve.wait_ge(stats_ready, n * NT + i + 1)
                        nc.vector.bn_aggr(mv[:, n, i], stats[:, n, i]).then_inc(mv_ready, 1)
                    dve.wait_ge(mv_ready, n * NT + (h + 1) * HT)
                    nc.vector.tensor_scalar(var_eps[:, n, g], mv[:, n, g, 1], LN_EPS, None, ALU.add).then_inc(var_ready, 1)

                def centre(n, h, src, dst, done):
                    dve.wait_ge(rstd_ready, 2 * n + h + 1)
                    for i in tiles(h):
                        nc.vector.tensor_scalar(dst[:, i], src[:, i], mv[:, n, i, 0:1], rstd[:, n, i:i + 1], ALU.subtract, ALU.mult).then_inc(done, 1)

                dve.wait_ge(prepared_out, SCALE_ROW)
                dve.wait_ge(x1_bo_ready, 1)
                for h in range(2):
                    for i in tiles(h):
                        if i % 2 == 0:
                            dve.wait_ge(y_in_psum, i + 2)
                        nc.vector.scalar_tensor_tensor(out=tmp[:, i], in0=ps[0:TT, 6 + i // 2 % 2, (i % 2) * D:(i % 2 + 1) * D],
                                                       scalar=o_scale[:, i:i + 1], in1=wo_scale_row[:], op0=ALU.mult, op1=ALU.mult).then_inc(y_scaled, 1)
                    g = slice(h * HT, (h + 1) * HT)
                    dve.wait_ge(y_scaled, (h + 1) * HT)
                    nc.vector.tensor_tensor(resid[:, g], tmp[:, g], x1_bo[:, g], ALU.add).then_inc(resid_ready, 1)
                    dve.wait_ge(resid_ready, h + 1)
                    normalise(0, h, resid, x2, x2_ready, 0)
                for h in range(2):
                    centre(0, h, resid, x2, x2_ready)
                dve.wait_ge(load["idx_row"], 16)
                dve.wait_ge(load["idx_col"], 16)
                dve.wait_ge(channels, 4)
                nc.vector.tensor_single_scalar(col_i[:], idx_row[:], D - 1, ALU.bitwise_and).then_inc(idx_steps, 1)
                nc.vector.tensor_single_scalar(row_i[:], idx_col[:], 8, ALU.arith_shift_right).then_inc(idx_steps, 1)
                dve.wait_ge(idx_steps, 2)
                nc.vector.tensor_copy(row_f[:], row_i[:]).then_inc(idx_steps, 2)
                for m in range(KT):
                    nc.vector.tensor_scalar(pick_c[:, m], col_i[:], channel[:, m:m + 1], None, ALU.is_equal).then_inc(idx_steps, 1)
                dve.wait_ge(idx_steps, 4)
                for h in range(2):
                    for m in range(KT):
                        dve.wait_ge(x2T_hi_ready, KT * h + m + 1)
                        nc.vector.tensor_tensor(x2T_lo[:, m, half(h)], ps[:, 2 * h + m, 0:HALF], x2T_hi[:, m, half(h)].bitcast(F32), ALU.subtract).then_inc(x2T_lo_ready, 1)
                for j in range(NST):
                    nc.vector.tensor_scalar(pick_r[:, j], channel_row[:], row_f[:, j:j + 1], None, ALU.is_equal).then_inc(idx_steps, 1)

                step = [0]

                def routed(ins, wait=True):
                    step[0] += 1
                    ins.then_inc(route_steps, 1)
                    if wait:
                        dve.wait_ge(route_steps, step[0])

                dve.wait_ge(logits_in_psum, 1)
                routed(nc.vector.tensor_scalar(logits[:], ps[0:TT, 6, 0:NT * E].rearrange("p (i e) -> p i e", e=E), CLIP, -CLIP, ALU.min, ALU.max))
                for i in range(NT):
                    routed(nc.vector.max(top[:, i], logits[:, i]), wait=i == NT - 1)
                routed(nc.vector.tensor_tensor(gap[:], top[:, :, 1], top[:, :, 0], ALU.subtract), wait=False)
                for i in range(NT):
                    routed(nc.vector.max_index(top_i[:, i], top[:, i], logits[:, i]), wait=i == NT - 1)
                routed(nc.vector.tensor_copy(top_f[:], top_i[:]))
                dve.wait_ge(egap_ready, 1)
                routed(nc.vector.tensor_scalar(den[:], egap[:], 1.0, None, ALU.add))
                routed(nc.vector.reciprocal(route[:, 0], den[:]))
                routed(nc.vector.tensor_tensor(route[:, 1], egap[:], route[:, 0], ALU.mult), wait=False)
                for n in range(2):
                    routed(nc.vector.tensor_tensor(hit[:, n], expert_row[:].unsqueeze(1).broadcast_to([TT, NT, E]),
                                                   top_f[:, :, n:n + 1].broadcast_to([TT, NT, E]), ALU.is_equal), wait=n == 1)
                for n in range(2):
                    routed(nc.vector.tensor_tensor(hit_w[:, n], hit[:, n], route[:, n].unsqueeze(2).broadcast_to([TT, NT, E]), ALU.mult), wait=n == 1)
                routed(nc.vector.tensor_tensor(comb[:], hit_w[:, 0], hit_w[:, 1], ALU.add), wait=False)
                assert step[0] == ROUTE_STEPS
                for h in range(2):
                    dve.wait_ge(c_hi_ready, h + 1)
                    nc.vector.tensor_tensor(c_lo[:, half(h)], ps[0:E, 7, 0:HALF], c_stack[0:E, half(h)].bitcast(F32), ALU.subtract).then_inc(c_lo_ready, 1)

                def finish(h):
                    for j, i in enumerate(tiles(h)):
                        if j % 2 == 0:
                            dve.wait_ge(ff_in_psum, 2 * h + j // 2 + 1)
                        nc.vector.tensor_tensor(resid3[:, i], ps[0:TT, 4 + 2 * h + j // 2, (j % 2) * D:(j % 2 + 1) * D], x2[:, i], ALU.add).then_inc(resid3_ready, 1)
                    dve.wait_ge(resid3_ready, (h + 1) * HT)
                    normalise(1, h, resid3, y_sb, y_ready, 0)

                for n, (h, j) in enumerate(UNIT):
                    dve.wait_ge(xg_copied, n + 1)
                    dve.wait_ge(vals_in_psum, n + 1)
                    if n >= 3:
                        dve.wait_ge(prod_lo_ready, n - 2)
                    nc.vector.tensor_tensor(prod[:, n % 3], ps[:, 2 + n % 2, 0:HALF], xg_sb[:, n % 2], ALU.mult).then_inc(prod_ready, 1)
                    if (h, j) == (1, 12):
                        finish(0)
                finish(1)
                for h in range(2):
                    centre(1, h, resid3, y_sb, y_ready)


ROUTE_STEPS = 2 * NT + 11


def build_program(nc, io):
    with ExitStack() as ctx:
        keep = kept(nc, ctx)
        self_attention_phase(nc, io, keep)
        cross_attention_phase(nc, io, keep)
        feed_forward_phase(nc, io, keep)


_INS = ["x", "ctx_2048", "mask_BxSxS2_ff0",
        "L0_attn_Wq", "L0_attn_bq", "L0_attn_Wk", "L0_attn_bk", "L0_attn_Wv", "L0_attn_bv", "L0_attn_Wo", "L0_attn_bo",
        "L0_xattn_wq", "L0_xattn_bq", "L0_xattn_wk", "L0_xattn_bk", "L0_xattn_wv", "L0_xattn_bv", "L0_xattn_wo", "L0_xattn_bo",
        "L0_ffn_gate_w", "L0_ffn_W", "L0_ffn_atoms", "L0_ffn_expert_atom_weights", "L0_ffn_importance", "L0_ffn_mask_idx"]


def kernel(**inputs):
    import numpy as np
    import concourse.bacc as bacc
    from concourse import mybir as mb
    from concourse.bass_utils import run_bass_kernel_spmd

    nc = bacc.Bacc("TRN2", target_bir_lowering=False, num_devices=1)
    arrays, io = {}, {}
    for name in _INS:
        a = np.ascontiguousarray(inputs[name])
        arrays[f"in_{name}"] = a
        io[name] = nc.dram_tensor(f"in_{name}", a.shape, mb.dt.from_np(a.dtype), kind="ExternalInput").ap()
    io["ctx"], io["mask"] = io["ctx_2048"], io["mask_BxSxS2_ff0"]
    io["out"] = nc.dram_tensor("out_0", (B, S, D), F32, kind="ExternalOutput").ap()
    for name in ("q_hi", "q_lo"):
        io[name] = nc.dram_tensor(name, (KT, P, B, PN), F32, kind="Internal").ap()
    io["sig"] = nc.dram_tensor("sig", (E, NS), F32, kind="Internal").ap()
    build_program(nc, io)
    r = run_bass_kernel_spmd(nc, [arrays], core_ids=[0])
    return r.results[0]["out_0"]
```

```python
import concourse.bass as bass
from concourse import mybir
from contextlib import ExitStack

F32 = mybir.dt.float32
F32R = mybir.dt.float32r
BF16 = mybir.dt.bfloat16
I32 = mybir.dt.int32
U32 = mybir.dt.uint32
ALU = mybir.AluOpType
ACT = mybir.ActivationFunctionType
AX = mybir.AxisListType

B, S, D = 16, 56, 256
H, DH = 16, 16
L = 1500
P = 128
KT = D // P
T = B * S
TT = 2 * S
NT = T // TT
HALF = T // 2
HT = HALF // TT
LT = 125
LC = 500
NC = L // LC
TC = LC // LT
NL = L // LT
NP = H // 2
PD = 2 * DH
PN = 2 * S
GP = P // PD
SCALE = DH ** -0.5
QMAX = 127.0
QEPS = 1e-8
LN_EPS = 1e-5
ROUND = 1.5 * 2.0 ** 23
BIG = 3.0e38


def split(ap, n):
    return ap.rearrange("p (a b) -> p a b", a=n)


def self_attention_phase(nc, io, keep):
    ctx = ExitStack()
    with ctx:
        sb = lambda n, s, d=F32: ctx.enter_context(nc.sbuf_tensor(n, s, d))
        sem = lambda n: ctx.enter_context(nc.semaphore(n))
        WK, WV, WQ, WO, XK, XV, XQ = range(7)
        names = ["L0_attn_Wk", "L0_attn_Wv", "L0_attn_Wq", "L0_attn_Wo",
                 "L0_xattn_wk", "L0_xattn_wv", "L0_xattn_wq"]
        w_raw = sb("w_raw", [P, 7, KT, D])
        wT = sb("wT", [P, 4, KT, D])
        x_sb = sb("x_sb", [TT, NT, D])
        xT = sb("xT", [P, KT, T])
        qkv_bias = sb("qkv_bias", [P, 3, KT])
        neg_bias = sb("neg_bias", [P, 3, KT])
        bo_row = sb("bo_row", [TT, D])
        xbq_row = sb("xbq_row", [TT, D])
        relu_pos = sb("relu_pos", [P, 4, 2, HALF])
        relu_neg = sb("relu_neg", [P, 4, 2, HALF])
        phi = sb("phi", [P, 4, 2, HALF])
        kv = sb("kv", [P, 4, HALF])
        kv_sum = sb("kv_sum", [P, 4, HALF])
        context = sb("context", [P, KT, T])
        keep_going = sb("keep_going", [P, HALF])
        def tokens_in(buf):
            return buf[0:TT].rearrange("p u n c -> p (u n c)")[:, 0:NT * D].rearrange("p (i d) -> p i d", i=NT)
        resid = tokens_in(relu_neg)
        stats = sb("stats", [TT, NT, 6])
        mv = sb("mv", [TT, NT, 2])
        var_eps = sb("var_eps", [TT, NT])
        minus_half = sb("minus_half", [TT, NT])
        rstd = sb("rstd", [TT, NT])
        wq_scale = sb("wq_scale", [P, KT])
        wq_inv = sb("wq_inv", [P, KT])
        wq_tmp = sb("wq_tmp", [P, KT, D])
        wq_int = sb("wq_int", [P, KT, D], BF16)
        wq_intT = sb("wq_intT", [P, KT, D], BF16)
        diag = sb("diag", [P, KT, P])
        ones = sb("ones", [P, TT])
        wq_scale_row = sb("wq_scale_row", [TT, D])
        x_scale = sb("x_scale", [TT, NT])
        x_inv = sb("x_inv", [TT, NT])
        x_tmp = tokens_in(phi)
        x_int = sb("x_int", [TT, NT, D], BF16)
        x_intT = sb("x_intT", [P, KT, T], BF16)
        head_of = sb("head_of", [P, 2 * GP])
        head_mask = sb("head_mask", [P, 2])
        query = sb("query", [TT, NT, D])
        q_scaled = sb("q_scaled", [TT, NT, D])
        qbd = relu_pos[:].rearrange("p u n c -> p (u n c)").rearrange("p (m b e s) -> p m b e s", m=KT, b=B, e=2)
        qbd_hi = sb("qbd_hi", [P, KT, B, 2, S], F32R)
        qbd_lo = sb("qbd_lo", [P, KT, B, 2, S], F32R)
        ps = ctx.enter_context(nc.psum_tensor("psA", [P, 8, 512], F32))
        psb = ps[:, :, :].bitcast(BF16)

        x_in = sem("x_in")
        w_in = [sem(f"w_in{k}") for k in range(7)]
        bias_in = sem("bias_in")
        row_in = sem("row_in")
        const_set = sem("const_set")
        dve_const = sem("dve_const")
        ident_ready = sem("ident_ready")
        identb_ready = sem("identb_ready")
        sel_ready = sem("sel_ready")
        head_of_ready = sem("head_of_ready")
        mask_ready = sem("mask_ready")
        xT_in_psum = sem("xT_in_psum")
        xT_dve = sem("xT_dve")
        xT_act = sem("xT_act")
        wT_in_psum = sem("wT_in_psum")
        wT_act = sem("wT_act")
        wT_lo = sem("wT_lo")
        qkv_in_psum = sem("qkv_in_psum")
        relus = sem("relus")
        exps = sem("exps")
        phis = sem("phis")
        v_used = sem("v_used")
        scanned = sem("scanned")
        context_ready = sem("context_ready")
        attn_in_psum = sem("attn_in_psum")
        xbo_ready = sem("xbo_ready")
        resid_ready = sem("resid_ready")
        stats_ready = sem("stats_ready")
        mv_ready = sem("mv_ready")
        var_ready = sem("var_ready")
        rstd_ready = sem("rstd_ready")
        x1_ready = sem("x1_ready")
        wq_steps = sem("wq_steps")
        wq_int_ready = sem("wq_int_ready")
        diag_ready = sem("diag_ready")
        wqT_in_psum = sem("wqT_in_psum")
        wqT_ready = sem("wqT_ready")
        row_in_psum = sem("row_in_psum")
        row_ready = sem("row_ready")
        x_steps = sem("x_steps")
        x_int_ready = sem("x_int_ready")
        x_intT_in_psum = sem("x_intT_in_psum")
        x_intT_ready = sem("x_intT_ready")
        q_in_psum = sem("q_in_psum")
        q_scaled_ready = sem("q_scaled_ready")
        query_ready = sem("query_ready")
        qT_in_psum = sem("qT_in_psum")
        qbd_ready = sem("qbd_ready")
        qbd_hi_ready = sem("qbd_hi_ready")
        qbd_lo_ready = sem("qbd_lo_ready")
        q_stored = sem("q_stored")

        def column(ap):
            return ap.rearrange("(k p) -> p k", k=KT)

        def row(ap, n):
            return ap.unsqueeze(0).broadcast_to([n, D])

        with nc.Block() as block:

            @block.sync
            def _(sp):
                sp.dma_start(x_sb[:], io["x"].rearrange("b s d -> (b s) d").rearrange("(i p) d -> p i d", p=TT)
                             ).then_inc(x_in, 16)
                for k in range(7):
                    sp.dma_start(w_raw[:, k], io[names[k]].rearrange("(k p) d -> p k d", p=P)).then_inc(w_in[k], 16)
                for h in range(2):
                    for m in range(KT):
                        bs = slice(h * B // 2, (h + 1) * B // 2)
                        sp.wait_ge(qbd_hi_ready, 2 * h + m + 1)
                        sp.dma_start(io["q_hi"][m, :, bs], qbd_hi[:, m, bs].bitcast(F32).rearrange("p b e n -> p b (e n)")).then_inc(q_stored, 16)
                        sp.wait_ge(qbd_lo_ready, 2 * h + m + 1)
                        sp.dma_start(io["q_lo"][m, :, bs], qbd_lo[:, m, bs].bitcast(F32).rearrange("p b e n -> p b (e n)")).then_inc(q_stored, 16)
                sp.wait_ge(q_stored, 16 * 4 * KT)

            @block.gpsimd
            def _(pool):
                nc.gpsimd.memset(keep["ident"][:], 0.0).then_inc(const_set, 1)
                nc.gpsimd.memset(keep["sel"][:], 0.0).then_inc(const_set, 1)
                nc.gpsimd.memset(head_of[:], 1.0).then_inc(const_set, 1)
                nc.gpsimd.memset(minus_half[:], -0.5).then_inc(const_set, 1)
                pool.wait_ge(const_set, 4)
                nc.gpsimd.affine_select(out=keep["ident"][:], in_=keep["ident"][:], compare_op=ALU.not_equal,
                                        fill=1.0, base=0, pattern=[[-1, P]], channel_multiplier=1).then_inc(ident_ready, 1)
                for e in range(2):
                    for a in range(2):
                        v = keep["sel"][:, 2 * e + a, a * S:(a + 1) * S]
                        nc.gpsimd.affine_select(out=v, in_=v, compare_op=ALU.not_equal, fill=1.0, base=-e * S,
                                                pattern=[[-1, S]], channel_multiplier=1).then_inc(sel_ready, 1)
                nc.gpsimd.affine_select(out=head_of[:], in_=head_of[:], compare_op=ALU.is_ge, fill=0.0, base=0,
                                        pattern=[[-DH, 2 * GP]], channel_multiplier=1).then_inc(head_of_ready, 1)
                pool.wait_ge(head_of_ready, 1)
                nc.gpsimd.affine_select(out=head_of[:], in_=head_of[:], compare_op=ALU.is_ge, fill=0.0, base=DH - 1,
                                        pattern=[[DH, 2 * GP]], channel_multiplier=-1).then_inc(head_of_ready, 1)
                pool.wait_ge(sel_ready, 4)
                for h in range(2):
                    g = slice(h * HT, (h + 1) * HT)
                    pool.wait_ge(var_ready, h + 1)
                    nc.gpsimd.tensor_tensor(rstd[:, g], var_eps[:, g], minus_half[:, g], ALU.pow).then_inc(rstd_ready, 1)

            @block.tensor
            def _(pe):
                pe.wait_ge(ident_ready, 1)
                pe.wait_ge(x_in, 16)
                for m in range(KT):
                    for h in range(2):
                        for j in range(HT):
                            last = nc.tensor.transpose(ps[:, 2 * m + h, j * TT:(j + 1) * TT],
                                                       x_sb[:, h * HT + j, m * P:(m + 1) * P], keep["ident"][0:TT, 0:TT])
                        last.then_inc(xT_in_psum, 1)

                def weight_transpose(k):
                    pe.wait_ge(w_in[k], 16)
                    if k >= 2:
                        pe.wait_ge(wT_act, k - 1)
                    if k >= 6:
                        pe.wait_ge(wT_lo, k - 5)
                    for m in range(KT):
                        for e in range(KT):
                            last = nc.tensor.transpose(ps[:, 6 + k % 2, m * D + e * P:m * D + (e + 1) * P],
                                                       w_raw[:, k, e, m * P:(m + 1) * P], keep["ident"][:])
                    last.then_inc(wT_in_psum, 1)

                for k in (WK, WV, WQ):
                    weight_transpose(k)
                pe.wait_ge(xT_dve, 2)
                pe.wait_ge(xT_act, 2)
                pe.wait_ge(wT_act, 3)
                for u in range(4):
                    h, e = divmod(u, KT)
                    bank = 3 * (u % 2)
                    if u >= 2:
                        pe.wait_ge(relus, 4 * (u - 1))
                        pe.wait_ge(v_used, u - 1)
                    for n, k in enumerate((WK, WQ, WV)):
                        for m in range(KT):
                            last = nc.tensor.matmul(ps[:, bank + n, 0:HALF], wT[:, k, m, e * P:(e + 1) * P],
                                                    xT[:, m, h * HALF:(h + 1) * HALF], start=m == 0, stop=m == KT - 1)
                        last.then_inc(qkv_in_psum, 1)
                    if u == 0:
                        weight_transpose(WO)
                        weight_transpose(XK)
                    if u == 1:
                        weight_transpose(XV)
                pe.wait_ge(identb_ready, 1)
                pe.wait_ge(wq_int_ready, 1)
                pe.wait_ge(wT_lo, 1)
                for m in range(KT):
                    for e in range(KT):
                        last = nc.tensor.transpose(psb[:, 6, m * D + e * P:m * D + (e + 1) * P],
                                                   wq_int[:, e, m * P:(m + 1) * P], keep["ident_b"][:])
                last.then_inc(wqT_in_psum, 1)
                pe.wait_ge(diag_ready, KT)
                pe.wait_ge(dve_const, 2)
                pe.wait_ge(wT_lo, 2)
                for e in range(KT):
                    last = nc.tensor.matmul(ps[0:TT, 7, e * P:(e + 1) * P], ones[:], diag[:, e], start=True, stop=True)
                last.then_inc(row_in_psum, 1)
                for h in range(2):
                    pe.wait_ge(context_ready, KT * (h + 1))
                    if h == 0:
                        pe.wait_ge(relus, 16)
                        pe.wait_ge(v_used, 4)
                    for i in range(h * HT, (h + 1) * HT):
                        for m in range(KT):
                            last = nc.tensor.matmul(ps[0:TT, i // 2, (i % 2) * D:(i % 2 + 1) * D],
                                                    context[:, m, i * TT:(i + 1) * TT], wT[:, WO, m], start=m == 0, stop=m == KT - 1)
                        if i % 2:
                            last.then_inc(attn_in_psum, 1)
                for h in range(2):
                    for j in range(HT):
                        i = h * HT + j
                        pe.wait_ge(x_int_ready, i + 1)
                        for m in range(KT):
                            last = nc.tensor.transpose(psb[:, 4 + h, m * HALF + j * TT:m * HALF + (j + 1) * TT],
                                                       x_int[:, i, m * P:(m + 1) * P], keep["ident_b"][0:TT, 0:TT])
                    last.then_inc(x_intT_in_psum, 1)
                    pe.wait_ge(wqT_ready, 1)
                    pe.wait_ge(x_intT_ready, h + 1)
                    for i in range(h * HT, (h + 1) * HT):
                        if i % 2 == 0:
                            pe.wait_ge(resid_ready, i + 2)
                        for m in range(KT):
                            last = nc.tensor.matmul(ps[0:TT, i // 2, (i % 2) * D:(i % 2 + 1) * D],
                                                    x_intT[:, m, i * TT:(i + 1) * TT], wq_intT[:, m], start=m == 0, stop=m == KT - 1)
                        if i % 2:
                            last.then_inc(q_in_psum, 1)
                pe.wait_ge(row_ready, 1)
                pe.wait_ge(x_intT_ready, 2)
                for h in range(2):
                    pe.wait_ge(query_ready, (h + 1) * HT)
                    for m in range(KT):
                        for j in range(HT):
                            last = nc.tensor.transpose(ps[:, 4 + 2 * m + h, j * TT:(j + 1) * TT],
                                                       query[:, h * HT + j, m * P:(m + 1) * P], keep["ident"][0:TT, 0:TT])
                        last.then_inc(qT_in_psum, 1)

            @block.scalar
            def _(act):
                for n, name in enumerate(["L0_attn_bk", "L0_attn_bq", "L0_attn_bv"]):
                    act.dma_start(qkv_bias[:, n], column(io[name]), allow_slow_non_contiguous=True).then_inc(bias_in, 16)
                act.dma_start(keep["xbk"][:], column(io["L0_xattn_bk"]), allow_slow_non_contiguous=True).then_inc(bias_in, 16)
                act.dma_start(bo_row[:], row(io["L0_attn_bo"], TT)).then_inc(row_in, 16)
                act.dma_start(xbq_row[:], row(io["L0_xattn_bq"], TT)).then_inc(row_in, 16)
                act.wait_ge(bias_in, 64)
                act.wait_ge(row_in, 32)
                act.wait_ge(ident_ready, 1)
                nc.scalar.activation(keep["ident_b"][:], keep["ident"][:], ACT.Copy).then_inc(identb_ready, 1)
                nc.scalar.activation(neg_bias[:], qkv_bias[:], ACT.Copy, scale=-1.0).then_inc(identb_ready, 1)
                for n in (1, 3):
                    act.wait_ge(xT_in_psum, n + 1)
                    nc.scalar.activation(xT[:, n // 2, HALF:T], ps[:, n, 0:HALF], ACT.Copy).then_inc(xT_act, 1)

                def weight_out(k):
                    act.wait_ge(wT_in_psum, k + 1)
                    src = ps[:, 6 + k % 2]
                    if k < XK:
                        dst = wT[:, k]
                    else:
                        dst = keep["wkT_hi" if k == XK else "wvT_hi"][:]
                    nc.scalar.activation(dst, split(src, KT), ACT.Copy).then_inc(wT_act, 1)

                for k in (WK, WV, WQ):
                    weight_out(k)
                act.wait_ge(identb_ready, 2)
                for u in range(4):
                    h, e = divmod(u, KT)
                    for n in range(2):
                        act.wait_ge(qkv_in_psum, 3 * u + n + 1)
                        src = ps[:, 3 * (u % 2) + n, 0:HALF]
                        nc.scalar.activation(relu_neg[:, u, n], src, ACT.Relu, scale=-1.0,
                                             bias=neg_bias[:, n, e:e + 1]).then_inc(relus, 1)
                        nc.scalar.activation(relu_pos[:, u, n], src, ACT.Relu,
                                             bias=qkv_bias[:, n, e:e + 1]).then_inc(relus, 1)
                    act.wait_ge(relus, 4 * u + 4)
                    nc.scalar.activation(relu_neg[:, u], relu_neg[:, u], ACT.Exp, scale=-1.0).then_inc(exps, 1)
                    if u == 0:
                        weight_out(WO)
                        weight_out(XK)
                    if u == 1:
                        weight_out(XV)
                act.wait_ge(wqT_in_psum, 1)
                nc.scalar.activation(wq_intT[:], split(psb[:, 6, 0:KT * D], KT), ACT.Copy).then_inc(wqT_ready, 1)
                act.wait_ge(row_in_psum, 1)
                nc.scalar.activation(wq_scale_row[:], ps[0:TT, 7, 0:D], ACT.Copy, scale=SCALE).then_inc(row_ready, 1)
                for n in range(4):
                    m, h = n % 2, n // 2
                    act.wait_ge(qbd_ready, 2 * n + 2)
                    bs = slice(h * B // 2, (h + 1) * B // 2)
                    nc.scalar.activation(qbd_hi[:, m, bs], qbd[:, m, bs], ACT.Copy).then_inc(qbd_hi_ready, 1)

            @block.vector
            def _(dve):
                nc.vector.memset(keep_going[:], 1.0).then_inc(dve_const, 1)
                nc.vector.memset(ones[:], 1.0).then_inc(dve_const, 1)
                dve.wait_ge(dve_const, 1)
                nc.vector.memset(keep_going[:].rearrange("p (b s) -> p b s", s=S)[:, :, 0:1], 0.0).then_inc(dve_const, 1)
                dve.wait_ge(head_of_ready, 2)
                nc.vector.tensor_reduce(head_mask[:], head_of[:].rearrange("p (k e) -> p e k", e=2), AX.X, ALU.add).then_inc(mask_ready, 1)
                for n in (0, 2):
                    dve.wait_ge(xT_in_psum, n + 1)
                    nc.vector.tensor_copy(xT[:, n // 2, 0:HALF], ps[:, n, 0:HALF]).then_inc(xT_dve, 1)
                dve.wait_ge(w_in[XQ], 16)
                nc.vector.tensor_reduce(wq_scale[:], w_raw[:, XQ], AX.X, ALU.max, apply_absolute_value=True).then_inc(wq_steps, 1)
                dve.wait_ge(wq_steps, 1)
                nc.vector.tensor_scalar(wq_scale[:], wq_scale[:], 1.0 / QMAX, QEPS, ALU.mult, ALU.max).then_inc(wq_steps, 1)
                dve.wait_ge(wq_steps, 2)
                nc.vector.reciprocal(wq_inv[:], wq_scale[:]).then_inc(wq_steps, 1)
                dve.wait_ge(ident_ready, 1)
                for e in range(KT):
                    nc.vector.tensor_scalar(diag[:, e], keep["ident"][:], wq_scale[:, e:e + 1], None, ALU.mult).then_inc(diag_ready, 1)
                dve.wait_ge(wq_steps, 3)
                for e in range(KT):
                    nc.vector.tensor_scalar(wq_tmp[:, e], w_raw[:, XQ, e], wq_inv[:, e:e + 1], ROUND, ALU.mult, ALU.add).then_inc(wq_steps, 1)
                dve.wait_ge(wq_steps, 5)
                nc.vector.tensor_scalar(wq_tmp[:], wq_tmp[:], ROUND, QMAX, ALU.subtract, ALU.min).then_inc(wq_steps, 1)
                dve.wait_ge(wq_steps, 6)
                nc.vector.tensor_scalar(wq_int[:], wq_tmp[:], -QMAX, None, ALU.max).then_inc(wq_int_ready, 1)
                dve.wait_ge(bias_in, 64)
                dve.wait_ge(row_in, 32)
                dve.wait_ge(dve_const, 3)
                dve.wait_ge(xT_in_psum, 4)
                nc.vector.tensor_tensor(x_sb[:], x_sb[:], bo_row[:].unsqueeze(1).broadcast_to([TT, NT, D]), ALU.add).then_inc(xbo_ready, 1)
                nc.vector.tensor_scalar(xbq_row[:], xbq_row[:], SCALE, None, ALU.mult).then_inc(xbo_ready, 1)

                def weight_lo(k):
                    dve.wait_ge(wT_act, k + 1)
                    hi = keep["wkT_hi" if k == XK else "wvT_hi"]
                    lo = keep["wkT_lo" if k == XK else "wvT_lo"]
                    nc.vector.tensor_tensor(lo[:], split(ps[:, 6 + k % 2], KT), hi[:].bitcast(F32), ALU.subtract).then_inc(wT_lo, 1)

                for u in range(4):
                    h, e = divmod(u, KT)
                    dve.wait_ge(exps, u + 1)
                    nc.vector.tensor_tensor(phi[:, u], relu_pos[:, u], relu_neg[:, u], ALU.add).then_inc(phis, 1)
                    dve.wait_ge(phis, u + 1)
                    dve.wait_ge(qkv_in_psum, 3 * u + 3)
                    nc.vector.scalar_tensor_tensor(out=kv[:, u], in0=ps[:, 3 * (u % 2) + 2, 0:HALF], scalar=qkv_bias[:, 2, e:e + 1],
                                                   in1=phi[:, u, 0], op0=ALU.add, op1=ALU.mult).then_inc(v_used, 1)
                    dve.wait_ge(v_used, u + 1)
                    nc.vector.tensor_tensor_scan(kv_sum[:, u], keep_going[:], kv[:, u], 0.0, ALU.mult, ALU.add).then_inc(scanned, 1)
                    dve.wait_ge(scanned, u + 1)
                    nc.vector.scalar_tensor_tensor(out=context[:, e, h * HALF:(h + 1) * HALF], in0=kv_sum[:, u], scalar=SCALE,
                                                   in1=phi[:, u, 1], op0=ALU.mult, op1=ALU.mult).then_inc(context_ready, 1)
                    if u == 1:
                        weight_lo(XK)
                    if u == 2:
                        weight_lo(XV)
                dve.wait_ge(xbo_ready, 2)
                for h in range(2):
                    for i in range(h * HT, (h + 1) * HT):
                        if i % 2 == 0:
                            dve.wait_ge(attn_in_psum, i // 2 + 1)
                        nc.vector.tensor_tensor(resid[:, i], ps[0:TT, i // 2, (i % 2) * D:(i % 2 + 1) * D], x_sb[:, i], ALU.add).then_inc(resid_ready, 1)
                    for i in range(h * HT, (h + 1) * HT):
                        dve.wait_ge(resid_ready, i + 1)
                        nc.vector.bn_stats(stats[:, i], resid[:, i]).then_inc(stats_ready, 1)
                    for i in range(h * HT, (h + 1) * HT):
                        dve.wait_ge(stats_ready, i + 1)
                        nc.vector.bn_aggr(mv[:, i], stats[:, i]).then_inc(mv_ready, 1)
                    g = slice(h * HT, (h + 1) * HT)
                    dve.wait_ge(mv_ready, (h + 1) * HT)
                    nc.vector.tensor_scalar(var_eps[:, g], mv[:, g, 1], LN_EPS, None, ALU.add).then_inc(var_ready, 1)
                for h in range(2):
                    dve.wait_ge(rstd_ready, h + 1)
                    for i in range(h * HT, (h + 1) * HT):
                        nc.vector.tensor_scalar(keep["x1"][:, i], resid[:, i], mv[:, i, 0:1], rstd[:, i:i + 1],
                                                ALU.subtract, ALU.mult).then_inc(x1_ready, 1)
                    g = slice(h * HT, (h + 1) * HT)
                    dve.wait_ge(x1_ready, (h + 1) * HT)
                    nc.vector.tensor_reduce(x_scale[:, g], keep["x1"][:, g], AX.X, ALU.max, apply_absolute_value=True).then_inc(x_steps, 1)
                    dve.wait_ge(x_steps, 4 * h + 1)
                    nc.vector.tensor_scalar(x_scale[:, g], x_scale[:, g], 1.0 / QMAX, QEPS, ALU.mult, ALU.max).then_inc(x_steps, 1)
                    dve.wait_ge(x_steps, 4 * h + 2)
                    nc.vector.reciprocal(x_inv[:, g], x_scale[:, g]).then_inc(x_steps, 1)
                    dve.wait_ge(x_steps, 4 * h + 3)
                    for i in range(h * HT, (h + 1) * HT):
                        ins = nc.vector.tensor_scalar(x_tmp[:, i], keep["x1"][:, i], x_inv[:, i:i + 1], ROUND, ALU.mult, ALU.add)
                    ins.then_inc(x_steps, 1)
                    dve.wait_ge(x_steps, 4 * h + 4)
                    for i in range(h * HT, (h + 1) * HT):
                        nc.vector.tensor_scalar(x_int[:, i], x_tmp[:, i], ROUND, QMAX, ALU.subtract, ALU.min).then_inc(x_int_ready, 1)
                    dve.wait_ge(x_intT_in_psum, h + 1)
                    nc.vector.tensor_scalar(x_intT[:, :, h * HALF:(h + 1) * HALF], split(psb[:, 4 + h, 0:KT * HALF], KT),
                                            -QMAX, None, ALU.max).then_inc(x_intT_ready, 1)
                dve.wait_ge(row_ready, 1)
                for i in range(NT):
                    if i % 2 == 0:
                        dve.wait_ge(q_in_psum, i // 2 + 1)
                    nc.vector.scalar_tensor_tensor(out=q_scaled[:, i], in0=ps[0:TT, i // 2, (i % 2) * D:(i % 2 + 1) * D],
                                                   scalar=x_scale[:, i:i + 1], in1=wq_scale_row[:], op0=ALU.mult, op1=ALU.mult).then_inc(q_scaled_ready, 1)
                for h in range(2):
                    g = slice(h * HT, (h + 1) * HT)
                    dve.wait_ge(q_scaled_ready, (h + 1) * HT)
                    nc.vector.tensor_tensor(query[:, g], q_scaled[:, g], xbq_row[:].unsqueeze(1).broadcast_to([TT, HT, D]), ALU.add).then_inc(query_ready, HT)
                dve.wait_ge(mask_ready, 1)
                for n in range(4):
                    m, h = n % 2, n // 2
                    dve.wait_ge(qT_in_psum, n + 1)
                    src = ps[:, 4 + 2 * m + h, 0:HALF].rearrange("p (b s) -> p b s", s=S)
                    bs = slice(h * B // 2, (h + 1) * B // 2)
                    for e in range(2):
                        nc.vector.tensor_scalar(qbd[:, m, bs, e], src, head_mask[:, e:e + 1], None, ALU.mult).then_inc(qbd_ready, 1)
                for n in range(4):
                    m, h = n % 2, n // 2
                    bs = slice(h * B // 2, (h + 1) * B // 2)
                    dve.wait_ge(qbd_hi_ready, n + 1)
                    nc.vector.tensor_tensor(qbd_lo[:, m, bs], qbd[:, m, bs], qbd_hi[:, m, bs].bitcast(F32), ALU.subtract).then_inc(qbd_lo_ready, 1)


UNITS = [
    ([("X", 0, 0)], [("X", 0, 1)]),
    ([("V", 0, 0), ("X", 1, 0)], [("X", 1, 1)]),
    ([("K", 0, 0), ("X", 2, 0)], [("X", 2, 1)]),
    ([("K", 0, 1)], [("K", 0, 2)]),
    ([("V", 1, 0)], [("V", 2, 0)]),
    ([("V", 3, 0)], [("V", 4, 0)]),
    ([("K", 1, 0)], [("K", 1, 1)]),
    ([("K", 1, 2)], [("V", 5, 0)]),
]
RESULT_AFTER = {3: 0, 4: 1, 5: 2, 6: 3}
UNITS_R = [(before, after + ([("R", RESULT_AFTER[t], 0)] if t in RESULT_AFTER else [])) for t, (before, after) in enumerate(UNITS)]


def ordered(units):
    return {u: n for n, u in enumerate(u for before, after in units for u in before + after)}


AT, AT_R = ordered(UNITS), ordered(UNITS_R)
ORDER = list(AT)
NU, NR = len(AT), len(RESULT_AFTER)
NU2 = 2 * NU + NR
AT_LAST = {("R", k, 0): k for k in range(NR)}
HI = [u for u in ORDER if u[0] != "V"]
HI_AT = {u: n for n, u in enumerate(HI)}
NHI = len(HI)
R_STEPS = 11


def units_before(half, a):
    if isinstance(half, int) and half == 0:
        return NU * (1 + a)
    return half * NU2 + NU - NR + a * (NU + NR)


PREPARE_AT = {3: 1, 7: 2, 10: 3, 12: 4, 14: 5, 16: 6}
TB = 3
E, A_ATOMS, NS = 8, 64, 2048
EST = 3
STACK = 3


def cross_attention_phase(nc, io, keep):
    ctx = ExitStack()
    with ctx:
        sb = lambda n, s, d=F32: ctx.enter_context(nc.sbuf_tensor(n, s, d))
        sem = lambda n: ctx.enter_context(nc.semaphore(n))
        context = sb("ctx_rows", [LT, NL, D])
        cT_hi = sb("cT_hi", [P, KT, L], F32R)
        cT_lo = sb("cT_lo", [P, KT, L], F32R)
        k_hi = sb("k_hi", [P, L], F32R)
        k_lo = sb("k_lo", [P, L], F32R)
        k_stack = sb("k_stack", [STACK * PD, NP, L], F32R)
        q_stack = sb("q_stack", [STACK * PD, 2, NP, PN], F32R)
        v_sb = sb("v_sb", [P, 2, NL, D])
        mask_sb = sb("mask_sb", [PN, 2, L])
        scores = sb("scores", [PN, 2, L])
        shift = sb("shift", [PN, 2])
        wait_cell = sb("wait_cell", [PN, 1])
        probsT = sb("probsT", [LT, 2, NL, PN])
        rsum = sb("rsum", [PN, 2, NP])
        r_norm = sb("r_norm", [PN, 2 * NP, PD])
        r_sb = sb("r_sb", [TT, D])
        r_scale = sb("r_scale", [TT, 1])
        r_inv = sb("r_inv", [TT, 1])
        r_tmp = sb("r_tmp", [TT, D])
        r_int = sb("r_int", [TT, D], BF16)
        r_intT = sb("r_intT", [P, KT, TT], BF16)
        resid = sb("resid_x", [TT, D])
        stats = sb("stats_x", [TT, 6])
        mv = sb("mv_x", [TT, 2])
        var_eps = sb("var_eps_x", [TT, NT])
        minus_half = sb("minus_half_x", [TT, NT])
        rstd = sb("rstd_x", [TT, NT])
        r_cell = sb("r_cell", [TT, 1])
        x1, x2 = keep["x1"], keep["x1"]
        room = v_sb[:, 1].rearrange("p l d -> p (l d)")
        wo_raw, w_raw, wo_tmp = (split(room[:, n * KT * D:(n + 1) * KT * D], KT) for n in range(3))
        diag = split(room[:, 3 * KT * D:3 * KT * D + KT * P], KT)
        wo_int = split(room[:, 4 * KT * D:4 * KT * D + KT * D // 2].bitcast(BF16), KT)
        ones = room[:, 5 * KT * D:5 * KT * D + TT]
        bo_row = room[0:TT, 5 * KT * D + TT:5 * KT * D + TT + D]
        importance = sb("importance", [P, E * NS // P])
        gate = probsT[0:E].rearrange("p h j n -> p (h j n)")[:, 0:NS]
        atoms = scores[0:A_ATOMS].rearrange("p h l -> p (h l)")[:, 0:NS]
        w8_lo = k_stack[0:E, NP - 2:NP].rearrange("p k l -> p (k l)")[:, 0:NS]
        wo_scale = sb("wo_scale", [P, KT])
        wo_inv = sb("wo_inv", [P, KT])
        gate_raw = sb("gate_raw", [E, D])
        atom_w = sb("atom_w", [E, A_ATOMS])
        atom_shift = sb("atom_shift", [E, 1])
        atom_sum = sb("atom_sum", [E, 1])
        atom_rsum = sb("atom_rsum", [E, 1])
        atom_p = sb("atom_p", [E, A_ATOMS])
        atom_pn = sb("atom_pn", [E, A_ATOMS])
        atom_pT = sb("atom_pT", [A_ATOMS, E])
        ps_scores = ctx.enter_context(nc.psum_tensor("ps_scores", [P, NC, 512], F32))
        ps_T = ctx.enter_context(nc.psum_tensor("ps_T", [P, 2, 512], F32))
        ps_proj = ctx.enter_context(nc.psum_tensor("ps_proj", [P, 2, 512], F32))
        psb_proj, psb_scores = ps_proj[:, :, :].bitcast(BF16), ps_scores[:, :, :].bitcast(BF16)
        ps_out = ctx.enter_context(nc.psum_tensor("ps_out", [P, 512], F32))

        ctx_in = [sem(f"ctx_in{c}") for c in range(NC)]
        mask_in = [sem(f"mask_in{a}") for a in range(2)]
        q_in = [sem(f"q_in{a}") for a in range(2)]
        k_in = [sem(f"k_in{p}") for p in range(NP)]
        unit_in_psum = sem("unit_in_psum")
        hi_ready = sem("hi_ready")
        unit_out = sem("unit_out")
        scores_in_psum = sem("scores_in_psum")
        scores_ready = sem("scores_ready")
        wait_taken = sem("wait_taken")
        probs_ready = sem("probs_ready")
        probsT_in_psum = sem("probsT_in_psum")
        probsT_dve = sem("probsT_dve")
        probsT_act = sem("probsT_act")
        values_done = sem("values_done")
        out_copied = sem("out_copied")
        r_steps = sem("r_steps")
        r_int_ready = sem("r_int_ready")
        var_ready = sem("var_x_ready")
        rstd_ready = sem("rstd_x_ready")
        half_set = sem("half_set")
        load = {n: sem(f"in_{n}") for n in ("wo", "w", "gate", "atom_w", "atoms", "imp", "bo", "bv")}
        ones_set = sem("ones_set")
        wo_steps = sem("wo_steps")
        wo_int_ready = sem("wo_int_ready")
        diag_ready = sem("diag_o_ready")
        W_T, GATE_T, WO_T, SCALE_ROW, ATOM_T, DELTAS = range(1, 7)
        prepared_in_psum = sem("prepared_in_psum")
        prepared_out = sem("prepared_out")
        wT_lo_ready = sem("wfT_lo_ready")
        atom_steps = sem("atom_steps")
        atom_exp = sem("atom_exp")
        gate_exp = sem("gate_exp")
        gate_steps = sem("gate_steps")
        gate_stored = sem("gate_stored")
        gate_in = sem("gate_in")
        w8_hi_ready = sem("w8_hi_ready")
        w8_lo_ready = sem("w8_lo_ready")
        w_stacked = sem("w_stacked")
        x1_bo_ready = sem("x1_bo_ready")

        def q_rows(src, b):
            return src[:, :, b].rearrange("m (k r) n -> r (m k) n", r=PD)

        with nc.Block() as block:

            @block.sync
            def _(sp):
                def load_chunk(b, c):
                    sp.dma_start(context[:, c * TC:(c + 1) * TC],
                                 io["ctx"][b, c * LC:(c + 1) * LC].rearrange("(j p) d -> p j d", p=LT)).then_inc(ctx_in[c], 16)

                def load_mask(b, a):
                    for e in range(2):
                        sp.dma_start(mask_sb[e * S:(e + 1) * S, a], io["mask"][b]).then_inc(mask_in[a], 16)

                def load_q(b, a):
                    for g, src in enumerate(("q_hi", "q_lo", "q_hi")):
                        sp.dma_start(q_stack[g * PD:(g + 1) * PD, a].bitcast(F32), q_rows(io[src], b)).then_inc(q_in[a], 16)

                def wide(ap):
                    return ap.rearrange("e (a c) -> (e a) c", c=E * NS // P)

                def load_weights():
                    rows = lambda w: w.rearrange("(k p) d -> p k d", p=P)
                    row = lambda v: v.unsqueeze(0).broadcast_to([TT, D])
                    sp.dma_start(wo_raw, rows(io["L0_xattn_wo"])).then_inc(load["wo"], 16)
                    sp.dma_start(w_raw, rows(io["L0_ffn_W"])).then_inc(load["w"], 16)
                    sp.dma_start(gate_raw[:], io["L0_ffn_gate_w"]).then_inc(load["gate"], 16)
                    sp.dma_start(atom_w[:], io["L0_ffn_expert_atom_weights"]).then_inc(load["atom_w"], 16)
                    sp.dma_start(importance[:], wide(io["L0_ffn_importance"])).then_inc(load["imp"], 16)
                    sp.dma_start(atoms, io["L0_ffn_atoms"]).then_inc(load["atoms"], 16)
                    sp.dma_start(bo_row, row(io["L0_xattn_bo"])).then_inc(load["bo"], 16)
                    sp.dma_start(keep["bv_row"][:], row(io["L0_xattn_bv"])).then_inc(load["bv"], 16)

                def k_out(first, at, m):
                    return first + at[("K", m, NC - 1)] + 1 + 2

                def stack_k(m):
                    for k in range(GP):
                        rows = slice(k * PD, (k + 1) * PD)
                        for g, src in enumerate((k_hi, k_hi, k_lo)):
                            sp.dma_start(k_stack[g * PD:(g + 1) * PD, m * GP + k].bitcast(F32), src[rows].bitcast(F32)).then_inc(k_in[m * GP + k], 16)

                def batch(b, half, a, at, project, load):
                    if project:
                        first = units_before(half, a)
                        for c in range(NC):
                            if load:
                                sp.wait_ge(unit_in_psum, first + at[("X", c, 1)] + 1)
                                load_chunk(b + 2, c)
                        sp.wait_ge(unit_out, k_out(first, at, 0))
                        stack_k(0)
                        if load:
                            sp.wait_ge(scores_ready, (b + 1) * NP)
                            load_mask(b + 2, a)
                            load_q(b + 2, a)
                        sp.wait_ge(unit_out, k_out(first, at, 1))
                        stack_k(1)

                for c in range(NC):
                    load_chunk(0, c)
                load_weights()
                for a in range(2):
                    load_q(a, a)
                    load_mask(a, a)
                for c in range(NC):
                    sp.wait_ge(unit_in_psum, AT[("X", c, 1)] + 1)
                    load_chunk(1, c)
                sp.wait_ge(gate_steps, 2)
                sp.dma_start(wide(io["gate"]), importance[:]).then_inc(gate_stored, 16)
                sp.wait_ge(gate_stored, 16)
                sp.dma_start(gate, io["gate"]).then_inc(gate_in, 16)
                sp.wait_ge(unit_out, k_out(0, AT, 0))
                stack_k(0)
                sp.wait_ge(w8_lo_ready, 1)
                w_stack = keep["w_stack"]
                sp.dma_start(w_stack[E:2 * E].bitcast(F32), w8_lo.bitcast(F32)).then_inc(w_stacked, 16)
                sp.dma_start(w_stack[2 * E:3 * E].bitcast(F32), w_stack[0:E].bitcast(F32)).then_inc(w_stacked, 16)
                sp.wait_ge(w_stacked, 32)
                sp.wait_ge(unit_out, k_out(0, AT, 1))
                stack_k(1)
                for a in range(2):
                    batch(a, 0, a, AT, True, True)
                with sp.Fori(1, B // 2 - 1) as i:
                    for a in range(2):
                        batch(2 * i + a, i, a, AT if a else AT_R, True, True)
                batch(B - 2, B // 2 - 1, 0, AT_R, True, False)

            @block.gpsimd
            def _(pool):
                nc.gpsimd.memset(minus_half[:], -0.5).then_inc(half_set, 1)
                pool.wait_ge(half_set, 1)
                for i in range(NT):
                    pool.wait_ge(var_ready, i + 1)
                    nc.gpsimd.tensor_tensor(rstd[:, i:i + 1], var_eps[:, i:i + 1], minus_half[:, i:i + 1], ALU.pow).then_inc(rstd_ready, 1)

            @block.tensor
            def _(pe):
                def terms(w_hi, w_lo, x_hi, x_lo):
                    return ((w_hi, x_hi), (w_hi, x_lo), (w_lo, x_hi))

                def result(first, at, k):
                    bank = at[("R", k, 0)] % 2
                    if k == 0:
                        for b in range(2):
                            for g in range(2):
                                last = nc.tensor.transpose(ps_proj[0:PN, bank, b * D + g * P:b * D + (g + 1) * P],
                                                           keep["outT"][:, b, g * PN:(g + 1) * PN], keep["ident"][:])
                    elif k == 1:
                        pe.wait_ge(unit_out, first + at[("R", 0, 0)] + 1 + 2)
                        for e in range(2):
                            dst = ps_proj[0:TT, bank, 0:D].rearrange("p (k e d) -> p k e d", k=NP, e=2)[:, :, e]
                            for b in range(2):
                                last = nc.tensor.matmul(dst, keep["sel"][:, 2 * e + b], r_norm[:, b * NP:(b + 1) * NP, e * DH:(e + 1) * DH],
                                                        start=b == 0, stop=b == 1)
                    elif k == 2:
                        for m in range(KT):
                            last = nc.tensor.transpose(psb_proj[:, bank, m * TT:(m + 1) * TT], r_int[:, m * P:(m + 1) * P],
                                                       keep["ident_b"][0:TT, 0:TT])
                    else:
                        pe.wait_ge(unit_out, first + at[("R", 2, 0)] + 1 + 2)
                        for m in range(KT):
                            last = nc.tensor.matmul(ps_proj[0:TT, bank, 0:D], r_intT[:, m], keep["wo_intT"][:, m], start=m == 0, stop=m == KT - 1)
                    last.then_inc(unit_in_psum, 1)

                def unit(first, at, n, u, a):
                    kind, p, q = u
                    bank = at[u] % 2
                    pe.wait_ge(unit_out, first + at[u] + 1)
                    if kind == "R":
                        if p == 2:
                            pe.wait_ge(r_int_ready, n)
                        return result(first, at, p)
                    if kind == "X":
                        if q == 0:
                            pe.wait_ge(ctx_in[p], 16 * (n + 1))
                        for j in range(TC):
                            last = nc.tensor.transpose(ps_proj[:, bank, j * LT:(j + 1) * LT],
                                                       context[:, p * TC + j, q * P:(q + 1) * P], keep["ident"][0:LT, 0:LT])
                    elif kind == "K":
                        pe.wait_ge(unit_out, first + at[("X", q, 1)] + 1 + 2)
                        c, e = slice(q * LC, (q + 1) * LC), slice(p * P, (p + 1) * P)
                        mm = [t for m in range(KT) for t in terms(keep["wkT_hi"][:, m, e], keep["wkT_lo"][:, m, e],
                                                                  cT_hi[:, m, c], cT_lo[:, m, c])]
                        for i, (w, x) in enumerate(mm):
                            last = nc.tensor.matmul(ps_proj[:, bank, 0:LC], w, x, start=i == 0, stop=i == len(mm) - 1)
                    else:
                        pe.wait_ge(unit_out, first + at[("X", (2 * p + 1) // TC, 1)] + 1 + 2)
                        for j in range(2):
                            c = slice((2 * p + j) * LT, (2 * p + j + 1) * LT)
                            mm = [t for m in range(KT) for t in terms(cT_hi[:, m, c], cT_lo[:, m, c],
                                                                      keep["wvT_hi"][:, m], keep["wvT_lo"][:, m])]
                            for i, (w, x) in enumerate(mm):
                                last = nc.tensor.matmul(ps_proj[0:LT, bank, j * D:(j + 1) * D], w, x, start=i == 0, stop=i == len(mm) - 1)
                    last.then_inc(unit_in_psum, 1)


                def scores_of(b, half, a, t, before):
                    if t == 0:
                        pe.wait_ge(q_in[a], 16 * STACK * (half + 1))
                    pe.wait_ge(k_in[t], 16 * STACK * (b + 1))
                    if before:
                        pe.wait_ge(scores_ready, b * NP + t)
                    for c in range(NC):
                        last = nc.tensor.matmul(ps_scores[0:PN, c, 0:LC], q_stack[:, a, t], k_stack[:, t, c * LC:(c + 1) * LC],
                                                start=True, stop=True)
                        if c == 0 and not before:
                            last.then_inc(values_done, 2)
                    last.then_inc(scores_in_psum, 1)

                def transposes(b, t, k):
                    if k == 0:
                        pe.wait_ge(probs_ready, b * NP + t + 1)
                    if k < 2:
                        pe.wait_ge(probsT_act, 2 * (b * NP + t) + k + 1)
                    else:
                        pe.wait_ge(probsT_dve, b * NP + t + 1)
                    for j in range(TC):
                        last = nc.tensor.transpose(ps_T[0:LT, (TB * t + k) % 2, j * PN:(j + 1) * PN],
                                                   scores[:, t % 2, (k * TC + j) * LT:(k * TC + j + 1) * LT], keep["ident"][0:PN, 0:PN])
                    last.then_inc(probsT_in_psum, 1)

                def values(b, half, a, t, tiles):
                    g, k = divmod(t, GP)
                    for j in tiles:
                        if j == 0:
                            pe.wait_ge(probsT_dve, b * NP + t + 1)
                            if t == 0:
                                pe.wait_ge(out_copied, b + 1)
                                pe.wait_ge(unit_out, units_before(half, a) + 2)
                        if j == TC:
                            pe.wait_ge(probsT_act, 2 * (b * NP + t) + 1 + 2)
                        if j == 2 * TC:
                            pe.wait_ge(probsT_act, 2 * (b * NP + t) + 2 + 2)
                        last = nc.tensor.matmul(ps_out[k * PD:(k + 1) * PD, g * PN:(g + 1) * PN], v_sb[0:LT, a, j, t * PD:(t + 1) * PD],
                                                probsT[:, t % 2, j], start=j == 0, stop=j == NL - 1)
                    if j == NL - 1:
                        last.then_inc(values_done, 1)

                def batch(b, half, a, slots, at):
                    project = bool(at)
                    for t in range(NP):
                        transposes(b, t, 0)
                        transposes(b, t, 1)
                        if t + 2 < NP:
                            scores_of(b, half, a, t + 2, True)
                        elif project:
                            scores_of(b + 1, half + a, 1 - a, t + 2 - NP, True)
                        transposes(b, t, 2)
                        before, after = slots[t]
                        for u in before:
                            unit(units_before(half, a), at, half if u[0] == "R" else b + 1, u, 1 - a)
                        values(b, half, a, t, range(0, 2 * TC))
                        for u in after:
                            unit(units_before(half, a), at, half if u[0] == "R" else b + 1, u, 1 - a)
                        values(b, half, a, t, range(2 * TC, NL))

                def prepare(n):
                    if n == 1:
                        pe.wait_ge(load["w"], 16)
                        for m in range(KT):
                            for e in range(KT):
                                last = nc.tensor.transpose(ps_scores[:, 0, m * D + e * P:m * D + (e + 1) * P], w_raw[:, e, m * P:(m + 1) * P], keep["ident"][:])
                        last.then_inc(prepared_in_psum, 1)
                        pe.wait_ge(load["gate"], 16)
                        for m in range(KT):
                            last = nc.tensor.transpose(ps_out[:, m * E:(m + 1) * E], gate_raw[:, m * P:(m + 1) * P], keep["ident"][0:E, 0:E])
                        last.then_inc(prepared_in_psum, 1)
                    if n == 2:
                        pe.wait_ge(wo_int_ready, 1)
                        for m in range(KT):
                            for e in range(KT):
                                last = nc.tensor.transpose(psb_scores[:, 1, m * D + e * P:m * D + (e + 1) * P], wo_int[:, e, m * P:(m + 1) * P], keep["ident_b"][:])
                        last.then_inc(prepared_in_psum, 1)
                        pe.wait_ge(ones_set, 1)
                        pe.wait_ge(diag_ready, KT)
                        for e in range(KT):
                            last = nc.tensor.matmul(ps_scores[0:TT, 2, e * P:(e + 1) * P], ones, diag[:, e], start=True, stop=True)
                        last.then_inc(prepared_in_psum, 1)
                    if n == 3:
                        pe.wait_ge(atom_steps, 3)
                        pe.wait_ge(prepared_out, GATE_T)
                        nc.tensor.transpose(ps_out[0:A_ATOMS, 0:E], atom_pn[:], keep["ident"][0:E, 0:E]).then_inc(prepared_in_psum, 1)
                    if n == 4:
                        pe.wait_ge(prepared_out, ATOM_T)
                        pe.wait_ge(wT_lo_ready, 1)
                        pe.wait_ge(load["atoms"], 16)
                        for c in range(NS // 512):
                            dst = ps_scores[0:E, c] if c < NC else ps_T[0:E, 0]
                            last = nc.tensor.matmul(dst, atom_pT[:], atoms[:, c * 512:(c + 1) * 512], start=True, stop=True)
                        last.then_inc(prepared_in_psum, 1)

                for n, u in enumerate(ORDER):
                    unit(0, AT, 0, u, 0)
                    prepare(PREPARE_AT.get(n, 0))
                pe.wait_ge(gate_steps, 4)
                scores_of(0, 0, 0, 0, False)
                scores_of(0, 0, 0, 1, True)
                for a in range(2):
                    batch(a, 0, a, UNITS, AT)
                with pe.Fori(1, B // 2 - 1) as i:
                    batch(2 * i, i, 0, UNITS_R, AT_R)
                    batch(2 * i + 1, i, 1, UNITS, AT)
                batch(B - 2, B // 2 - 1, 0, UNITS_R, AT_R)
                batch(B - 1, B // 2 - 1, 1, [([], [])] * NP, {})
                pe.wait_ge(out_copied, B + 1)
                for k in range(NR):
                    unit(units_before(B // 2 - 1, 1), AT_LAST, NT, ("R", k, 0), 0)

            @block.scalar
            def _(act):
                def unit_hi(first, at, n, u):
                    kind, p, q = u
                    if kind in "VR":
                        return
                    act.wait_ge(unit_in_psum, first + at[u] + 1)
                    src = ps_proj[:, at[u] % 2, 0:LC]
                    if kind == "X":
                        nc.scalar.activation(cT_hi[:, q, p * LC:(p + 1) * LC], src, ACT.Copy).then_inc(hi_ready, 1)
                    else:
                        if q == 0:
                            for k in range(GP):
                                done = n * 16 * STACK if p == 0 else (n + 1) * 16 * STACK
                                other = (1 - p) * GP + k
                                if p == 1 or not isinstance(n, int) or n > 0:
                                    act.wait_ge(k_in[other], done)
                        nc.scalar.activation(k_hi[:, q * LC:(q + 1) * LC], src, ACT.Identity,
                                             bias=keep["xbk"][:, p:p + 1]).then_inc(hi_ready, 1)

                def exponentials(b, t):
                    act.wait_ge(scores_ready, b * NP + t + 1)
                    nc.scalar.activation(scores[:, t % 2], scores[:, t % 2], ACT.Exp, scale=-1.0, bias=shift[:, t % 2:t % 2 + 1],
                                         accum_out=keep["sums"][:, b, t:t + 1]).then_inc(probs_ready, 1)

                def batch(b, half, a, slots, at):
                    project = bool(at)
                    for t in range(NP):
                        act.wait_ge(values_done, b * NP + t + 1)
                        for k in (1, 2):
                            act.wait_ge(probsT_in_psum, TB * (b * NP + t) + k + 1)
                            nc.scalar.activation(probsT[:, t % 2, k * TC:(k + 1) * TC],
                                                 ps_T[0:LT, (TB * t + k) % 2, 0:TC * PN].rearrange("p (j n) -> p j n", j=TC),
                                                 ACT.Copy).then_inc(probsT_act, 1)
                        for u in slots[t][0]:
                            unit_hi(units_before(half, a), at, b + 1, u)
                        if t + 2 < NP:
                            exponentials(b, t + 2)
                        elif project:
                            exponentials(b + 1, t + 2 - NP)
                        for u in slots[t][1]:
                            unit_hi(units_before(half, a), at, b + 1, u)
                    act.wait_ge(values_done, (b + 1) * NP + 2)
                    nc.scalar.activation(keep["outT"][:, a], ps_out[:, 0:2 * PN], ACT.Copy).then_inc(out_copied, 1)

                nc.scalar.activation(keep["credit"][:, 1:2], keep["ident"][:, 0:1], ACT.Copy).then_inc(probsT_act, 2)
                nc.scalar.activation(keep["credit"][:, 2:3], keep["ident"][:, 0:1], ACT.Copy).then_inc(out_copied, 1)

                def prepare(n):
                    if n == 1:
                        act.wait_ge(prepared_in_psum, W_T)
                        nc.scalar.activation(keep["wT_hi"][:], split(ps_scores[:, 0], KT), ACT.Copy).then_inc(prepared_out, 1)
                        act.wait_ge(prepared_in_psum, GATE_T)
                        nc.scalar.activation(keep["gateT"][:], split(ps_out[:, 0:KT * E], KT), ACT.Copy).then_inc(prepared_out, 1)
                        act.wait_ge(atom_steps, 1)
                        nc.scalar.activation(atom_p[:], atom_w[:], ACT.Exp, bias=atom_shift[:, 0:1], accum_out=atom_sum[:, 0:1]).then_inc(atom_exp, 1)
                        act.wait_ge(load["imp"], 16)
                        nc.scalar.activation(importance[:], importance[:], ACT.Exp, scale=-1.0).then_inc(gate_exp, 1)
                    if n == 2:
                        act.wait_ge(prepared_in_psum, WO_T)
                        nc.scalar.activation(keep["wo_intT"][:], split(psb_scores[:, 1, 0:KT * D], KT), ACT.Copy).then_inc(prepared_out, 1)
                        act.wait_ge(prepared_in_psum, SCALE_ROW)
                        nc.scalar.activation(keep["wo_scale_row"][:], ps_scores[0:TT, 2, 0:D], ACT.Copy).then_inc(prepared_out, 1)
                    if n == 3:
                        act.wait_ge(prepared_in_psum, ATOM_T)
                        nc.scalar.activation(atom_pT[:], ps_out[0:A_ATOMS, 0:E], ACT.Copy).then_inc(prepared_out, 1)
                    if n == 5:
                        act.wait_ge(gate_steps, 4)
                        nc.scalar.activation(keep["w_stack"][0:E], gate, ACT.Copy).then_inc(w8_hi_ready, 1)

                for n, u in enumerate(ORDER):
                    unit_hi(0, AT, 0, u)
                    prepare(PREPARE_AT.get(n, 0))
                exponentials(0, 0)
                exponentials(0, 1)
                for a in range(2):
                    batch(a, 0, a, UNITS, AT)
                with act.Fori(1, B // 2 - 1) as i:
                    batch(2 * i, i, 0, UNITS_R, AT_R)
                    batch(2 * i + 1, i, 1, UNITS, AT)
                batch(B - 2, B // 2 - 1, 0, UNITS_R, AT_R)
                batch(B - 1, B // 2 - 1, 1, [([], [])] * NP, {})

            @block.vector
            def _(dve):
                def result(first, at, tile, k):
                    bank = at[("R", k, 0)] % 2
                    done = tile * R_STEPS
                    dve.wait_ge(unit_in_psum, first + at[("R", k, 0)] + 1)
                    if k == 0:
                        nc.vector.reciprocal(rsum[:], keep["sums"][:, bass.ds(2 * tile, 2)]).then_inc(r_steps, 1)
                        dve.wait_ge(r_steps, done + 1)
                        nc.vector.tensor_tensor(r_norm[:], ps_proj[0:PN, bank].rearrange("p (k d) -> p k d", d=PD),
                                                rsum[:].rearrange("p b k -> p (b k)").unsqueeze(2).broadcast_to([PN, 2 * NP, PD]),
                                                ALU.mult).then_inc(unit_out, 1)
                    elif k == 1:
                        nc.vector.tensor_tensor(r_sb[:], ps_proj[0:TT, bank, 0:D], keep["bv_row"][:], ALU.add).then_inc(unit_out, 1)
                        dve.wait_ge(unit_out, first + at[("R", 1, 0)] + 1 + 2)
                        nc.vector.tensor_reduce(r_scale[:], r_sb[:], AX.X, ALU.max, apply_absolute_value=True).then_inc(r_steps, 1)
                        dve.wait_ge(r_steps, done + 2)
                        nc.vector.tensor_scalar(r_scale[:], r_scale[:], 1.0 / QMAX, QEPS, ALU.mult, ALU.max).then_inc(r_steps, 1)
                        dve.wait_ge(r_steps, done + 3)
                        nc.vector.reciprocal(r_inv[:], r_scale[:]).then_inc(r_steps, 1)
                        dve.wait_ge(r_steps, done + 4)
                        nc.vector.tensor_scalar(r_tmp[:], r_sb[:], r_inv[:, 0:1], ROUND, ALU.mult, ALU.add).then_inc(r_steps, 1)
                        dve.wait_ge(r_steps, done + 5)
                        nc.vector.tensor_scalar(r_int[:], r_tmp[:], ROUND, QMAX, ALU.subtract, ALU.min).then_inc(r_int_ready, 1)
                    elif k == 2:
                        nc.vector.tensor_scalar(r_intT[:], split(psb_proj[:, bank, 0:KT * TT], KT), -QMAX, None, ALU.max).then_inc(unit_out, 1)
                    else:
                        nc.vector.scalar_tensor_tensor(out=r_tmp[:], in0=ps_proj[0:TT, bank, 0:D], scalar=r_scale[:, 0:1],
                                                       in1=keep["wo_scale_row"][:], op0=ALU.mult, op1=ALU.mult).then_inc(unit_out, 1)
                        dve.wait_ge(unit_out, first + at[("R", 3, 0)] + 1 + 2)
                        nc.vector.tensor_tensor(resid[:], r_tmp[:], x1[:, tile], ALU.add).then_inc(r_steps, 1)
                        dve.wait_ge(r_steps, done + 6)
                        nc.vector.bn_stats(stats[:], resid[:]).then_inc(r_steps, 1)
                        dve.wait_ge(r_steps, done + 7)
                        nc.vector.memset(r_cell[:], 0.0).then_inc(r_steps, 1)
                        nc.vector.bn_aggr(mv[:], stats[:]).then_inc(r_steps, 1)
                        dve.wait_ge(r_steps, done + 9)
                        nc.vector.tensor_scalar(var_eps[:, bass.ds(tile, 1)], mv[:, 1:2], LN_EPS, None, ALU.add).then_inc(var_ready, 1)

                def centre(tile):
                    dve.wait_ge(rstd_ready, tile + 1)
                    nc.vector.tensor_scalar(x2[:, tile], resid[:], mv[:, 0:1], rstd[:, bass.ds(tile, 1)], ALU.subtract, ALU.mult).then_inc(r_steps, 2)

                def unit_rest(first, at, n, u, a):
                    kind, p, q = u
                    bank = at[u] % 2
                    if kind == "R":
                        result(first, at, n, p)
                        return
                    if kind == "V":
                        dve.wait_ge(unit_in_psum, first + at[u] + 1)
                        nc.vector.tensor_copy(v_sb[0:LT, a, 2 * p:2 * p + 2], split(ps_proj[0:LT, bank], 2)).then_inc(unit_out, 1)
                        return
                    dve.wait_ge(hi_ready, n * NHI + HI_AT[u] + 1)
                    if kind == "X":
                        c = slice(p * LC, (p + 1) * LC)
                        nc.vector.tensor_tensor(cT_lo[:, q, c], ps_proj[:, bank, 0:LC], cT_hi[:, q, c].bitcast(F32),
                                                ALU.subtract).then_inc(unit_out, 1)
                    else:
                        c = slice(q * LC, (q + 1) * LC)
                        nc.vector.scalar_tensor_tensor(out=k_lo[:, c], in0=ps_proj[:, bank, 0:LC], scalar=keep["xbk"][:, p:p + 1],
                                                       in1=k_hi[:, c].bitcast(F32), op0=ALU.add, op1=ALU.subtract).then_inc(unit_out, 1)

                def masked_scores(b, half, a, t, before):
                    if t == 0:
                        dve.wait_ge(mask_in[a], 32 * (half + 1))
                    if before:
                        dve.wait_ge(probsT_in_psum, TB * (b * NP + t - 1))
                    if before:
                        dve.wait_ge(wait_taken, b * NP + t)
                    dve.wait_ge(scores_in_psum, b * NP + t + 1)
                    nc.vector.memset(wait_cell[:], 0.0).then_inc(wait_taken, 1)
                    nc.vector.tensor_tensor_reduce(out=split(scores[:, t % 2], NC), in0=ps_scores[0:PN, :, 0:LC],
                                                   in1=split(mask_sb[:, a], NC), scale=-1.0, scalar=BIG, op0=ALU.add, op1=ALU.min,
                                                   accum_out=shift[:, t % 2:t % 2 + 1]).then_inc(scores_ready, 1)

                def units_rest(b, half, a, slots, at, t, after):
                    for u in slots[t][after]:
                        unit_rest(units_before(half, a), at, half - 1 if u[0] == "R" else b + 1, u, 1 - a)

                def batch(b, half, a, slots, at, former=None):
                    project = bool(at)
                    now = (b, half, a, slots, at)
                    for t in range(NP):
                        dve.wait_ge(values_done, b * NP + t + 1)
                        dve.wait_ge(probsT_in_psum, TB * (b * NP + t) + 1)
                        nc.vector.tensor_copy(probsT[:, t % 2, 0:TC],
                                              ps_T[0:LT, (TB * t) % 2, 0:TC * PN].rearrange("p (j n) -> p j n", j=TC)).then_inc(probsT_dve, 1)
                        if t > 0:
                            units_rest(*now, t - 1, 1)
                        elif former:
                            units_rest(*former, NP - 1, 1)
                        if t + 2 < NP:
                            masked_scores(b, half, a, t + 2, True)
                        elif project:
                            masked_scores(b + 1, half + a, 1 - a, t + 2 - NP, True)
                        units_rest(*now, t, 0)
                    if at is AT_R:
                        centre(half - 1)

                nc.vector.memset(keep["credit"][:, 0:1], 0.0).then_inc(unit_out, 2)

                def prepare(n):
                    if n == 1:
                        nc.vector.memset(ones, 1.0).then_inc(ones_set, 1)
                        dve.wait_ge(load["wo"], 16)
                        nc.vector.tensor_reduce(wo_scale[:], wo_raw, AX.X, ALU.max, apply_absolute_value=True).then_inc(wo_steps, 1)
                        dve.wait_ge(load["atom_w"], 16)
                        nc.vector.tensor_reduce(atom_shift[:], atom_w[:], AX.X, ALU.max, negate=True).then_inc(atom_steps, 1)
                        dve.wait_ge(wo_steps, 1)
                        nc.vector.tensor_scalar(wo_scale[:], wo_scale[:], 1.0 / QMAX, QEPS, ALU.mult, ALU.max).then_inc(wo_steps, 1)
                        dve.wait_ge(wo_steps, 2)
                        nc.vector.reciprocal(wo_inv[:], wo_scale[:]).then_inc(wo_steps, 1)
                        for e in range(KT):
                            nc.vector.tensor_scalar(diag[:, e], keep["ident"][:], wo_scale[:, e:e + 1], None, ALU.mult).then_inc(diag_ready, 1)
                        dve.wait_ge(wo_steps, 3)
                        for e in range(KT):
                            nc.vector.tensor_scalar(wo_tmp[:, e], wo_raw[:, e], wo_inv[:, e:e + 1], ROUND, ALU.mult, ALU.add).then_inc(wo_steps, 1)
                        dve.wait_ge(wo_steps, 5)
                        nc.vector.tensor_scalar(wo_tmp, wo_tmp, ROUND, QMAX, ALU.subtract, ALU.min).then_inc(wo_steps, 1)
                        dve.wait_ge(wo_steps, 6)
                        nc.vector.tensor_scalar(wo_int, wo_tmp, -QMAX, None, ALU.max).then_inc(wo_int_ready, 1)
                        dve.wait_ge(prepared_out, W_T)
                        nc.vector.tensor_tensor(keep["wT_lo"][:], split(ps_scores[:, 0], KT), keep["wT_hi"][:].bitcast(F32), ALU.subtract).then_inc(wT_lo_ready, 1)
                    if n == 2:
                        dve.wait_ge(atom_exp, 1)
                        nc.vector.reciprocal(atom_rsum[:], atom_sum[:]).then_inc(atom_steps, 1)
                        dve.wait_ge(atom_steps, 2)
                        nc.vector.tensor_scalar(atom_pn[:], atom_p[:], atom_rsum[:, 0:1], None, ALU.mult).then_inc(atom_steps, 1)
                        dve.wait_ge(gate_exp, 1)
                        nc.vector.tensor_scalar(importance[:], importance[:], 1.0, None, ALU.add).then_inc(gate_steps, 1)
                        dve.wait_ge(gate_steps, 1)
                        nc.vector.reciprocal(importance[:], importance[:]).then_inc(gate_steps, 1)
                    if n == 3:
                        dve.wait_ge(load["bo"], 16)
                        nc.vector.tensor_tensor(x1[:], x1[:], bo_row.unsqueeze(1).broadcast_to([TT, NT, D]), ALU.add).then_inc(x1_bo_ready, 1)
                    if n == 5:
                        dve.wait_ge(prepared_in_psum, DELTAS)
                        dve.wait_ge(gate_in, 16)
                        g = gate[:, 0:NC * 512].rearrange("p (a b) -> p a b", a=NC)
                        nc.vector.tensor_tensor(g, ps_scores[0:E, 0:NC], g, ALU.mult).then_inc(gate_steps, 1)
                        g = gate[:, NC * 512:NS]
                        nc.vector.tensor_tensor(g, ps_T[0:E, 0], g, ALU.mult).then_inc(gate_steps, 1)
                    if n == 6:
                        dve.wait_ge(w8_hi_ready, 1)
                        nc.vector.tensor_tensor(w8_lo, gate, keep["w_stack"][0:E].bitcast(F32), ALU.subtract).then_inc(w8_lo_ready, 1)

                for n, u in enumerate(ORDER):
                    unit_rest(0, AT, 0, u, 0)
                    prepare(PREPARE_AT.get(n, 0))
                dve.wait_ge(w8_lo_ready, 1)
                dve.wait_ge(x1_bo_ready, 1)
                dve.wait_ge(load["bv"], 16)
                masked_scores(0, 0, 0, 0, False)
                masked_scores(0, 0, 0, 1, False)
                def plain(half, a):
                    return 2 * half + a, half, a, UNITS, AT

                def finishing(half):
                    return 2 * half, half, 0, UNITS_R, AT_R

                batch(*plain(0, 0))
                batch(*plain(0, 1), former=plain(0, 0))
                with dve.Fori(1, B // 2 - 1) as i:
                    batch(*finishing(i), former=plain(i - 1, 1))
                    batch(*plain(i, 1), former=finishing(i))
                last = B // 2 - 1
                batch(*finishing(last), former=plain(last - 1, 1))
                batch(B - 1, last, 1, [([], [])] * NP, {}, former=finishing(last))
                for k in range(NR):
                    unit_rest(units_before(B // 2 - 1, 1), AT_LAST, NT - 1, ("R", k, 0), 0)
                centre(NT - 1)


def kept(nc, ctx):
    sb = lambda n, s, d=F32: ctx.enter_context(nc.sbuf_tensor(n, s, d))
    return {
        "ident": sb("ident", [P, P]),
        "ident_b": sb("ident_b", [P, P], BF16),
        "sel": sb("sel", [PN, 4, TT]),
        "x1": sb("x1", [TT, NT, D]),
        "outT": sb("outT", [P, 2, 2 * PN]),
        "sums": sb("sums", [PN, B, NP]),
        "wkT_hi": sb("wkT_hi", [P, KT, D], F32R),
        "wkT_lo": sb("wkT_lo", [P, KT, D], F32R),
        "wvT_hi": sb("wvT_hi", [P, KT, D], F32R),
        "wvT_lo": sb("wvT_lo", [P, KT, D], F32R),
        "xbk": sb("xbk", [P, KT]),
        "credit": sb("credit", [P, 4]),
        "wT_hi": sb("wfT_hi", [P, KT, D], F32R),
        "wT_lo": sb("wfT_lo", [P, KT, D], F32R),
        "wo_intT": sb("wo_intT", [P, KT, D], BF16),
        "wo_scale_row": sb("wo_scale_row", [TT, D]),
        "bv_row": sb("bv_row", [TT, D]),
        "gateT": sb("gateT", [P, KT, E]),
        "w_stack": sb("w_stack", [EST * E, NS], F32R),
    }


NST = NS // P
CLIP = 50.0


def feed_forward_phase(nc, io, keep):
    ctx = ExitStack()
    with ctx:
        sb = lambda n, s, d=F32: ctx.enter_context(nc.sbuf_tensor(n, s, d))
        sem = lambda n: ctx.enter_context(nc.semaphore(n))
        wT_hi, wT_lo, gateT, w_stack = (keep[n] for n in ("wT_hi", "wT_lo", "gateT", "w_stack"))
        x2 = keep["x1"]
        idx_row = sb("idx_row", [P, NS], I32)
        idx_col = sb("idx_col", [P, NST], I32)
        col_i = idx_row
        row_i = sb("row_i", [P, NST], I32)
        row_f = sb("row_f", [P, NST])
        channel = sb("channel", [P, KT])
        channel_row = sb("channel_row", [P, D])
        expert_row = sb("expert_row", [TT, E])
        pick_c = sb("pick_c", [P, KT, NS], F32R)
        pick_r = sb("pick_r", [P, NST, D], F32R)
        stats = sb("stats3", [TT, NT, 6])
        mv = sb("mv3", [TT, NT, 2])
        var_eps = sb("var_eps3", [TT, NT])
        minus_half = sb("minus_half3", [TT, NT])
        rstd = sb("rstd3", [TT, NT])
        x2T_hi = sb("x2T_hi", [P, KT, T], F32R)
        x2T_lo = sb("x2T_lo", [P, KT, T], F32R)
        logits = sb("logits", [TT, NT, E])
        top = sb("top", [TT, NT, 8])
        top_i = sb("top_i", [TT, NT, 8], U32)
        top_f = sb("top_f", [TT, NT, 8])
        gap = sb("gap", [TT, NT])
        egap = sb("egap", [TT, NT])
        den = sb("den", [TT, NT])
        route = sb("route", [TT, 2, NT])
        hit = sb("hit", [TT, 2, NT, E])
        hit_w = sb("hit_w", [TT, 2, NT, E])
        comb = sb("comb", [TT, NT, E])
        c_stack = sb("c_stack", [EST * E, T], F32R)
        c_lo = sb("c_lo", [E, T], F32R)
        xg_sb = sb("xg_sb", [P, 2, HALF])
        prod = sb("prod", [P, 3, HALF])
        prod_hi = sb("prod_hi", [P, 3, HALF], F32R)
        prod_lo = sb("prod_lo", [P, 3, HALF], F32R)
        ffT = sb("ffT", [P, KT, T])
        resid3 = y_sb = sb("y_sb", [TT, NT, D])
        ps = ctx.enter_context(nc.psum_tensor("psC", [P, 8, 512], F32))

        load = {n: sem(f"in_{n}") for n in ("idx_row", "idx_col")}
        channels = sem("channels")
        idx_steps = sem("idx_steps")
        stats_ready = sem("stats3_ready")
        mv_ready = sem("mv3_ready")
        var_ready = sem("var3_ready")
        rstd_ready = sem("rstd3_ready")
        x2T_in_psum = sem("x2T_in_psum")
        x2T_hi_ready = sem("x2T_hi_ready")
        x2T_lo_ready = sem("x2T_lo_ready")
        logits_in_psum = sem("logits_in_psum")
        route_steps = sem("route_steps")
        egap_ready = sem("egap_ready")
        combT_in_psum = sem("combT_in_psum")
        c_hi_ready = sem("c_hi_ready")
        c_lo_ready = sem("c_lo_ready")
        c_stacked = [sem(f"c_stacked{h}") for h in range(2)]
        xg_in_psum = sem("xg_in_psum")
        xg_copied = sem("xg_copied")
        vals_in_psum = sem("vals_in_psum")
        prod_ready = sem("prod_ready")
        prod_hi_ready = sem("prod_hi_ready")
        prod_lo_ready = sem("prod_lo_ready")
        contributed = sem("contributed")
        ff_copied = sem("ff_copied")
        ff_in_psum = sem("ff_in_psum")
        resid3_ready = sem("resid3_ready")
        y_ready = sem("y_ready")
        stored = sem("stored")

        def row(ap, n, width=D):
            return ap.unsqueeze(0).broadcast_to([n, width])

        def half(h):
            return slice(h * HALF, (h + 1) * HALF)

        def tiles(h):
            return range(h * HT, (h + 1) * HT)

        UNIT = [(h, j) for h in range(2) for j in range(NST)]
        LAG = 2

        with nc.Block() as block:

            @block.sync
            def _(sp):
                sp.dma_start(idx_col[:], io["L0_ffn_mask_idx"].rearrange("(j p) -> p j", p=P),
                             allow_slow_non_contiguous=True).then_inc(load["idx_col"], 16)
                sp.dma_start(idx_row[:], row(io["L0_ffn_mask_idx"], P, NS)).then_inc(load["idx_row"], 16)
                for h in range(2):
                    sp.wait_ge(c_hi_ready, h + 1)
                    sp.dma_start(c_stack[E:2 * E, half(h)].bitcast(F32), c_stack[0:E, half(h)].bitcast(F32)).then_inc(c_stacked[h], 16)
                    sp.wait_ge(c_lo_ready, h + 1)
                    sp.dma_start(c_stack[2 * E:3 * E, half(h)].bitcast(F32), c_lo[:, half(h)].bitcast(F32)).then_inc(c_stacked[h], 16)
                for h in range(2):
                    sp.wait_ge(y_ready, (h + 1) * HT)
                    sp.dma_start(io["out"].rearrange("b s d -> (b s) d").rearrange("(i p) d -> p i d", p=TT)[:, h * HT:(h + 1) * HT],
                                 y_sb[:, h * HT:(h + 1) * HT]).then_inc(stored, 16)
                sp.wait_ge(stored, 32)

            @block.gpsimd
            def _(pool):
                nc.gpsimd.iota(channel[:], pattern=[[P, KT]], base=0, channel_multiplier=1,
                               allow_small_or_imprecise_dtypes=True).then_inc(channels, 1)
                nc.gpsimd.iota(channel_row[:], pattern=[[1, D]], base=0, channel_multiplier=0,
                               allow_small_or_imprecise_dtypes=True).then_inc(channels, 1)
                nc.gpsimd.iota(expert_row[:], pattern=[[1, E]], base=0, channel_multiplier=0,
                               allow_small_or_imprecise_dtypes=True).then_inc(channels, 1)
                nc.gpsimd.memset(minus_half[:], -0.5).then_inc(channels, 1)
                pool.wait_ge(channels, 4)
                for n, (h, j) in enumerate(UNIT):
                    pool.wait_ge(prod_hi_ready, n + 1)
                    nc.gpsimd.tensor_tensor(prod_lo[:, n % 3], prod[:, n % 3], prod_hi[:, n % 3].bitcast(F32), ALU.subtract).then_inc(prod_lo_ready, 1)
                for h in range(2):
                    g = slice(h * HT, (h + 1) * HT)
                    pool.wait_ge(var_ready, h + 1)
                    nc.gpsimd.tensor_tensor(rstd[:, g], var_eps[:, g], minus_half[:, g], ALU.pow).then_inc(rstd_ready, 1)

            @block.tensor
            def _(pe):
                for h in range(2):
                    for m in range(KT):
                        for j, i in enumerate(tiles(h)):
                            last = nc.tensor.transpose(ps[:, 2 * h + m, j * TT:(j + 1) * TT], x2[:, i, m * P:(m + 1) * P], keep["ident"][0:TT, 0:TT])
                        last.then_inc(x2T_in_psum, 1)
                for h in range(2):
                    pe.wait_ge(x2T_lo_ready, KT * (h + 1))
                    for i in tiles(h):
                        mm = [(part[:, m, i * TT:(i + 1) * TT].bitcast(F32), gateT[:, m]) for m in range(KT) for part in (x2T_hi, x2T_lo)]
                        for n, (x, g) in enumerate(mm):
                            last = nc.tensor.matmul(ps[0:TT, 6, i * E:(i + 1) * E], x, g, start=n == 0, stop=n == len(mm) - 1)
                last.then_inc(logits_in_psum, 1)
                def dense(h):
                    for m in range(KT):
                        e = slice(m * P, (m + 1) * P)
                        mm = [t for k in range(KT) for t in ((wT_hi[:, k, e], x2T_hi[:, k, half(h)]), (wT_hi[:, k, e], x2T_lo[:, k, half(h)]),
                                                             (wT_lo[:, k, e], x2T_hi[:, k, half(h)]))]
                        for n, (w, x) in enumerate(mm):
                            nc.tensor.matmul(ps[:, 4 + 2 * h + m, 0:HALF], w, x, start=n == 0, stop=False)

                dense(0)

                def gather(n):
                    h, j = UNIT[n]
                    if n >= 2:
                        pe.wait_ge(xg_copied, n - 1)
                    mm = [(pick_c[:, m, j * P:(j + 1) * P], part[:, m, half(h)]) for m in range(KT) for part in (x2T_hi, x2T_lo)]
                    for k, (w, x) in enumerate(mm):
                        last = nc.tensor.matmul(ps[:, n % 2, 0:HALF], w, x, start=k == 0, stop=k == len(mm) - 1)
                    last.then_inc(xg_in_psum, 1)

                def values(n):
                    h, j = UNIT[n]
                    if n >= 2:
                        pe.wait_ge(prod_ready, n - 1)
                    if j == 0:
                        pe.wait_ge(c_stacked[h], 32)
                    nc.tensor.matmul(ps[:, 2 + n % 2, 0:HALF], w_stack[:, j * P:(j + 1) * P], c_stack[:, half(h)],
                                     start=True, stop=True).then_inc(vals_in_psum, 1)

                def scatter(n):
                    h, j = UNIT[n]
                    pe.wait_ge(prod_lo_ready, n + 1)
                    for m in range(KT):
                        for part in (prod_hi, prod_lo):
                            last = nc.tensor.matmul(ps[:, 4 + 2 * h + m, 0:HALF], pick_r[:, j, m * P:(m + 1) * P], part[:, n % 3],
                                                    start=False, stop=j == NST - 1 and part is prod_lo)
                    last.then_inc(contributed, 1)

                def back(h):
                    pe.wait_ge(ff_copied, KT * (h + 1))
                    for j, i in enumerate(tiles(h)):
                        for m in range(KT):
                            last = nc.tensor.transpose(ps[0:TT, 4 + 2 * h + j // 2, (j % 2) * D + m * P:(j % 2) * D + (m + 1) * P],
                                                       ffT[:, m, i * TT:(i + 1) * TT], keep["ident"][:])
                        if j % 2:
                            last.then_inc(ff_in_psum, 1)

                pe.wait_ge(idx_steps, 4 + KT + NST)
                gather(0)
                gather(1)
                pe.wait_ge(route_steps, ROUTE_STEPS)
                for h in range(2):
                    if h == 1:
                        pe.wait_ge(c_lo_ready, 1)
                    for j, i in enumerate(tiles(h)):
                        last = nc.tensor.transpose(ps[0:E, 7, j * TT:(j + 1) * TT], comb[:, i], keep["ident"][0:TT, 0:TT])
                    last.then_inc(combT_in_psum, 1)
                pe.wait_ge(c_lo_ready, 2)
                for n, (h, j) in enumerate(UNIT):
                    if n >= 2:
                        gather(n)
                    values(n)
                    if n >= LAG:
                        scatter(n - LAG)
                    if (h, j) == (0, 8):
                        dense(1)
                    if (h, j) == (1, 6):
                        back(0)
                scatter(len(UNIT) - 2)
                scatter(len(UNIT) - 1)
                back(1)

            @block.scalar
            def _(act):
                for h in range(2):
                    for m in range(KT):
                        act.wait_ge(x2T_in_psum, KT * h + m + 1)
                        nc.scalar.activation(x2T_hi[:, m, half(h)], ps[:, 2 * h + m, 0:HALF], ACT.Copy).then_inc(x2T_hi_ready, 1)
                act.wait_ge(route_steps, NT + 2)
                nc.scalar.activation(egap[:], gap[:], ACT.Exp).then_inc(egap_ready, 1)
                def routing_hi(h):
                    act.wait_ge(combT_in_psum, h + 1)
                    nc.scalar.activation(c_stack[0:E, half(h)], ps[0:E, 7, 0:HALF], ACT.Copy).then_inc(c_hi_ready, 1)

                def gathered(n):
                    act.wait_ge(xg_in_psum, n + 1)
                    if n >= 2:
                        act.wait_ge(prod_ready, n - 1)
                    nc.scalar.activation(xg_sb[:, n % 2], ps[:, n % 2, 0:HALF], ACT.Copy).then_inc(xg_copied, 1)

                gathered(0)
                routing_hi(0)
                routing_hi(1)
                gathered(1)
                for n, (h, j) in enumerate(UNIT):
                    act.wait_ge(prod_ready, n + 1)
                    if n >= 3:
                        act.wait_ge(contributed, n - 2)
                    nc.scalar.activation(prod_hi[:, n % 3], prod[:, n % 3], ACT.Copy).then_inc(prod_hi_ready, 1)
                    if n + 2 < len(UNIT):
                        gathered(n + 2)
                    if (h, j) == (1, 3):
                        act.wait_ge(contributed, NST)
                        for m in range(KT):
                            nc.scalar.activation(ffT[:, m, half(0)], ps[:, 4 + m, 0:HALF], ACT.Copy).then_inc(ff_copied, 1)
                act.wait_ge(contributed, 2 * NST)
                for m in range(KT):
                    nc.scalar.activation(ffT[:, m, half(1)], ps[:, 6 + m, 0:HALF], ACT.Copy).then_inc(ff_copied, 1)

            @block.vector
            def _(dve):
                def normalise(h):
                    g = slice(h * HT, (h + 1) * HT)
                    for i in tiles(h):
                        nc.vector.bn_stats(stats[:, i], resid3[:, i]).then_inc(stats_ready, 1)
                    for i in tiles(h):
                        dve.wait_ge(stats_ready, i + 1)
                        nc.vector.bn_aggr(mv[:, i], stats[:, i]).then_inc(mv_ready, 1)
                    dve.wait_ge(mv_ready, (h + 1) * HT)
                    nc.vector.tensor_scalar(var_eps[:, g], mv[:, g, 1], LN_EPS, None, ALU.add).then_inc(var_ready, 1)

                def centre(h):
                    dve.wait_ge(rstd_ready, h + 1)
                    for i in tiles(h):
                        nc.vector.tensor_scalar(y_sb[:, i], resid3[:, i], mv[:, i, 0:1], rstd[:, i:i + 1], ALU.subtract, ALU.mult).then_inc(y_ready, 1)

                dve.wait_ge(load["idx_row"], 16)
                dve.wait_ge(load["idx_col"], 16)
                dve.wait_ge(channels, 4)
                nc.vector.tensor_single_scalar(col_i[:], idx_row[:], D - 1, ALU.bitwise_and).then_inc(idx_steps, 1)
                nc.vector.tensor_single_scalar(row_i[:], idx_col[:], 8, ALU.arith_shift_right).then_inc(idx_steps, 1)
                dve.wait_ge(idx_steps, 2)
                nc.vector.tensor_copy(row_f[:], row_i[:]).then_inc(idx_steps, 2)
                for m in range(KT):
                    nc.vector.tensor_scalar(pick_c[:, m], col_i[:], channel[:, m:m + 1], None, ALU.is_equal).then_inc(idx_steps, 1)
                dve.wait_ge(idx_steps, 4)
                for h in range(2):
                    for m in range(KT):
                        dve.wait_ge(x2T_hi_ready, KT * h + m + 1)
                        nc.vector.tensor_tensor(x2T_lo[:, m, half(h)], ps[:, 2 * h + m, 0:HALF], x2T_hi[:, m, half(h)].bitcast(F32), ALU.subtract).then_inc(x2T_lo_ready, 1)
                for j in range(NST):
                    nc.vector.tensor_scalar(pick_r[:, j], channel_row[:], row_f[:, j:j + 1], None, ALU.is_equal).then_inc(idx_steps, 1)

                step = [0]

                def routed(ins, wait=True):
                    step[0] += 1
                    ins.then_inc(route_steps, 1)
                    if wait:
                        dve.wait_ge(route_steps, step[0])

                dve.wait_ge(logits_in_psum, 1)
                routed(nc.vector.tensor_scalar(logits[:], ps[0:TT, 6, 0:NT * E].rearrange("p (i e) -> p i e", e=E), CLIP, -CLIP, ALU.min, ALU.max))
                for i in range(NT):
                    routed(nc.vector.max(top[:, i], logits[:, i]), wait=i == NT - 1)
                routed(nc.vector.tensor_tensor(gap[:], top[:, :, 1], top[:, :, 0], ALU.subtract), wait=False)
                for i in range(NT):
                    routed(nc.vector.max_index(top_i[:, i], top[:, i], logits[:, i]), wait=i == NT - 1)
                routed(nc.vector.tensor_copy(top_f[:], top_i[:]))
                dve.wait_ge(egap_ready, 1)
                routed(nc.vector.tensor_scalar(den[:], egap[:], 1.0, None, ALU.add))
                routed(nc.vector.reciprocal(route[:, 0], den[:]))
                routed(nc.vector.tensor_tensor(route[:, 1], egap[:], route[:, 0], ALU.mult), wait=False)
                for n in range(2):
                    routed(nc.vector.tensor_tensor(hit[:, n], expert_row[:].unsqueeze(1).broadcast_to([TT, NT, E]),
                                                   top_f[:, :, n:n + 1].broadcast_to([TT, NT, E]), ALU.is_equal), wait=n == 1)
                for n in range(2):
                    routed(nc.vector.tensor_tensor(hit_w[:, n], hit[:, n], route[:, n].unsqueeze(2).broadcast_to([TT, NT, E]), ALU.mult), wait=n == 1)
                routed(nc.vector.tensor_tensor(comb[:], hit_w[:, 0], hit_w[:, 1], ALU.add), wait=False)
                assert step[0] == ROUTE_STEPS
                for h in range(2):
                    dve.wait_ge(c_hi_ready, h + 1)
                    nc.vector.tensor_tensor(c_lo[:, half(h)], ps[0:E, 7, 0:HALF], c_stack[0:E, half(h)].bitcast(F32), ALU.subtract).then_inc(c_lo_ready, 1)

                def finish(h):
                    for j, i in enumerate(tiles(h)):
                        if j % 2 == 0:
                            dve.wait_ge(ff_in_psum, 2 * h + j // 2 + 1)
                        nc.vector.tensor_tensor(resid3[:, i], ps[0:TT, 4 + 2 * h + j // 2, (j % 2) * D:(j % 2 + 1) * D], x2[:, i], ALU.add).then_inc(resid3_ready, 1)
                    dve.wait_ge(resid3_ready, (h + 1) * HT)
                    normalise(h)

                for n, (h, j) in enumerate(UNIT):
                    dve.wait_ge(xg_copied, n + 1)
                    dve.wait_ge(vals_in_psum, n + 1)
                    if n >= 3:
                        dve.wait_ge(prod_lo_ready, n - 2)
                    nc.vector.tensor_tensor(prod[:, n % 3], ps[:, 2 + n % 2, 0:HALF], xg_sb[:, n % 2], ALU.mult).then_inc(prod_ready, 1)
                    if (h, j) == (1, 12):
                        finish(0)
                finish(1)
                for h in range(2):
                    centre(h)


ROUTE_STEPS = 2 * NT + 11


def build_program(nc, io):
    with ExitStack() as ctx:
        keep = kept(nc, ctx)
        self_attention_phase(nc, io, keep)
        cross_attention_phase(nc, io, keep)
        feed_forward_phase(nc, io, keep)


_INS = ["x", "ctx_2048", "mask_BxSxS2_ff0",
        "L0_attn_Wq", "L0_attn_bq", "L0_attn_Wk", "L0_attn_bk", "L0_attn_Wv", "L0_attn_bv", "L0_attn_Wo", "L0_attn_bo",
        "L0_xattn_wq", "L0_xattn_bq", "L0_xattn_wk", "L0_xattn_bk", "L0_xattn_wv", "L0_xattn_bv", "L0_xattn_wo", "L0_xattn_bo",
        "L0_ffn_gate_w", "L0_ffn_W", "L0_ffn_atoms", "L0_ffn_expert_atom_weights", "L0_ffn_importance", "L0_ffn_mask_idx"]


def kernel(**inputs):
    import numpy as np
    import concourse.bacc as bacc
    from concourse import mybir as mb
    from concourse.bass_utils import run_bass_kernel_spmd

    nc = bacc.Bacc("TRN2", target_bir_lowering=False, num_devices=1)
    arrays, io = {}, {}
    for name in _INS:
        a = np.ascontiguousarray(inputs[name])
        arrays[f"in_{name}"] = a
        io[name] = nc.dram_tensor(f"in_{name}", a.shape, mb.dt.from_np(a.dtype), kind="ExternalInput").ap()
    io["ctx"], io["mask"] = io["ctx_2048"], io["mask_BxSxS2_ff0"]
    io["out"] = nc.dram_tensor("out_0", (B, S, D), F32, kind="ExternalOutput").ap()
    for name in ("q_hi", "q_lo"):
        io[name] = nc.dram_tensor(name, (KT, P, B, PN), F32, kind="Internal").ap()
    io["gate"] = nc.dram_tensor("gate", (E, NS), F32, kind="Internal").ap()
    build_program(nc, io)
    r = run_bass_kernel_spmd(nc, [arrays], core_ids=[0])
    return r.results[0]["out_0"]
```

```python
import concourse.bass as bass
from concourse import mybir
from contextlib import ExitStack

F32 = mybir.dt.float32
F32R = mybir.dt.float32r
BF16 = mybir.dt.bfloat16
I32 = mybir.dt.int32
U32 = mybir.dt.uint32
ALU = mybir.AluOpType
ACT = mybir.ActivationFunctionType
AX = mybir.AxisListType

B, S, D = 16, 56, 256
H, DH = 16, 16
L = 1500
P = 128
KT = D // P
T = B * S
TT = 2 * S
NT = T // TT
HALF = T // 2
HT = HALF // TT
LT = 125
LC = 500
NC = L // LC
TC = LC // LT
NL = L // LT
NP = H // 2
PD = 2 * DH
PN = 2 * S
GP = P // PD
E, A_ATOMS, NS = 8, 64, 2048
SCALE = DH ** -0.5
QMAX = 127.0
QEPS = 1e-8
LN_EPS = 1e-5
ROUND = 1.5 * 2.0 ** 23
BIG = 3.0e38


def split(ap, n):
    return ap.rearrange("p (a b) -> p a b", a=n)


def load_chunk(sp, io, keep, b, c):
    sp.dma_start(split(keep["context"][0:LT], NL)[:, c * TC:(c + 1) * TC],
                 io["ctx"][b, c * LC:(c + 1) * LC].rearrange("(j p) d -> p j d", p=LT)).then_inc(keep["ctx_in"][c], 16)


def self_attention_phase(nc, io, keep):
    ctx = ExitStack()
    with ctx:
        sb = lambda n, s, d=F32: ctx.enter_context(nc.sbuf_tensor(n, s, d))
        sem = lambda n: ctx.enter_context(nc.semaphore(n))
        WK, WV, WQ, WO, XK, XV, XQ = range(7)
        names = ["L0_attn_Wk", "L0_attn_Wv", "L0_attn_Wq", "L0_attn_Wo",
                 "L0_xattn_wk", "L0_xattn_wv", "L0_xattn_wq"]
        w_raw = sb("w_raw", [P, 7, KT, D])
        wT = sb("wT", [P, 4, KT, D])
        x_sb = sb("x_sb", [TT, NT, D])
        xT = sb("xT", [P, KT, T])
        qkv_bias = sb("qkv_bias", [P, 3, KT])
        neg_bias = sb("neg_bias", [P, 3, KT])
        bo_row = sb("bo_row", [TT, D])
        xbq_row = sb("xbq_row", [TT, D])
        relu_pos = sb("relu_pos", [P, 4, 2, HALF])
        relu_neg = sb("relu_neg", [P, 4, 2, HALF])
        phi = sb("phi", [P, 4, 2, HALF])
        kv = sb("kv", [P, 4, HALF])
        kv_sum = sb("kv_sum", [P, 4, HALF])
        context = sb("context", [P, KT, T])
        keep_going = sb("keep_going", [P, HALF])
        def tokens_in(buf):
            return buf[0:TT].rearrange("p u n c -> p (u n c)")[:, 0:NT * D].rearrange("p (i d) -> p i d", i=NT)
        resid = tokens_in(relu_neg)
        stats = sb("stats", [TT, NT, 6])
        mv = sb("mv", [TT, NT, 2])
        var_eps = sb("var_eps", [TT, NT])
        minus_half = sb("minus_half", [TT, NT])
        rstd = sb("rstd", [TT, NT])
        wq_scale = sb("wq_scale", [P, KT])
        wq_inv = sb("wq_inv", [P, KT])
        wq_tmp = sb("wq_tmp", [P, KT, D])
        wq_int = sb("wq_int", [P, KT, D], BF16)
        wq_intT = sb("wq_intT", [P, KT, D], BF16)
        diag = sb("diag", [P, KT, P])
        ones = sb("ones", [P, TT])
        wq_scale_row = sb("wq_scale_row", [TT, D])
        x_scale = sb("x_scale", [TT, NT])
        x_inv = sb("x_inv", [TT, NT])
        x_tmp = tokens_in(phi)
        x_int = split(w_raw[0:TT].rearrange("p n k d -> p (n k d)")[:, NT * D:NT * D + NT * D // 2].bitcast(BF16), NT)
        x_intT = split(wT[:].rearrange("p n k d -> p (n k d)")[:, 0:KT * T // 2].bitcast(BF16), KT)
        head_of = sb("head_of", [P, 2 * GP])
        head_mask = sb("head_mask", [P, 2])
        query = resid
        q_scaled = split(w_raw[0:TT].rearrange("p n k d -> p (n k d)")[:, 0:NT * D], NT)
        stacks = keep["k_stack"][:].rearrange("p k l -> p (k l)")
        qbd_hi, qbd_lo = (stacks[:, n * KT * B * PN:(n + 1) * KT * B * PN].rearrange("p (m b e s) -> p m b e s", m=KT, b=B, e=2) for n in range(2))
        ps = ctx.enter_context(nc.psum_tensor("psA", [P, 8, 512], F32))
        psb = ps[:, :, :].bitcast(BF16)

        x_in = sem("x_in")
        w_in = [sem(f"w_in{k}") for k in range(7)]
        bias_in = sem("bias_in")
        row_in = sem("row_in")
        const_set = sem("const_set")
        dve_const = sem("dve_const")
        ident_ready = sem("ident_ready")
        identb_ready = sem("identb_ready")
        sel_ready = sem("sel_ready")
        head_of_ready = sem("head_of_ready")
        mask_ready = sem("mask_ready")
        xT_in_psum = sem("xT_in_psum")
        xT_dve = sem("xT_dve")
        xT_act = sem("xT_act")
        wT_in_psum = sem("wT_in_psum")
        wT_act = sem("wT_act")
        wT_lo = sem("wT_lo")
        qkv_in_psum = sem("qkv_in_psum")
        relus = sem("relus")
        exps = sem("exps")
        phis = sem("phis")
        v_used = sem("v_used")
        scanned = sem("scanned")
        context_ready = sem("context_ready")
        attn_in_psum = sem("attn_in_psum")
        xbo_ready = sem("xbo_ready")
        resid_ready = sem("resid_ready")
        stats_ready = sem("stats_ready")
        mv_ready = sem("mv_ready")
        var_ready = sem("var_ready")
        rstd_ready = sem("rstd_ready")
        x1_ready = sem("x1_ready")
        x1_pool = sem("x1_pool")
        wq_steps = sem("wq_steps")
        wq_int_ready = sem("wq_int_ready")
        diag_ready = sem("diag_ready")
        wqT_in_psum = sem("wqT_in_psum")
        wqT_ready = sem("wqT_ready")
        row_in_psum = sem("row_in_psum")
        row_ready = sem("row_ready")
        x_steps = sem("x_steps")
        x_int_ready = sem("x_int_ready")
        x_intT_in_psum = sem("x_intT_in_psum")
        x_intT_ready = sem("x_intT_ready")
        q_in_psum = sem("q_in_psum")
        q_scaled_ready = sem("q_scaled_ready")
        query_ready = sem("query_ready")
        qT_in_psum = sem("qT_in_psum")
        qbd_hi_ready = sem("qbd_hi_ready")
        qbd_lo_ready = sem("qbd_lo_ready")
        q_stored = keep["q_stored"]

        def batches(h):
            return slice(h * B // 2, (h + 1) * B // 2)

        def qT(m, h):
            return ps[:, 4 + 2 * m + h, 0:HALF].rearrange("p (b s) -> p b s", s=S)

        def column(ap):
            return ap.rearrange("(k p) -> p k", k=KT)

        def row(ap, n):
            return ap.unsqueeze(0).broadcast_to([n, D])

        with nc.Block() as block:

            @block.sync
            def _(sp):
                sp.dma_start(x_sb[:], io["x"].rearrange("b s d -> (b s) d").rearrange("(i p) d -> p i d", p=TT)
                             ).then_inc(x_in, 16)
                for k in range(7):
                    sp.dma_start(w_raw[:, k], io[names[k]].rearrange("(k p) d -> p k d", p=P)).then_inc(w_in[k], 16)
                for c in range(NC):
                    load_chunk(sp, io, keep, 0, c)
                for h in range(2):
                    for m in range(KT):
                        bs = slice(h * B // 2, (h + 1) * B // 2)
                        sp.wait_ge(qbd_hi_ready, 2 * (2 * h + m + 1))
                        sp.dma_start(io["q_hi"][m, :, bs], qbd_hi[:, m, bs].bitcast(F32).rearrange("p b e n -> p b (e n)")).then_inc(q_stored, 16)
                        sp.wait_ge(qbd_lo_ready, 2 * (2 * h + m + 1))
                        sp.dma_start(io["q_lo"][m, :, bs], qbd_lo[:, m, bs].bitcast(F32).rearrange("p b e n -> p b (e n)")).then_inc(q_stored, 16)

            @block.gpsimd
            def _(pool):
                nc.gpsimd.memset(keep["ident"][:], 0.0).then_inc(const_set, 1)
                nc.gpsimd.memset(keep["sel"][:], 0.0).then_inc(const_set, 1)
                nc.gpsimd.memset(head_of[:], 1.0).then_inc(const_set, 1)
                nc.gpsimd.memset(minus_half[:], -0.5).then_inc(const_set, 1)
                pool.wait_ge(const_set, 4)
                nc.gpsimd.affine_select(out=keep["ident"][:], in_=keep["ident"][:], compare_op=ALU.not_equal,
                                        fill=1.0, base=0, pattern=[[-1, P]], channel_multiplier=1).then_inc(ident_ready, 1)
                for e in range(2):
                    for a in range(2):
                        v = keep["sel"][:, 2 * e + a, a * S:(a + 1) * S]
                        nc.gpsimd.affine_select(out=v, in_=v, compare_op=ALU.not_equal, fill=1.0, base=-e * S,
                                                pattern=[[-1, S]], channel_multiplier=1).then_inc(sel_ready, 1)
                nc.gpsimd.affine_select(out=head_of[:], in_=head_of[:], compare_op=ALU.is_ge, fill=0.0, base=0,
                                        pattern=[[-DH, 2 * GP]], channel_multiplier=1).then_inc(head_of_ready, 1)
                pool.wait_ge(head_of_ready, 1)
                nc.gpsimd.affine_select(out=head_of[:], in_=head_of[:], compare_op=ALU.is_ge, fill=0.0, base=DH - 1,
                                        pattern=[[DH, 2 * GP]], channel_multiplier=-1).then_inc(head_of_ready, 1)
                pool.wait_ge(sel_ready, 4)
                for h in range(2):
                    g = slice(h * HT, (h + 1) * HT)
                    pool.wait_ge(var_ready, h + 1)
                    nc.gpsimd.tensor_tensor(rstd[:, g], var_eps[:, g], minus_half[:, g], ALU.pow).then_inc(rstd_ready, 1)
                pool.wait_ge(rstd_ready, 2)
                for i in range(HT + 1, NT):
                    nc.gpsimd.tensor_scalar(keep["x1"][:, i], resid[:, i], mv[:, i, 0:1], rstd[:, i:i + 1],
                                            ALU.subtract, ALU.mult).then_inc(x1_pool, 1)

            @block.tensor
            def _(pe):
                pe.wait_ge(ident_ready, 1)
                pe.wait_ge(x_in, 16)
                for m in range(KT):
                    for h in range(2):
                        for j in range(HT):
                            last = nc.tensor.transpose(ps[:, 2 * m + h, j * TT:(j + 1) * TT],
                                                       x_sb[:, h * HT + j, m * P:(m + 1) * P], keep["ident"][0:TT, 0:TT])
                        last.then_inc(xT_in_psum, 1)

                def weight_transpose(k):
                    pe.wait_ge(w_in[k], 16)
                    if k >= 2:
                        pe.wait_ge(wT_act, k - 1)
                    if k >= 6:
                        pe.wait_ge(wT_lo, k - 5)
                    for m in range(KT):
                        for e in range(KT):
                            last = nc.tensor.transpose(ps[:, 6 + k % 2, m * D + e * P:m * D + (e + 1) * P],
                                                       w_raw[:, k, e, m * P:(m + 1) * P], keep["ident"][:])
                    last.then_inc(wT_in_psum, 1)

                for k in (WK, WV, WQ):
                    weight_transpose(k)
                pe.wait_ge(xT_dve, 2)
                pe.wait_ge(xT_act, 2)
                pe.wait_ge(wT_act, 3)
                for u in range(4):
                    h, e = divmod(u, KT)
                    bank = 3 * (u % 2)
                    if u >= 2:
                        pe.wait_ge(relus, 4 * (u - 1))
                        pe.wait_ge(v_used, u - 1)
                    for n, k in enumerate((WK, WQ, WV)):
                        for m in range(KT):
                            last = nc.tensor.matmul(ps[:, bank + n, 0:HALF], wT[:, k, m, e * P:(e + 1) * P],
                                                    xT[:, m, h * HALF:(h + 1) * HALF], start=m == 0, stop=m == KT - 1)
                        last.then_inc(qkv_in_psum, 1)
                    if u == 0:
                        weight_transpose(WO)
                        weight_transpose(XK)
                    if u == 1:
                        weight_transpose(XV)
                pe.wait_ge(identb_ready, 1)
                pe.wait_ge(wq_int_ready, 1)
                pe.wait_ge(wT_lo, 1)
                for m in range(KT):
                    for e in range(KT):
                        last = nc.tensor.transpose(psb[:, 6, m * D + e * P:m * D + (e + 1) * P],
                                                   wq_int[:, e, m * P:(m + 1) * P], keep["ident_b"][:])
                last.then_inc(wqT_in_psum, 1)
                pe.wait_ge(diag_ready, KT)
                pe.wait_ge(dve_const, 2)
                pe.wait_ge(wT_lo, 2)
                for e in range(KT):
                    last = nc.tensor.matmul(ps[0:TT, 7, e * P:(e + 1) * P], ones[:], diag[:, e], start=True, stop=True)
                last.then_inc(row_in_psum, 1)
                for h in range(2):
                    pe.wait_ge(context_ready, KT * (h + 1))
                    if h == 0:
                        pe.wait_ge(relus, 16)
                        pe.wait_ge(v_used, 4)
                    for i in range(h * HT, (h + 1) * HT):
                        for m in range(KT):
                            last = nc.tensor.matmul(ps[0:TT, i // 2, (i % 2) * D:(i % 2 + 1) * D],
                                                    context[:, m, i * TT:(i + 1) * TT], wT[:, WO, m], start=m == 0, stop=m == KT - 1)
                        if i % 2:
                            last.then_inc(attn_in_psum, 1)
                for h in range(2):
                    for j in range(HT):
                        i = h * HT + j
                        pe.wait_ge(x_int_ready, i + 1)
                        for m in range(KT):
                            last = nc.tensor.transpose(psb[:, 4 + h, m * HALF + j * TT:m * HALF + (j + 1) * TT],
                                                       x_int[:, i, m * P:(m + 1) * P], keep["ident_b"][0:TT, 0:TT])
                    last.then_inc(x_intT_in_psum, 1)
                    pe.wait_ge(wqT_ready, 1)
                    pe.wait_ge(x_intT_ready, h + 1)
                    for i in range(h * HT, (h + 1) * HT):
                        if i % 2 == 0:
                            pe.wait_ge(resid_ready, i + 2)
                        for m in range(KT):
                            last = nc.tensor.matmul(ps[0:TT, i // 2, (i % 2) * D:(i % 2 + 1) * D],
                                                    x_intT[:, m, i * TT:(i + 1) * TT], wq_intT[:, m], start=m == 0, stop=m == KT - 1)
                        if i % 2:
                            last.then_inc(q_in_psum, 1)
                pe.wait_ge(row_ready, 1)
                pe.wait_ge(x_intT_ready, 2)
                for h in range(2):
                    pe.wait_ge(query_ready, (h + 1) * HT)
                    for m in range(KT):
                        for j in range(HT):
                            last = nc.tensor.transpose(ps[:, 4 + 2 * m + h, j * TT:(j + 1) * TT],
                                                       query[:, h * HT + j, m * P:(m + 1) * P], keep["ident"][0:TT, 0:TT])
                        last.then_inc(qT_in_psum, 1)

            @block.scalar
            def _(act):
                for n, name in enumerate(["L0_attn_bk", "L0_attn_bq", "L0_attn_bv"]):
                    act.dma_start(qkv_bias[:, n], column(io[name]), allow_slow_non_contiguous=True).then_inc(bias_in, 16)
                act.dma_start(keep["xbk"][:], column(io["L0_xattn_bk"]), allow_slow_non_contiguous=True).then_inc(bias_in, 16)
                act.dma_start(bo_row[:], row(io["L0_attn_bo"], TT)).then_inc(row_in, 16)
                act.dma_start(xbq_row[:], row(io["L0_xattn_bq"], TT)).then_inc(row_in, 16)
                act.wait_ge(bias_in, 64)
                act.wait_ge(row_in, 32)
                act.wait_ge(ident_ready, 1)
                nc.scalar.activation(keep["ident_b"][:], keep["ident"][:], ACT.Copy).then_inc(identb_ready, 1)
                nc.scalar.activation(neg_bias[:], qkv_bias[:], ACT.Copy, scale=-1.0).then_inc(identb_ready, 1)
                for n in (1, 3):
                    act.wait_ge(xT_in_psum, n + 1)
                    nc.scalar.activation(xT[:, n // 2, HALF:T], ps[:, n, 0:HALF], ACT.Copy).then_inc(xT_act, 1)

                def weight_out(k):
                    act.wait_ge(wT_in_psum, k + 1)
                    src = ps[:, 6 + k % 2]
                    if k < XK:
                        dst = wT[:, k]
                    else:
                        dst = keep["wkvT"][:, 0 if k == XK else 2]
                    nc.scalar.activation(dst, split(src, KT), ACT.Copy).then_inc(wT_act, 1)

                for k in (WK, WV, WQ):
                    weight_out(k)
                act.wait_ge(identb_ready, 2)
                for u in range(4):
                    h, e = divmod(u, KT)
                    for n in range(2):
                        act.wait_ge(qkv_in_psum, 3 * u + n + 1)
                        src = ps[:, 3 * (u % 2) + n, 0:HALF]
                        nc.scalar.activation(relu_neg[:, u, n], src, ACT.Relu, scale=-1.0,
                                             bias=neg_bias[:, n, e:e + 1]).then_inc(relus, 1)
                        nc.scalar.activation(relu_pos[:, u, n], src, ACT.Relu,
                                             bias=qkv_bias[:, n, e:e + 1]).then_inc(relus, 1)
                    act.wait_ge(relus, 4 * u + 4)
                    nc.scalar.activation(relu_neg[:, u], relu_neg[:, u], ACT.Exp, scale=-1.0).then_inc(exps, 1)
                    if u == 0:
                        weight_out(WO)
                        weight_out(XK)
                    if u == 1:
                        weight_out(XV)
                act.wait_ge(wqT_in_psum, 1)
                nc.scalar.activation(wq_intT[:], split(psb[:, 6, 0:KT * D], KT), ACT.Copy).then_inc(wqT_ready, 1)
                act.wait_ge(row_in_psum, 1)
                nc.scalar.activation(wq_scale_row[:], ps[0:TT, 7, 0:D], ACT.Copy, scale=SCALE).then_inc(row_ready, 1)
                act.wait_ge(mask_ready, 1)
                for n in range(4):
                    m, h = n % 2, n // 2
                    act.wait_ge(qT_in_psum, n + 1)
                    for e in range(2):
                        nc.scalar.activation(qbd_hi[:, m, batches(h), e], qT(m, h), ACT.Identity, scale=head_mask[:, e:e + 1]).then_inc(qbd_hi_ready, 1)

            @block.vector
            def _(dve):
                nc.vector.memset(keep_going[:], 1.0).then_inc(dve_const, 1)
                nc.vector.memset(ones[:], 1.0).then_inc(dve_const, 1)
                dve.wait_ge(dve_const, 1)
                nc.vector.memset(keep_going[:].rearrange("p (b s) -> p b s", s=S)[:, :, 0:1], 0.0).then_inc(dve_const, 1)
                dve.wait_ge(head_of_ready, 2)
                nc.vector.tensor_reduce(head_mask[:], head_of[:].rearrange("p (k e) -> p e k", e=2), AX.X, ALU.add).then_inc(mask_ready, 1)
                for n in (0, 2):
                    dve.wait_ge(xT_in_psum, n + 1)
                    nc.vector.tensor_copy(xT[:, n // 2, 0:HALF], ps[:, n, 0:HALF]).then_inc(xT_dve, 1)
                dve.wait_ge(w_in[XQ], 16)
                nc.vector.tensor_reduce(wq_scale[:], w_raw[:, XQ], AX.X, ALU.max, apply_absolute_value=True).then_inc(wq_steps, 1)
                dve.wait_ge(wq_steps, 1)
                nc.vector.tensor_scalar(wq_scale[:], wq_scale[:], 1.0 / QMAX, QEPS, ALU.mult, ALU.max).then_inc(wq_steps, 1)
                dve.wait_ge(wq_steps, 2)
                nc.vector.reciprocal(wq_inv[:], wq_scale[:]).then_inc(wq_steps, 1)
                dve.wait_ge(ident_ready, 1)
                for e in range(KT):
                    nc.vector.tensor_scalar(diag[:, e], keep["ident"][:], wq_scale[:, e:e + 1], None, ALU.mult).then_inc(diag_ready, 1)
                dve.wait_ge(wq_steps, 3)
                for e in range(KT):
                    nc.vector.tensor_scalar(wq_tmp[:, e], w_raw[:, XQ, e], wq_inv[:, e:e + 1], ROUND, ALU.mult, ALU.add).then_inc(wq_steps, 1)
                dve.wait_ge(wq_steps, 5)
                nc.vector.tensor_scalar(wq_tmp[:], wq_tmp[:], ROUND, QMAX, ALU.subtract, ALU.min).then_inc(wq_steps, 1)
                dve.wait_ge(wq_steps, 6)
                nc.vector.tensor_scalar(wq_int[:], wq_tmp[:], -QMAX, None, ALU.max).then_inc(wq_int_ready, 1)
                dve.wait_ge(bias_in, 64)
                dve.wait_ge(row_in, 32)
                dve.wait_ge(dve_const, 3)
                dve.wait_ge(xT_in_psum, 4)
                nc.vector.tensor_tensor(x_sb[:], x_sb[:], bo_row[:].unsqueeze(1).broadcast_to([TT, NT, D]), ALU.add).then_inc(xbo_ready, 1)
                nc.vector.tensor_scalar(xbq_row[:], xbq_row[:], SCALE, None, ALU.mult).then_inc(xbo_ready, 1)

                def weight_lo(k):
                    dve.wait_ge(wT_act, k + 1)
                    hi = keep["wkvT"][:, 0 if k == XK else 2]
                    lo = keep["wkvT"][:, 1 if k == XK else 3]
                    nc.vector.tensor_tensor(lo[:], split(ps[:, 6 + k % 2], KT), hi[:].bitcast(F32), ALU.subtract).then_inc(wT_lo, 1)

                for u in range(4):
                    h, e = divmod(u, KT)
                    dve.wait_ge(exps, u + 1)
                    nc.vector.tensor_tensor(phi[:, u], relu_pos[:, u], relu_neg[:, u], ALU.add).then_inc(phis, 1)
                    dve.wait_ge(phis, u + 1)
                    dve.wait_ge(qkv_in_psum, 3 * u + 3)
                    nc.vector.scalar_tensor_tensor(out=kv[:, u], in0=ps[:, 3 * (u % 2) + 2, 0:HALF], scalar=qkv_bias[:, 2, e:e + 1],
                                                   in1=phi[:, u, 0], op0=ALU.add, op1=ALU.mult).then_inc(v_used, 1)
                    dve.wait_ge(v_used, u + 1)
                    nc.vector.tensor_tensor_scan(kv_sum[:, u], keep_going[:], kv[:, u], 0.0, ALU.mult, ALU.add).then_inc(scanned, 1)
                    dve.wait_ge(scanned, u + 1)
                    nc.vector.scalar_tensor_tensor(out=context[:, e, h * HALF:(h + 1) * HALF], in0=kv_sum[:, u], scalar=SCALE,
                                                   in1=phi[:, u, 1], op0=ALU.mult, op1=ALU.mult).then_inc(context_ready, 1)
                    if u == 1:
                        weight_lo(XK)
                    if u == 2:
                        weight_lo(XV)
                dve.wait_ge(xbo_ready, 2)
                for h in range(2):
                    for i in range(h * HT, (h + 1) * HT):
                        if i % 2 == 0:
                            dve.wait_ge(attn_in_psum, i // 2 + 1)
                        nc.vector.tensor_tensor(resid[:, i], ps[0:TT, i // 2, (i % 2) * D:(i % 2 + 1) * D], x_sb[:, i], ALU.add).then_inc(resid_ready, 1)
                    for i in range(h * HT, (h + 1) * HT):
                        dve.wait_ge(resid_ready, i + 1)
                        nc.vector.bn_stats(stats[:, i], resid[:, i]).then_inc(stats_ready, 1)
                    for i in range(h * HT, (h + 1) * HT):
                        dve.wait_ge(stats_ready, i + 1)
                        nc.vector.bn_aggr(mv[:, i], stats[:, i]).then_inc(mv_ready, 1)
                    g = slice(h * HT, (h + 1) * HT)
                    dve.wait_ge(mv_ready, (h + 1) * HT)
                    nc.vector.tensor_scalar(var_eps[:, g], mv[:, g, 1], LN_EPS, None, ALU.add).then_inc(var_ready, 1)
                def scaled_query(i):
                    if i % 2 == 0:
                        dve.wait_ge(q_in_psum, i // 2 + 1)
                    nc.vector.scalar_tensor_tensor(out=q_scaled[:, i], in0=ps[0:TT, i // 2, (i % 2) * D:(i % 2 + 1) * D],
                                                   scalar=x_scale[:, i:i + 1], in1=wq_scale_row[:], op0=ALU.mult, op1=ALU.mult).then_inc(q_scaled_ready, 1)

                def biased_query(h):
                    g = slice(h * HT, (h + 1) * HT)
                    dve.wait_ge(q_scaled_ready, (h + 1) * HT)
                    nc.vector.tensor_tensor(query[:, g], q_scaled[:, g], xbq_row[:].unsqueeze(1).broadcast_to([TT, HT, D]), ALU.add).then_inc(query_ready, HT)

                for i in range(HT + 1):
                    if i % HT == 0:
                        dve.wait_ge(rstd_ready, i // HT + 1)
                    nc.vector.tensor_scalar(keep["x1"][:, i], resid[:, i], mv[:, i, 0:1], rstd[:, i:i + 1],
                                            ALU.subtract, ALU.mult).then_inc(x1_ready, 1)
                for h in range(2):
                    g = slice(h * HT, (h + 1) * HT)
                    dve.wait_ge(x1_ready, HT + h)
                    if h == 1:
                        dve.wait_ge(x1_pool, HT - 1)
                    nc.vector.tensor_reduce(x_scale[:, g], keep["x1"][:, g], AX.X, ALU.max, apply_absolute_value=True).then_inc(x_steps, 1)
                    dve.wait_ge(x_steps, 4 * h + 1)
                    nc.vector.tensor_scalar(x_scale[:, g], x_scale[:, g], 1.0 / QMAX, QEPS, ALU.mult, ALU.max).then_inc(x_steps, 1)
                    dve.wait_ge(x_steps, 4 * h + 2)
                    nc.vector.reciprocal(x_inv[:, g], x_scale[:, g]).then_inc(x_steps, 1)
                    dve.wait_ge(x_steps, 4 * h + 3)
                    for i in range(h * HT, (h + 1) * HT):
                        ins = nc.vector.tensor_scalar(x_tmp[:, i], keep["x1"][:, i], x_inv[:, i:i + 1], ROUND, ALU.mult, ALU.add)
                    ins.then_inc(x_steps, 1)
                    dve.wait_ge(x_steps, 4 * h + 4)
                    for i in range(h * HT, (h + 1) * HT):
                        nc.vector.tensor_scalar(x_int[:, i], x_tmp[:, i], ROUND, QMAX, ALU.subtract, ALU.min).then_inc(x_int_ready, 1)
                    if h == 1:
                        dve.wait_ge(row_ready, 1)
                        scaled_query(0)
                        scaled_query(1)
                    dve.wait_ge(x_intT_in_psum, h + 1)
                    nc.vector.tensor_scalar(x_intT[:, :, h * HALF:(h + 1) * HALF], split(psb[:, 4 + h, 0:KT * HALF], KT),
                                            -QMAX, None, ALU.max).then_inc(x_intT_ready, 1)
                scaled_query(2)
                scaled_query(3)
                biased_query(0)
                for i in range(HT, NT):
                    scaled_query(i)
                biased_query(1)
                for n in range(4):
                    m, h = n % 2, n // 2
                    dve.wait_ge(qbd_hi_ready, 2 * n + 2)
                    for e in range(2):
                        nc.vector.scalar_tensor_tensor(out=qbd_lo[:, m, batches(h), e], in0=qT(m, h), scalar=head_mask[:, e:e + 1],
                                                       in1=qbd_hi[:, m, batches(h), e].bitcast(F32), op0=ALU.mult, op1=ALU.subtract).then_inc(qbd_lo_ready, 1)


UNITS = [
    ([("X", 0, 0)], [("X", 0, 1)]),
    ([("X", 1, 0), ("V", 0, 0)], [("X", 1, 1)]),
    ([("X", 2, 0), ("K", 0, 0)], [("X", 2, 1)]),
    ([("K", 0, 1)], [("K", 0, 2)]),
    ([("V", 1, 0)], [("V", 2, 0)]),
    ([("V", 3, 0)], [("K", 1, 0)]),
    ([("K", 1, 1)], [("K", 1, 2)]),
    ([("V", 4, 0)], [("V", 5, 0)]),
]
READ = {1: (1, 1), 2: (1, 1)}
RESULT_AFTER = {3: 0, 4: 1, 6: 2, 7: 3}
UNITS_R = [(before, after + ([("R", RESULT_AFTER[t], 0)] if t in RESULT_AFTER else [])) for t, (before, after) in enumerate(UNITS)]


def ordered(units):
    return {u: n for n, u in enumerate(u for before, after in units for u in before + after)}


AT, AT_R = ordered(UNITS), ordered(UNITS_R)
FIRST = [("X", 0, 0), ("X", 0, 1), ("K", 0, 0), ("X", 1, 0), ("X", 1, 1), ("K", 0, 1), ("X", 2, 0), ("X", 2, 1), ("K", 0, 2),
         ("V", 0, 0), ("V", 1, 0), ("V", 2, 0), ("V", 3, 0), ("K", 1, 0), ("K", 1, 1), ("K", 1, 2), ("V", 4, 0), ("V", 5, 0)]
AT_FIRST = {u: n for n, u in enumerate(FIRST)}
SCORES_AFTER = {12: 0, 14: 1}
NU, NR = len(AT), len(RESULT_AFTER)
NU2 = 2 * NU + NR
UNITS_LAST = [([("T", 0, 0)], [("T", 1, 0)]), ([("L", 0, 0)], []), ([("L", 1, 0)], []), ([], []), ([], []), ([("C", 0, 0)], []), ([], []), ([], [])]
AT_LAST = ordered(UNITS_LAST)
HIDDEN = [("R", k, 0) for k in range(NR)] + [("T", 0, 0), ("T", 1, 0), ("L", 0, 0), ("L", 1, 0), ("C", 0, 0)]
HI_AT, HI_FIRST = ({u: n for n, u in enumerate(u for u in at if u[0] != "V")} for at in (AT, AT_FIRST))
NHI = len(HI_AT)
R_STEPS = 11
ROUTE_STEPS = 2 * HT + 10
NST = NS // P
CLIP = 50.0


def units_before(half, a):
    if isinstance(half, int) and half == 0:
        return NU * (1 + a)
    return half * NU2 + NU - NR + a * (NU + NR)


PREPARE_AT = {4: 1, 5: 2, 6: 3, 8: 4, 9: 5, 11: 6}
TB = 3
EST = 3
STACK = 3


def projection_room(keep):
    room, n = keep["room"], KT * L
    cT_hi, cT_lo = (split(room[:, k * n:(k + 1) * n], KT) for k in range(2))
    k_hi, k_lo = (room[:, 2 * n + k * L:2 * n + (k + 1) * L] for k in range(2))
    context = split(keep["context"][0:LT], NL)
    return cT_hi, cT_lo, k_hi, k_lo, context


def expert_room(keep):
    room = {"room": keep["room"][:], "context": keep["context"][:], "w": keep["wkvT"][:].rearrange("p k m d -> p (k m d)"),
            "v": keep["v_sb"][:, 0].rearrange("p l d -> p (l d)")}
    at = dict.fromkeys(room, 0)

    def take(which, cols, rows=P, dt=None):
        view = room[which][0:rows, at[which]:at[which] + cols]
        at[which] += cols
        return view.bitcast(dt) if dt else view

    return {
        "pick_c": split(take("room", KT * NS), KT),
        "pick_r": split(take("room", NST * D), NST),
        "c_stack": take("room", HALF, rows=EST * E),
        "idx_row": take("context", NS, dt=I32),
        "x2T_hi": split(take("w", KT * HALF), KT),
        "x2T_lo": split(take("w", KT * HALF), KT),
        "c_lo": take("v", T, rows=E, dt=F32R),
        "channel_row": take("context", D),
        "channel": take("context", KT),
        "idx_col": take("context", NST, dt=I32),
        "row_i": take("context", NST, dt=I32),
        "row_f": take("context", NST),
        "expert_row": take("context", E, rows=TT),
    }


def half_of(h):
    return slice(h * HALF, (h + 1) * HALF)


def x2T_parts(keep, h):
    if h == 0:
        e = expert_room(keep)
        return e["x2T_hi"], e["x2T_lo"]
    return keep["x2T_hi1"], keep["x2T_lo1"]


def shares_stack(keep, h):
    return expert_room(keep)["c_stack"] if h == 0 else keep["c_stack1"][:]


def load_indices(sp, io, keep):
    e = expert_room(keep)
    sp.dma_start(e["idx_col"], io["L0_ffn_mask_idx"].rearrange("(j p) -> p j", p=P),
                 allow_slow_non_contiguous=True).then_inc(keep["idx_col_in"], 16)
    sp.dma_start(e["idx_row"], io["L0_ffn_mask_idx"].unsqueeze(0).broadcast_to([P, NS])).then_inc(keep["idx_row_in"], 16)


def stack_shares(sp, keep, h, out, out_value):
    stack, c_lo = shares_stack(keep, h), expert_room(keep)["c_lo"][:, half_of(h)]
    sp.wait_ge(keep["c_hi_ready"], h + 1)
    sp.dma_start(stack[E:2 * E].bitcast(F32), stack[0:E].bitcast(F32)).then_inc(keep["c_stacked"][h], 16)
    sp.wait_ge(out, out_value)
    sp.dma_start(stack[2 * E:3 * E].bitcast(F32), c_lo.bitcast(F32)).then_inc(keep["c_stacked"][h], 16)


def result_on_gpsimd(nc, pool, keep, tile):
    pool.wait_ge(keep["var_ready"], tile + 1)
    t = slice(tile, tile + 1)
    nc.gpsimd.tensor_tensor(keep["rstd"][:, t], keep["var_eps"][:, t], keep["minus_half"][:, t], ALU.pow).then_inc(keep["rstd_ready"], 1)


def tables_on_gpsimd(nc, pool, keep):
    e = expert_room(keep)
    channels = keep["channels"]
    nc.gpsimd.iota(e["channel"], pattern=[[P, KT]], base=0, channel_multiplier=1,
                   allow_small_or_imprecise_dtypes=True).then_inc(channels, 1)
    nc.gpsimd.iota(e["channel_row"], pattern=[[1, D]], base=0, channel_multiplier=0,
                   allow_small_or_imprecise_dtypes=True).then_inc(channels, 1)
    nc.gpsimd.iota(e["expert_row"], pattern=[[1, E]], base=0, channel_multiplier=0,
                   allow_small_or_imprecise_dtypes=True).then_inc(channels, 1)


def rows_on_vector(nc, dve, keep):
    e, steps = expert_room(keep), keep["row_steps"]
    dve.wait_ge(keep["idx_col_in"], 16)
    nc.vector.tensor_single_scalar(e["row_i"], e["idx_col"], 8, ALU.arith_shift_right).then_inc(steps, 1)
    dve.wait_ge(steps, 1)
    nc.vector.tensor_copy(e["row_f"], e["row_i"]).then_inc(steps, 1)


def rows_on_gpsimd(nc, pool, keep):
    e, steps = expert_room(keep), keep["row_steps"]
    pool.wait_ge(steps, 2)
    pool.wait_ge(keep["channels"], 3)
    for j in range(NST):
        nc.gpsimd.tensor_scalar(e["pick_r"][:, j], e["channel_row"], e["row_f"][:, j:j + 1], None, ALU.is_equal).then_inc(steps, 1)


def columns_on_vector(nc, dve, keep, step):
    e, steps = expert_room(keep), keep["column_steps"]
    if step == 0:
        nc.vector.tensor_single_scalar(e["idx_row"], e["idx_row"], D - 1, ALU.bitwise_and).then_inc(steps, 1)
    else:
        dve.wait_ge(steps, 1)
        dve.wait_ge(keep["channels"], 3)
        nc.vector.tensor_scalar(e["pick_c"][:, step - 1], e["idx_row"], e["channel"][:, step - 1:step], None, ALU.is_equal).then_inc(steps, 1)


def late_unit_on_tensor(nc, keep, u, h, bank):
    kind, p, q = u
    tiles = range(h * HT, (h + 1) * HT)
    if u == ("R", 0, 0):
        for b in range(2):
            for g in range(2):
                last = nc.tensor.transpose(bank[0:PN, b * D + g * P:b * D + (g + 1) * P],
                                           keep["outT"][:, b, g * PN:(g + 1) * PN], keep["ident"][:])
    elif u == ("R", 1, 0):
        for e in range(2):
            dst = bank[0:TT, 0:D].rearrange("p (k e d) -> p k e d", k=NP, e=2)[:, :, e]
            for b in range(2):
                last = nc.tensor.matmul(dst, keep["sel"][:, 2 * e + b], keep["r_norm"][:, b * NP:(b + 1) * NP, e * DH:(e + 1) * DH],
                                        start=b == 0, stop=b == 1)
    elif u == ("R", 2, 0):
        for m in range(KT):
            last = nc.tensor.transpose(bank.bitcast(BF16)[:, m * TT:(m + 1) * TT], keep["r_int"][:, m * P:(m + 1) * P],
                                       keep["ident_b"][0:TT, 0:TT])
    elif u == ("R", 3, 0):
        for m in range(KT):
            last = nc.tensor.matmul(bank[0:TT, 0:D], keep["r_intT"][:, m], keep["wo_intT"][:, m], start=m == 0, stop=m == KT - 1)
    elif kind == "T":
        for j, i in enumerate(tiles):
            last = nc.tensor.transpose(bank[:, j * TT:(j + 1) * TT], keep["x1"][:, i, p * P:(p + 1) * P], keep["ident"][0:TT, 0:TT])
    elif u == ("L", 0, 0):
        (hi, lo), g_hi, g_lo = x2T_parts(keep, h), keep["gateT_hi"], keep["gateT_lo"]
        mm = [t for m in range(KT) for t in ((g_hi[:, m], hi[:, m]), (g_hi[:, m], lo[:, m]), (g_lo[:, m], hi[:, m]))]
        for n, (g, x) in enumerate(mm):
            last = nc.tensor.matmul(bank[0:E, 0:HALF], g, x, start=n == 0, stop=n == len(mm) - 1)
    elif u == ("L", 1, 0):
        for j in range(HT):
            last = nc.tensor.transpose(bank[0:TT, j * E:(j + 1) * E], keep["logitsT"][:, j * TT:(j + 1) * TT], keep["ident"][0:E, 0:E])
    else:
        for j in range(HT):
            last = nc.tensor.transpose(bank[0:E, j * TT:(j + 1) * TT], keep["shares"][:, j], keep["ident"][0:TT, 0:TT])
    return last


def late_unit_on_scalar(nc, keep, u, h, bank):
    if u[0] == "T":
        nc.scalar.activation(x2T_parts(keep, h)[0][:, u[1]], bank[:, 0:HALF], ACT.Copy).then_inc(keep["x2T_hi_ready"], 1)
    else:
        nc.scalar.activation(shares_stack(keep, h)[0:E], bank[0:E, 0:HALF], ACT.Copy).then_inc(keep["c_hi_ready"], 1)


def gap_on_scalar(nc, act, keep, h):
    act.wait_ge(keep["route_steps"], h * ROUTE_STEPS + HT + 1)
    nc.scalar.activation(keep["egap"][:], keep["gap"][:], ACT.Exp).then_inc(keep["egap_ready"], 1)


def late_unit_on_vector(nc, dve, keep, u, h, bank, tile, in_psum, in_value, out, out_value, read=True, chain=True):
    kind, p, q = u
    done = tile * R_STEPS
    steps = keep["r_steps"]
    k = keep
    if kind in "RL" and read:
        dve.wait_ge(in_psum, in_value)
    if not read and u in (("R", 0, 0), ("R", 2, 0)):
        return
    if u == ("R", 0, 0):
        nc.vector.reciprocal(k["rsum"][:], k["sums"][:, bass.ds(2 * tile, 2)]).then_inc(steps, 1)
        dve.wait_ge(steps, done + 1)
        nc.vector.tensor_tensor(k["r_norm"][:], bank[0:PN].rearrange("p (k d) -> p k d", d=PD),
                                k["rsum"][:].rearrange("p b k -> p (b k)").unsqueeze(2).broadcast_to([PN, 2 * NP, PD]),
                                ALU.mult).then_inc(out, 1)
    elif u == ("R", 1, 0):
        if read:
            nc.vector.tensor_tensor(k["r_sb"][:], bank[0:TT, 0:D], k["bv_row"][:], ALU.add).then_inc(out, 1)
        if not chain:
            return
        dve.wait_ge(out, out_value)
        nc.vector.tensor_reduce(k["r_scale"][:], k["r_sb"][:], AX.X, ALU.max, apply_absolute_value=True).then_inc(steps, 1)
        dve.wait_ge(steps, done + 2)
        nc.vector.tensor_scalar(k["r_scale"][:], k["r_scale"][:], 1.0 / QMAX, QEPS, ALU.mult, ALU.max).then_inc(steps, 1)
        dve.wait_ge(steps, done + 3)
        nc.vector.reciprocal(k["r_inv"][:], k["r_scale"][:]).then_inc(steps, 1)
        dve.wait_ge(steps, done + 4)
        nc.vector.tensor_scalar(k["r_tmp"][:], k["r_sb"][:], k["r_inv"][:, 0:1], ROUND, ALU.mult, ALU.add).then_inc(steps, 1)
        dve.wait_ge(steps, done + 5)
        nc.vector.tensor_scalar(k["r_int"][:], k["r_tmp"][:], ROUND, QMAX, ALU.subtract, ALU.min).then_inc(k["r_int_ready"], 1)
    elif u == ("R", 2, 0):
        nc.vector.tensor_scalar(k["r_intT"][:], split(bank.bitcast(BF16)[:, 0:KT * TT], KT), -QMAX, None, ALU.max).then_inc(out, 1)
    elif u == ("R", 3, 0):
        if read:
            nc.vector.scalar_tensor_tensor(out=k["r_tmp"][:], in0=bank[0:TT, 0:D], scalar=k["r_scale"][:, 0:1],
                                           in1=k["wo_scale_row"][:], op0=ALU.mult, op1=ALU.mult).then_inc(out, 1)
        if not chain:
            return
        dve.wait_ge(out, out_value)
        nc.vector.tensor_tensor(k["resid"][:], k["r_tmp"][:], k["x1"][:, tile], ALU.add).then_inc(steps, 1)
        dve.wait_ge(steps, done + 6)
        nc.vector.bn_stats(k["stats"][:], k["resid"][:]).then_inc(steps, 1)
        dve.wait_ge(steps, done + 7)
        nc.vector.memset(k["r_cell"][:], 0.0).then_inc(steps, 1)
        nc.vector.bn_aggr(k["mv"][:], k["stats"][:]).then_inc(steps, 1)
        dve.wait_ge(steps, done + 9)
        nc.vector.tensor_scalar(k["var_eps"][:, bass.ds(tile, 1)], k["mv"][:, 1:2], LN_EPS, None, ALU.add).then_inc(k["var_ready"], 1)
    elif kind == "T":
        dve.wait_ge(k["x2T_hi_ready"], KT * h + p + 1)
        hi, lo = x2T_parts(keep, h)
        nc.vector.tensor_tensor(lo[:, p], bank[:, 0:HALF], hi[:, p].bitcast(F32), ALU.subtract).then_inc(out, 1)
    elif u == ("L", 0, 0):
        nc.vector.tensor_copy(k["logitsT"][:], bank[0:E, 0:HALF]).then_inc(out, 1)
    elif u == ("L", 1, 0):
        nc.vector.tensor_scalar(k["logits"][:], bank[0:TT, 0:HT * E].rearrange("p (i e) -> p i e", e=E), CLIP, -CLIP, ALU.min, ALU.max).then_inc(out, 1)
        dve.wait_ge(out, out_value)
        route_on_vector(nc, dve, keep, h)
    else:
        dve.wait_ge(k["c_hi_ready"], h + 1)
        nc.vector.tensor_tensor(expert_room(k)["c_lo"][:, half_of(h)], bank[0:E, 0:HALF], shares_stack(k, h)[0:E].bitcast(F32), ALU.subtract).then_inc(out, 1)


def route_on_vector(nc, dve, keep, h):
    k, steps, first = keep, keep["route_steps"], h * ROUTE_STEPS
    for i in range(HT):
        nc.vector.max(k["top"][:, i], k["logits"][:, i]).then_inc(steps, 1)
    dve.wait_ge(steps, first + HT)
    nc.vector.tensor_tensor(k["gap"][:], k["top"][:, :, 1], k["top"][:, :, 0], ALU.subtract).then_inc(steps, 1)
    for i in range(HT):
        nc.vector.max_index(k["top_i"][:, i], k["top"][:, i], k["logits"][:, i]).then_inc(steps, 1)
    dve.wait_ge(steps, first + 2 * HT + 1)
    nc.vector.tensor_copy(k["top_f"][:], k["top_i"][:]).then_inc(steps, 1)


def shares_on_vector(nc, dve, keep, h):
    k, steps, first = keep, keep["route_steps"], h * ROUTE_STEPS + 2 * HT + 2
    route, hit, hit_w = k["route"], k["hit"], k["hit_w"]
    dve.wait_ge(k["egap_ready"], h + 1)
    nc.vector.tensor_scalar(k["den"][:], k["egap"][:], 1.0, None, ALU.add).then_inc(steps, 1)
    dve.wait_ge(steps, first + 1)
    nc.vector.reciprocal(route[:, 0], k["den"][:]).then_inc(steps, 1)
    dve.wait_ge(steps, first + 2)
    nc.vector.tensor_tensor(route[:, 1], k["egap"][:], route[:, 0], ALU.mult).then_inc(steps, 1)
    dve.wait_ge(k["channels"], 3)
    for n in range(2):
        nc.vector.tensor_tensor(hit[:, n], expert_room(k)["expert_row"].unsqueeze(1).broadcast_to([TT, HT, E]),
                                k["top_f"][:, :, n:n + 1].broadcast_to([TT, HT, E]), ALU.is_equal).then_inc(steps, 1)
    dve.wait_ge(steps, first + 5)
    for n in range(2):
        nc.vector.tensor_tensor(hit_w[:, n], hit[:, n], route[:, n].unsqueeze(2).broadcast_to([TT, HT, E]), ALU.mult).then_inc(steps, 1)
    dve.wait_ge(steps, first + 7)
    nc.vector.tensor_tensor(k["shares"][:], hit_w[:, 0], hit_w[:, 1], ALU.add).then_inc(steps, 1)


def centre(nc, dve, keep, tile):
    dve.wait_ge(keep["rstd_ready"], tile + 1)
    nc.vector.tensor_scalar(keep["x1"][:, tile], keep["resid"][:], keep["mv"][:, 0:1], keep["rstd"][:, bass.ds(tile, 1)],
                            ALU.subtract, ALU.mult).then_inc(keep["r_steps"], 2)


def cross_attention_phase(nc, io, keep):
    ctx = ExitStack()
    with ctx:
        sb = lambda n, s, d=F32: ctx.enter_context(nc.sbuf_tensor(n, s, d))
        sem = lambda n: ctx.enter_context(nc.semaphore(n))
        v_sb = keep["v_sb"]
        cT_hi, cT_lo, k_hi, k_lo, context = projection_room(keep)
        k_stack = keep["k_stack"]
        q_stack = sb("q_stack", [STACK * PD, 2, NP, PN], F32R)
        mask_sb = sb("mask_sb", [PN, 2, L])
        scores = sb("scores", [PN, 2, L])
        shift = sb("shift", [PN, 2])
        wait_cell = sb("wait_cell", [PN, 1])
        probsT = sb("probsT", [LT, 2, NL, PN])
        x1 = keep["x1"]
        room = v_sb[:, 1].rearrange("p l d -> p (l d)")
        wo_raw, w_raw, wo_tmp = (split(room[:, n * KT * D:(n + 1) * KT * D], KT) for n in range(3))
        diag = split(room[:, 3 * KT * D:3 * KT * D + KT * P], KT)
        wo_int = split(room[:, 4 * KT * D:4 * KT * D + KT * D // 2].bitcast(BF16), KT)
        ones = room[:, 5 * KT * D:5 * KT * D + TT]
        bo_row = room[0:TT, 5 * KT * D + TT:5 * KT * D + TT + D]
        importance = sb("importance", [P, E * NS // P])
        gate = probsT[0:E].rearrange("p h j n -> p (h j n)")[:, 0:NS]
        atoms = scores[0:A_ATOMS].rearrange("p h l -> p (h l)")[:, 0:NS]
        w8_lo = k_stack[0:E, NP - 2:NP].rearrange("p k l -> p (k l)")[:, 0:NS]
        wo_scale = sb("wo_scale", [P, KT])
        wo_inv = sb("wo_inv", [P, KT])
        gate_raw = sb("gate_raw", [E, D])
        atom_w = sb("atom_w", [E, A_ATOMS])
        atom_shift = sb("atom_shift", [E, 1])
        atom_sum = sb("atom_sum", [E, 1])
        atom_rsum = sb("atom_rsum", [E, 1])
        atom_p = sb("atom_p", [E, A_ATOMS])
        atom_pn = sb("atom_pn", [E, A_ATOMS])
        atom_pT = sb("atom_pT", [A_ATOMS, E])
        ps_scores = ctx.enter_context(nc.psum_tensor("ps_scores", [P, NC, 512], F32))
        ps_T = ctx.enter_context(nc.psum_tensor("ps_T", [P, 2, 512], F32))
        ps_proj = ctx.enter_context(nc.psum_tensor("ps_proj", [P, 2, 512], F32))
        psb_scores = ps_scores[:, :, :].bitcast(BF16)
        ps_out = ctx.enter_context(nc.psum_tensor("ps_out", [P, 512], F32))

        ctx_in = keep["ctx_in"]
        mask_in = [sem(f"mask_in{a}") for a in range(2)]
        q_in = [sem(f"q_in{a}") for a in range(2)]
        k_in = [sem(f"k_in{p}") for p in range(NP)]
        unit_in_psum = sem("unit_in_psum")
        hi_ready = sem("hi_ready")
        unit_out = sem("unit_out")
        scores_in_psum = sem("scores_in_psum")
        scores_ready = sem("scores_ready")
        wait_taken = sem("wait_taken")
        probs_ready = sem("probs_ready")
        probsT_in_psum = sem("probsT_in_psum")
        probsT_dve = sem("probsT_dve")
        probsT_act = sem("probsT_act")
        values_done = sem("values_done")
        out_copied = sem("out_copied")
        load = {n: sem(f"in_{n}") for n in ("wo", "w", "gate", "atom_w", "atoms", "imp", "bo", "bv")}
        ones_set = sem("ones_set")
        wo_steps = sem("wo_steps")
        wo_int_ready = sem("wo_int_ready")
        diag_ready = sem("diag_o_ready")
        W_T, GATE_T, WO_T, SCALE_ROW, ATOM_T, DELTAS = range(1, 7)
        prepared_in_psum = sem("prepared_in_psum")
        prepared_out = sem("prepared_out")
        wT_lo_ready = sem("wfT_lo_ready")
        atom_steps = sem("atom_steps")
        atom_exp = sem("atom_exp")
        gate_exp = sem("gate_exp")
        gate_steps = sem("gate_steps")
        gate_stored = sem("gate_stored")
        gate_in = sem("gate_in")
        w8_hi_ready = sem("w8_hi_ready")
        w8_lo_ready = sem("w8_lo_ready")
        w_stacked = sem("w_stacked")
        x1_bo_ready = sem("x1_bo_ready")

        last = B // 2 - 1

        def q_rows(src, b):
            return src[:, :, b].rearrange("m (k r) n -> r (m k) n", r=PD)

        with nc.Block() as block:

            @block.sync
            def _(sp):
                def load_mask(b, a):
                    for e in range(2):
                        sp.dma_start(mask_sb[e * S:(e + 1) * S, a], io["mask"][b]).then_inc(mask_in[a], 16)

                def load_q(b, a):
                    for g, src in enumerate(("q_hi", "q_lo", "q_hi")):
                        sp.dma_start(q_stack[g * PD:(g + 1) * PD, a].bitcast(F32), q_rows(io[src], b)).then_inc(q_in[a], 16)

                def wide(ap):
                    return ap.rearrange("e (a c) -> (e a) c", c=E * NS // P)

                def load_weights():
                    rows = lambda w: w.rearrange("(k p) d -> p k d", p=P)
                    row = lambda v: v.unsqueeze(0).broadcast_to([TT, D])
                    sp.dma_start(wo_raw, rows(io["L0_xattn_wo"])).then_inc(load["wo"], 16)
                    sp.dma_start(w_raw, rows(io["L0_ffn_W"])).then_inc(load["w"], 16)
                    sp.dma_start(gate_raw[:], io["L0_ffn_gate_w"]).then_inc(load["gate"], 16)
                    sp.dma_start(atom_w[:], io["L0_ffn_expert_atom_weights"]).then_inc(load["atom_w"], 16)
                    sp.dma_start(importance[:], wide(io["L0_ffn_importance"])).then_inc(load["imp"], 16)
                    sp.dma_start(atoms, io["L0_ffn_atoms"]).then_inc(load["atoms"], 16)
                    sp.dma_start(bo_row, row(io["L0_xattn_bo"])).then_inc(load["bo"], 16)
                    sp.dma_start(keep["bv_row"][:], row(io["L0_xattn_bv"])).then_inc(load["bv"], 16)

                def k_out(first, at, m):
                    return first + at[("K", m, NC - 1)] + 1 + 2

                def stack_k(m):
                    for k in range(GP):
                        rows = slice(k * PD, (k + 1) * PD)
                        for g, src in enumerate((k_hi, k_hi, k_lo)):
                            sp.dma_start(k_stack[g * PD:(g + 1) * PD, m * GP + k].bitcast(F32), src[rows].bitcast(F32)).then_inc(k_in[m * GP + k], 16)

                def batch(b, half, a, at, project, load):
                    if project:
                        first = units_before(half, a)
                        if not load:
                            sp.wait_ge(unit_in_psum, first + at[("X", NC - 1, 1)] + 1)
                            load_indices(sp, io, keep)
                        for c in range(NC):
                            if load:
                                sp.wait_ge(unit_in_psum, first + at[("X", c, 1)] + 1)
                                load_chunk(sp, io, keep, b + 2, c)
                        sp.wait_ge(unit_out, k_out(first, at, 0))
                        stack_k(0)
                        if load:
                            sp.wait_ge(scores_ready, (b + 1) * NP)
                            load_mask(b + 2, a)
                            load_q(b + 2, a)
                        sp.wait_ge(unit_out, k_out(first, at, 1))
                        stack_k(1)

                load_weights()
                sp.wait_ge(keep["q_stored"], 16 * 4 * KT)
                for a in range(2):
                    load_q(a, a)
                    load_mask(a, a)
                for c in range(NC):
                    sp.wait_ge(unit_in_psum, AT_FIRST[("X", c, 1)] + 1)
                    load_chunk(sp, io, keep, 1, c)
                sp.wait_ge(gate_steps, 2)
                sp.dma_start(wide(io["gate"]), importance[:]).then_inc(gate_stored, 16)
                sp.wait_ge(gate_stored, 16)
                sp.dma_start(gate, io["gate"]).then_inc(gate_in, 16)
                sp.wait_ge(unit_out, k_out(0, AT_FIRST, 0))
                stack_k(0)
                sp.wait_ge(w8_lo_ready, 1)
                w_stack = keep["w_stack"]
                sp.dma_start(w_stack[E:2 * E].bitcast(F32), w8_lo.bitcast(F32)).then_inc(w_stacked, 16)
                sp.dma_start(w_stack[2 * E:3 * E].bitcast(F32), w_stack[0:E].bitcast(F32)).then_inc(w_stacked, 16)
                sp.wait_ge(w_stacked, 32)
                sp.wait_ge(unit_out, k_out(0, AT_FIRST, 1))
                stack_k(1)
                for a in range(2):
                    batch(a, 0, a, AT, True, True)
                with sp.Fori(1, B // 2 - 1) as i:
                    for a in range(2):
                        batch(2 * i + a, i, a, AT if a else AT_R, True, True)
                batch(B - 2, B // 2 - 1, 0, AT_R, True, False)
                stack_shares(sp, keep, 0, unit_out, units_before(last, 1) + AT_LAST[("C", 0, 0)] + 1 + 2)

            @block.gpsimd
            def _(pool):
                pool.wait_ge(load["bo"], 16)
                nc.gpsimd.tensor_tensor(x1[:], x1[:], bo_row.unsqueeze(1).broadcast_to([TT, NT, D]), ALU.add).then_inc(x1_bo_ready, 1)
                nc.gpsimd.memset(keep["minus_half"][:], -0.5).then_inc(keep["half_set"], 1)
                pool.wait_ge(keep["half_set"], 1)
                for i in range(NT - 2):
                    result_on_gpsimd(nc, pool, keep, i)
                pool.wait_ge(unit_in_psum, units_before(last, 0) + AT_R[("X", NC - 1, 1)] + 1)
                tables_on_gpsimd(nc, pool, keep)
                result_on_gpsimd(nc, pool, keep, NT - 2)
                for p in range(NP):
                    pool.wait_ge(k_in[p], 16 * STACK * B)
                rows_on_gpsimd(nc, pool, keep)

            @block.tensor
            def _(pe):
                def terms(w_hi, w_lo, x_hi, x_lo):
                    return ((w_hi, x_hi), (w_hi, x_lo), (w_lo, x_hi))

                def unit(first, at, n, u, a):
                    kind, p, q = u
                    bank = at[u] % 2
                    pe.wait_ge(unit_out, first + at[u] + 1)
                    if kind in "RTLC":
                        if kind == "R" and p == 2:
                            pe.wait_ge(keep["r_int_ready"], n)
                        if kind == "R" and p in (1, 3):
                            pe.wait_ge(unit_out, first + at[("R", p - 1, 0)] + 1 + 2)
                        if kind == "L":
                            before = ("L", 0, 0) if p else ("T", 1, 0)
                            pe.wait_ge(unit_out, first + at[before] + 1 + 2)
                        if kind == "C":
                            pe.wait_ge(keep["route_steps"], ROUTE_STEPS)
                        late_unit_on_tensor(nc, keep, u, 0, ps_proj[:, bank]).then_inc(unit_in_psum, 1)
                        return
                    if kind == "X":
                        if q == 0:
                            pe.wait_ge(ctx_in[p], 16 * (n + 1))
                        for j in range(TC):
                            last = nc.tensor.transpose(ps_proj[:, bank, j * LT:(j + 1) * LT],
                                                       context[:, p * TC + j, q * P:(q + 1) * P], keep["ident"][0:LT, 0:LT])
                    elif kind == "K":
                        pe.wait_ge(unit_out, first + at[("X", q, 1)] + 1 + 2)
                        c, e = slice(q * LC, (q + 1) * LC), slice(p * P, (p + 1) * P)
                        mm = [t for m in range(KT) for t in terms(keep["wkvT"][:, 0, m, e], keep["wkvT"][:, 1, m, e],
                                                                  cT_hi[:, m, c], cT_lo[:, m, c])]
                        for i, (w, x) in enumerate(mm):
                            last = nc.tensor.matmul(ps_proj[:, bank, 0:LC], w, x, start=i == 0, stop=i == len(mm) - 1)
                    else:
                        pe.wait_ge(unit_out, first + at[("X", (2 * p + 1) // TC, 1)] + 1 + 2)
                        for j in range(2):
                            c = slice((2 * p + j) * LT, (2 * p + j + 1) * LT)
                            mm = [t for m in range(KT) for t in terms(cT_hi[:, m, c], cT_lo[:, m, c],
                                                                      keep["wkvT"][:, 2, m], keep["wkvT"][:, 3, m])]
                            for i, (w, x) in enumerate(mm):
                                last = nc.tensor.matmul(ps_proj[0:LT, bank, j * D:(j + 1) * D], w, x, start=i == 0, stop=i == len(mm) - 1)
                    last.then_inc(unit_in_psum, 1)


                def scores_of(b, half, a, t, before):
                    if t == 0:
                        pe.wait_ge(q_in[a], 16 * STACK * (half + 1))
                    pe.wait_ge(k_in[t], 16 * STACK * (b + 1))
                    if before:
                        pe.wait_ge(scores_ready, b * NP + t)
                    for c in range(NC):
                        last = nc.tensor.matmul(ps_scores[0:PN, c, 0:LC], q_stack[:, a, t], k_stack[0:STACK * PD, t, c * LC:(c + 1) * LC],
                                                start=True, stop=True)
                        if c == 0 and not before:
                            last.then_inc(values_done, 2)
                    last.then_inc(scores_in_psum, 1)

                def transposes(b, t, k):
                    if k == 0:
                        pe.wait_ge(probs_ready, b * NP + t + 1)
                    if k < 2:
                        pe.wait_ge(probsT_act, 2 * (b * NP + t) + k + 1)
                    else:
                        pe.wait_ge(probsT_dve, b * NP + t + 1)
                    for j in range(TC):
                        last = nc.tensor.transpose(ps_T[0:LT, (TB * t + k) % 2, j * PN:(j + 1) * PN],
                                                   scores[:, t % 2, (k * TC + j) * LT:(k * TC + j + 1) * LT], keep["ident"][0:PN, 0:PN])
                    last.then_inc(probsT_in_psum, 1)

                def values(b, half, a, t, tiles):
                    g, k = divmod(t, GP)
                    for j in tiles:
                        if j == 0:
                            pe.wait_ge(probsT_dve, b * NP + t + 1)
                            if t == 0:
                                pe.wait_ge(out_copied, b + 1)
                                pe.wait_ge(unit_out, units_before(half, a) + 2)
                        if j == TC:
                            pe.wait_ge(probsT_act, 2 * (b * NP + t) + 1 + 2)
                        if j == 2 * TC:
                            pe.wait_ge(probsT_act, 2 * (b * NP + t) + 2 + 2)
                        last = nc.tensor.matmul(ps_out[k * PD:(k + 1) * PD, g * PN:(g + 1) * PN], v_sb[0:LT, a, j, t * PD:(t + 1) * PD],
                                                probsT[:, t % 2, j], start=j == 0, stop=j == NL - 1)
                    if j == NL - 1:
                        last.then_inc(values_done, 1)

                def batch(b, half, a, slots, at):
                    project = at is not AT_LAST
                    for t in range(NP):
                        transposes(b, t, 0)
                        transposes(b, t, 1)
                        if t + 2 < NP:
                            scores_of(b, half, a, t + 2, True)
                        elif project:
                            scores_of(b + 1, half + a, 1 - a, t + 2 - NP, True)
                        transposes(b, t, 2)
                        before, after = slots[t]
                        for u in before:
                            unit(units_before(half, a), at, half if u[0] == "R" else b + 1, u, 1 - a)
                        values(b, half, a, t, range(NL))
                        for u in after:
                            unit(units_before(half, a), at, half if u[0] == "R" else b + 1, u, 1 - a)

                def prepare(n):
                    if n == 1:
                        pe.wait_ge(load["w"], 16)
                        for m in range(KT):
                            for e in range(KT):
                                last = nc.tensor.transpose(ps_scores[:, 0, m * D + e * P:m * D + (e + 1) * P], w_raw[:, e, m * P:(m + 1) * P], keep["ident"][:])
                        last.then_inc(prepared_in_psum, 1)
                        pe.wait_ge(load["gate"], 16)
                        for m in range(KT):
                            last = nc.tensor.transpose(ps_out[:, m * E:(m + 1) * E], gate_raw[:, m * P:(m + 1) * P], keep["ident"][0:E, 0:E])
                        last.then_inc(prepared_in_psum, 1)
                    if n == 2:
                        pe.wait_ge(wo_int_ready, 1)
                        for m in range(KT):
                            for e in range(KT):
                                last = nc.tensor.transpose(psb_scores[:, 1, m * D + e * P:m * D + (e + 1) * P], wo_int[:, e, m * P:(m + 1) * P], keep["ident_b"][:])
                        last.then_inc(prepared_in_psum, 1)
                        pe.wait_ge(ones_set, 1)
                        pe.wait_ge(diag_ready, KT)
                        for e in range(KT):
                            last = nc.tensor.matmul(ps_scores[0:TT, 2, e * P:(e + 1) * P], ones, diag[:, e], start=True, stop=True)
                        last.then_inc(prepared_in_psum, 1)
                    if n == 3:
                        pe.wait_ge(atom_steps, 3)
                        pe.wait_ge(wT_lo_ready, 2)
                        nc.tensor.transpose(ps_out[0:A_ATOMS, 0:E], atom_pn[:], keep["ident"][0:E, 0:E]).then_inc(prepared_in_psum, 1)
                    if n == 4:
                        pe.wait_ge(prepared_out, ATOM_T)
                        pe.wait_ge(wT_lo_ready, 2)
                        pe.wait_ge(load["atoms"], 16)
                        for c in range(NS // 512):
                            dst = ps_scores[0:E, c] if c < NC else ps_T[0:E, 0]
                            last = nc.tensor.matmul(dst, atom_pT[:], atoms[:, c * 512:(c + 1) * 512], start=True, stop=True)
                        last.then_inc(prepared_in_psum, 1)

                for n, u in enumerate(FIRST):
                    unit(0, AT_FIRST, 0, u, 0)
                    prepare(PREPARE_AT.get(n, 0))
                    if n in SCORES_AFTER:
                        pe.wait_ge(gate_steps, 4)
                        scores_of(0, 0, 0, SCORES_AFTER[n], SCORES_AFTER[n] > 0)
                for a in range(2):
                    batch(a, 0, a, UNITS, AT)
                with pe.Fori(1, B // 2 - 1) as i:
                    batch(2 * i, i, 0, UNITS_R, AT_R)
                    batch(2 * i + 1, i, 1, UNITS, AT)
                batch(B - 2, B // 2 - 1, 0, UNITS_R, AT_R)
                batch(B - 1, B // 2 - 1, 1, UNITS_LAST, AT_LAST)

            @block.scalar
            def _(act):
                def unit_hi(first, at, n, u):
                    kind, p, q = u
                    if kind in "VRL":
                        return
                    act.wait_ge(unit_in_psum, first + at[u] + 1)
                    if kind in "TC":
                        return late_unit_on_scalar(nc, keep, u, 0, ps_proj[:, at[u] % 2])
                    src = ps_proj[:, at[u] % 2, 0:LC]
                    if kind == "X":
                        nc.scalar.activation(cT_hi[:, q, p * LC:(p + 1) * LC], src, ACT.Copy).then_inc(hi_ready, 1)
                    else:
                        if q == 0:
                            for k in range(GP):
                                done = n * 16 * STACK if p == 0 else (n + 1) * 16 * STACK
                                other = (1 - p) * GP + k
                                if p == 1 or not isinstance(n, int) or n > 0:
                                    act.wait_ge(k_in[other], done)
                        nc.scalar.activation(k_hi[:, q * LC:(q + 1) * LC], src, ACT.Identity,
                                             bias=keep["xbk"][:, p:p + 1]).then_inc(hi_ready, 1)

                def exponentials(b, t):
                    act.wait_ge(scores_ready, b * NP + t + 1)
                    nc.scalar.activation(scores[:, t % 2], scores[:, t % 2], ACT.Exp, scale=-1.0, bias=shift[:, t % 2:t % 2 + 1],
                                         accum_out=keep["sums"][:, b, t:t + 1]).then_inc(probs_ready, 1)

                def batch(b, half, a, slots, at):
                    project = at is not AT_LAST
                    for t in range(NP):
                        act.wait_ge(values_done, b * NP + t + 1)
                        for k in (1, 2):
                            act.wait_ge(probsT_in_psum, TB * (b * NP + t) + k + 1)
                            nc.scalar.activation(probsT[:, t % 2, k * TC:(k + 1) * TC],
                                                 ps_T[0:LT, (TB * t + k) % 2, 0:TC * PN].rearrange("p (j n) -> p j n", j=TC),
                                                 ACT.Copy).then_inc(probsT_act, 1)
                        units = slots[t][0] + slots[t][1]
                        before = len(units) if READ.get(t, (0, 1))[0] else len(slots[t][0])
                        for u in units[:before]:
                            unit_hi(units_before(half, a), at, b + 1, u)
                        if t + 2 < NP:
                            exponentials(b, t + 2)
                        elif project:
                            exponentials(b + 1, t + 2 - NP)
                        for u in units[before:]:
                            unit_hi(units_before(half, a), at, b + 1, u)
                        if at is AT_LAST and t == 2:
                            gap_on_scalar(nc, act, keep, 0)
                    act.wait_ge(values_done, (b + 1) * NP + 2)
                    nc.scalar.activation(keep["outT"][:, a], ps_out[:, 0:2 * PN], ACT.Copy).then_inc(out_copied, 1)

                nc.scalar.activation(keep["credit"][:, 1:2], keep["ident"][:, 0:1], ACT.Copy).then_inc(probsT_act, 2)
                nc.scalar.activation(keep["credit"][:, 2:3], keep["ident"][:, 0:1], ACT.Copy).then_inc(out_copied, 1)

                def prepare(n):
                    if n == 1:
                        act.wait_ge(prepared_in_psum, W_T)
                        nc.scalar.activation(keep["wT_hi"][:], split(ps_scores[:, 0], KT), ACT.Copy).then_inc(prepared_out, 1)
                        act.wait_ge(prepared_in_psum, GATE_T)
                        nc.scalar.activation(keep["gateT_hi"][:], split(ps_out[:, 0:KT * E], KT), ACT.Copy).then_inc(prepared_out, 1)
                        act.wait_ge(atom_steps, 1)
                        nc.scalar.activation(atom_p[:], atom_w[:], ACT.Exp, bias=atom_shift[:, 0:1], accum_out=atom_sum[:, 0:1]).then_inc(atom_exp, 1)
                        act.wait_ge(load["imp"], 16)
                        nc.scalar.activation(importance[:], importance[:], ACT.Exp, scale=-1.0).then_inc(gate_exp, 1)
                    if n == 2:
                        act.wait_ge(prepared_in_psum, WO_T)
                        nc.scalar.activation(keep["wo_intT"][:], split(psb_scores[:, 1, 0:KT * D], KT), ACT.Copy).then_inc(prepared_out, 1)
                        act.wait_ge(prepared_in_psum, SCALE_ROW)
                        nc.scalar.activation(keep["wo_scale_row"][:], ps_scores[0:TT, 2, 0:D], ACT.Copy).then_inc(prepared_out, 1)
                    if n == 3:
                        act.wait_ge(prepared_in_psum, ATOM_T)
                        nc.scalar.activation(atom_pT[:], ps_out[0:A_ATOMS, 0:E], ACT.Copy).then_inc(prepared_out, 1)
                    if n == 5:
                        act.wait_ge(gate_steps, 4)
                        nc.scalar.activation(keep["w_stack"][0:E], gate, ACT.Copy).then_inc(w8_hi_ready, 1)

                for n, u in enumerate(FIRST):
                    unit_hi(0, AT_FIRST, 0, u)
                    prepare(PREPARE_AT.get(n, 0))
                exponentials(0, 0)
                exponentials(0, 1)
                for a in range(2):
                    batch(a, 0, a, UNITS, AT)
                with act.Fori(1, B // 2 - 1) as i:
                    batch(2 * i, i, 0, UNITS_R, AT_R)
                    batch(2 * i + 1, i, 1, UNITS, AT)
                batch(B - 2, B // 2 - 1, 0, UNITS_R, AT_R)
                batch(B - 1, B // 2 - 1, 1, UNITS_LAST, AT_LAST)

            @block.vector
            def _(dve):
                def unit_rest(first, at, n, u, a, out=True, chain=True):
                    kind, p, q = u
                    bank = at[u] % 2
                    if kind != "R" and not out:
                        return
                    if kind in "RTLC":
                        late_unit_on_vector(nc, dve, keep, u, 0, ps_proj[:, bank], n, unit_in_psum, first + at[u] + 1,
                                            unit_out, first + at[u] + 1 + 2, out, chain)
                        return
                    if kind == "V":
                        dve.wait_ge(unit_in_psum, first + at[u] + 1)
                        nc.vector.tensor_copy(v_sb[0:LT, a, 2 * p:2 * p + 2], split(ps_proj[0:LT, bank], 2)).then_inc(unit_out, 1)
                        return
                    dve.wait_ge(hi_ready, n * NHI + (HI_FIRST if at is AT_FIRST else HI_AT)[u] + 1)
                    if kind == "X":
                        c = slice(p * LC, (p + 1) * LC)
                        nc.vector.tensor_tensor(cT_lo[:, q, c], ps_proj[:, bank, 0:LC], cT_hi[:, q, c].bitcast(F32),
                                                ALU.subtract).then_inc(unit_out, 1)
                    else:
                        c = slice(q * LC, (q + 1) * LC)
                        nc.vector.scalar_tensor_tensor(out=k_lo[:, c], in0=ps_proj[:, bank, 0:LC], scalar=keep["xbk"][:, p:p + 1],
                                                       in1=k_hi[:, c].bitcast(F32), op0=ALU.add, op1=ALU.subtract).then_inc(unit_out, 1)

                def masked_scores(b, half, a, t, before):
                    if t == 0:
                        dve.wait_ge(mask_in[a], 32 * (half + 1))
                    if before:
                        dve.wait_ge(probsT_in_psum, TB * (b * NP + t - 1))
                    if before:
                        dve.wait_ge(wait_taken, b * NP + t)
                    dve.wait_ge(scores_in_psum, b * NP + t + 1)
                    nc.vector.memset(wait_cell[:], 0.0).then_inc(wait_taken, 1)
                    nc.vector.tensor_tensor_reduce(out=split(scores[:, t % 2], NC), in0=ps_scores[0:PN, :, 0:LC],
                                                   in1=split(mask_sb[:, a], NC), scale=-1.0, scalar=BIG, op0=ALU.add, op1=ALU.min,
                                                   accum_out=shift[:, t % 2:t % 2 + 1]).then_inc(scores_ready, 1)

                def units_rest(b, half, a, slots, at, t, which, **parts):
                    for u in (slots[t][0] + slots[t][1])[which]:
                        unit_rest(units_before(half, a), at, half - 1 if u[0] == "R" else b + 1, u, 1 - a, **parts)

                def batch(b, half, a, slots, at, former=None, beside=None):
                    project = at is not AT_LAST
                    now = (b, half, a, slots, at)
                    for t in range(NP):
                        early, same = READ.get(t, (0, 1))
                        dve.wait_ge(values_done, b * NP + t + 1)
                        dve.wait_ge(probsT_in_psum, TB * (b * NP + t) + 1)
                        nc.vector.tensor_copy(probsT[:, t % 2, 0:TC],
                                              ps_T[0:LT, (TB * t) % 2, 0:TC * PN].rearrange("p (j n) -> p j n", j=TC)).then_inc(probsT_dve, 1)
                        left = None
                        if t > 0:
                            left = (*now, t - 1, slice(READ.get(t - 1, (0, 1))[1], None))
                        elif former:
                            left = (*former, NP - 1, slice(1, None))
                        if left:
                            units_rest(*left, chain=False)
                        units_rest(*now, t, slice(0, early))
                        if t + 2 < NP:
                            masked_scores(b, half, a, t + 2, True)
                        elif project:
                            masked_scores(b + 1, half + a, 1 - a, t + 2 - NP, True)
                        units_rest(*now, t, slice(early, same))
                        if left:
                            units_rest(*left, out=False)
                        if beside:
                            beside(t)
                        if t == 1 and former and former[-1] is AT_R:
                            centre(nc, dve, keep, half - 1)

                nc.vector.memset(keep["credit"][:, 0:1], 0.0).then_inc(unit_out, 2)

                def prepare(n):
                    if n == 1:
                        nc.vector.memset(ones, 1.0).then_inc(ones_set, 1)
                        dve.wait_ge(load["wo"], 16)
                        nc.vector.tensor_reduce(wo_scale[:], wo_raw, AX.X, ALU.max, apply_absolute_value=True).then_inc(wo_steps, 1)
                        dve.wait_ge(load["atom_w"], 16)
                        nc.vector.tensor_reduce(atom_shift[:], atom_w[:], AX.X, ALU.max, negate=True).then_inc(atom_steps, 1)
                        dve.wait_ge(wo_steps, 1)
                        nc.vector.tensor_scalar(wo_scale[:], wo_scale[:], 1.0 / QMAX, QEPS, ALU.mult, ALU.max).then_inc(wo_steps, 1)
                        dve.wait_ge(wo_steps, 2)
                        nc.vector.reciprocal(wo_inv[:], wo_scale[:]).then_inc(wo_steps, 1)
                        for e in range(KT):
                            nc.vector.tensor_scalar(diag[:, e], keep["ident"][:], wo_scale[:, e:e + 1], None, ALU.mult).then_inc(diag_ready, 1)
                        dve.wait_ge(wo_steps, 3)
                        for e in range(KT):
                            nc.vector.tensor_scalar(wo_tmp[:, e], wo_raw[:, e], wo_inv[:, e:e + 1], ROUND, ALU.mult, ALU.add).then_inc(wo_steps, 1)
                        dve.wait_ge(wo_steps, 5)
                        nc.vector.tensor_scalar(wo_tmp, wo_tmp, ROUND, QMAX, ALU.subtract, ALU.min).then_inc(wo_steps, 1)
                        dve.wait_ge(wo_steps, 6)
                        nc.vector.tensor_scalar(wo_int, wo_tmp, -QMAX, None, ALU.max).then_inc(wo_int_ready, 1)
                        dve.wait_ge(prepared_out, W_T)
                        nc.vector.tensor_tensor(keep["wT_lo"][:], split(ps_scores[:, 0], KT), keep["wT_hi"][:].bitcast(F32), ALU.subtract).then_inc(wT_lo_ready, 1)
                        dve.wait_ge(prepared_out, GATE_T)
                        nc.vector.tensor_tensor(keep["gateT_lo"][:], split(ps_out[:, 0:KT * E], KT), keep["gateT_hi"][:].bitcast(F32), ALU.subtract).then_inc(wT_lo_ready, 1)
                    if n == 2:
                        dve.wait_ge(atom_exp, 1)
                        nc.vector.reciprocal(atom_rsum[:], atom_sum[:]).then_inc(atom_steps, 1)
                        dve.wait_ge(atom_steps, 2)
                        nc.vector.tensor_scalar(atom_pn[:], atom_p[:], atom_rsum[:, 0:1], None, ALU.mult).then_inc(atom_steps, 1)
                        dve.wait_ge(gate_exp, 1)
                        nc.vector.tensor_scalar(importance[:], importance[:], 1.0, None, ALU.add).then_inc(gate_steps, 1)
                        dve.wait_ge(gate_steps, 1)
                        nc.vector.reciprocal(importance[:], importance[:]).then_inc(gate_steps, 1)
                    if n == 5:
                        dve.wait_ge(prepared_in_psum, DELTAS)
                        dve.wait_ge(gate_in, 16)
                        g = gate[:, 0:NC * 512].rearrange("p (a b) -> p a b", a=NC)
                        nc.vector.tensor_tensor(g, ps_scores[0:E, 0:NC], g, ALU.mult).then_inc(gate_steps, 1)
                        g = gate[:, NC * 512:NS]
                        nc.vector.tensor_tensor(g, ps_T[0:E, 0], g, ALU.mult).then_inc(gate_steps, 1)
                    if n == 6:
                        dve.wait_ge(w8_hi_ready, 1)
                        nc.vector.tensor_tensor(w8_lo, gate, keep["w_stack"][0:E].bitcast(F32), ALU.subtract).then_inc(w8_lo_ready, 1)

                for n, u in enumerate(FIRST):
                    unit_rest(0, AT_FIRST, 0, u, 0)
                    prepare(PREPARE_AT.get(n, 0))
                    if n in SCORES_AFTER:
                        dve.wait_ge(w8_lo_ready, 1)
                        masked_scores(0, 0, 0, SCORES_AFTER[n], False)
                dve.wait_ge(x1_bo_ready, 1)
                dve.wait_ge(load["bv"], 16)
                def plain(half, a):
                    return 2 * half + a, half, a, UNITS, AT

                def finishing(half):
                    return 2 * half, half, 0, UNITS_R, AT_R

                batch(*plain(0, 0))
                batch(*plain(0, 1), former=plain(0, 0))
                with dve.Fori(1, B // 2 - 1) as i:
                    batch(*finishing(i), former=plain(i - 1, 1))
                    batch(*plain(i, 1), former=finishing(i))
                batch(*finishing(last), former=plain(last - 1, 1))
                def beside(t):
                    if t == 0:
                        columns_on_vector(nc, dve, keep, 0)
                        rows_on_vector(nc, dve, keep)
                    if t == 1:
                        for p in range(NP):
                            dve.wait_ge(k_in[p], 16 * STACK * B)
                    if t in (1, 4):
                        columns_on_vector(nc, dve, keep, {1: 1, 4: 2}[t])
                    if t == 3:
                        shares_on_vector(nc, dve, keep, 0)

                batch(B - 1, last, 1, UNITS_LAST, AT_LAST, former=finishing(last), beside=beside)


def kept(nc, ctx):
    sb = lambda n, s, d=F32: ctx.enter_context(nc.sbuf_tensor(n, s, d))
    return {
        "ident": sb("ident", [P, P]),
        "ident_b": sb("ident_b", [P, P], BF16),
        "sel": sb("sel", [PN, 4, TT]),
        "x1": sb("x1", [TT, NT, D]),
        "k_stack": sb("k_stack", [P, NP, L], F32R),
        "context": sb("ctx_rows", [P, NL * D]),
        "ctx_in": [ctx.enter_context(nc.semaphore(f"ctx_in{c}")) for c in range(NC)],
        "q_stored": ctx.enter_context(nc.semaphore("q_stored")),
        "outT": sb("outT", [P, 2, 2 * PN]),
        "sums": sb("sums", [PN, B, NP]),
        "wkvT": sb("wkvT", [P, 4, KT, D], F32R),
        "xbk": sb("xbk", [P, KT]),
        "credit": sb("credit", [P, 4]),
        "wT_hi": sb("wfT_hi", [P, KT, D], F32R),
        "wT_lo": sb("wfT_lo", [P, KT, D], F32R),
        "wo_intT": sb("wo_intT", [P, KT, D], BF16),
        "wo_scale_row": sb("wo_scale_row", [TT, D]),
        "bv_row": sb("bv_row", [TT, D]),
        "gateT_hi": sb("gateT_hi", [P, KT, E], F32R),
        "gateT_lo": sb("gateT_lo", [P, KT, E], F32R),
        "w_stack": sb("w_stack", [EST * E, NS], F32R),
    }


def kept_later(nc, ctx):
    sb = lambda n, s, d=F32: ctx.enter_context(nc.sbuf_tensor(n, s, d))
    sem = lambda n: ctx.enter_context(nc.semaphore(n))
    return {
        "room": sb("room", [P, 2 * KT * L + 2 * L], F32R),
        "v_sb": sb("v_sb", [P, 2, NL, D]),
        "rsum": sb("rsum", [PN, 2, NP]),
        "r_norm": sb("r_norm", [PN, 2 * NP, PD]),
        "r_sb": sb("r_sb", [TT, D]),
        "r_scale": sb("r_scale", [TT, 1]),
        "r_inv": sb("r_inv", [TT, 1]),
        "r_tmp": sb("r_tmp", [TT, D]),
        "r_int": sb("r_int", [TT, D], BF16),
        "r_intT": sb("r_intT", [P, KT, TT], BF16),
        "resid": sb("resid_x", [TT, D]),
        "stats": sb("stats_x", [TT, 6]),
        "mv": sb("mv_x", [TT, 2]),
        "var_eps": sb("var_eps_x", [TT, NT]),
        "minus_half": sb("minus_half_x", [TT, NT]),
        "rstd": sb("rstd_x", [TT, NT]),
        "r_cell": sb("r_cell", [TT, 1]),
        "logitsT": sb("logitsT", [E, HALF]),
        "logits": sb("logits", [TT, HT, E]),
        "top": sb("top", [TT, HT, 8]),
        "top_i": sb("top_i", [TT, HT, 8], U32),
        "top_f": sb("top_f", [TT, HT, 8]),
        "gap": sb("gap", [TT, HT]),
        "egap": sb("egap", [TT, HT]),
        "den": sb("den", [TT, HT]),
        "route": sb("route", [TT, 2, HT]),
        "hit": sb("hit", [TT, 2, HT, E]),
        "hit_w": sb("hit_w", [TT, 2, HT, E]),
        "shares": sb("shares", [TT, HT, E]),
        "r_steps": sem("r_steps"),
        "r_int_ready": sem("r_int_ready"),
        "var_ready": sem("var_x_ready"),
        "rstd_ready": sem("rstd_x_ready"),
        "half_set": sem("half_set"),
        "channels": sem("channels"),
        "idx_col_in": sem("idx_col_in"),
        "idx_row_in": sem("idx_row_in"),
        "row_steps": sem("row_steps"),
        "column_steps": sem("column_steps"),
        "x2T_hi_ready": sem("x2T_hi_ready"),
        "route_steps": sem("route_steps"),
        "egap_ready": sem("egap_ready"),
        "c_hi_ready": sem("c_hi_ready"),
        "c_stacked": [sem(f"c_stacked{h}") for h in range(2)],
    }


LAG = 3
BUFS = LAG + 1
UNIT = [(h, j) for h in range(2) for j in range(NST)]
HIDDEN_AT = {0: 0, 1: 1, 3: 2, 4: 3, 6: 4, 7: 5, 9: 6, 10: 7, 13: 8}
GAP_AT = 11
DENSE_AT = {0: -1, 1: 15}


def feed_forward_phase(nc, io, keep):
    ctx = ExitStack()
    with ctx:
        sb = lambda n, s, d=F32: ctx.enter_context(nc.sbuf_tensor(n, s, d))
        sem = lambda n: ctx.enter_context(nc.semaphore(n))
        keep["x2T_hi1"] = sb("x2T_hi1", [P, KT, HALF], F32R)
        keep["x2T_lo1"] = sb("x2T_lo1", [P, KT, HALF], F32R)
        keep["c_stack1"] = sb("c_stack1", [EST * E, HALF], F32R)
        e = expert_room(keep)
        pick_c, pick_r = e["pick_c"], e["pick_r"]
        wT_hi, wT_lo, w_stack, x2 = (keep[n] for n in ("wT_hi", "wT_lo", "w_stack", "x1"))
        xg_sb = sb("xg_sb", [P, 2, HALF])
        prod = sb("prod", [P, BUFS, HALF])
        stacks = keep["k_stack"][:].rearrange("p k l -> p (k l)")
        prod_hi, prod_lo = (split(stacks[:, k * BUFS * HALF:(k + 1) * BUFS * HALF], BUFS) for k in range(2))
        ffT = sb("ffT", [P, KT, T])
        resid3 = y_sb = sb("y_sb", [TT, NT, D])
        stats = sb("stats3", [TT, NT, 6])
        mv = sb("mv3", [TT, NT, 2])
        var_eps = sb("var_eps3", [TT, NT])
        rstd = sb("rstd3", [TT, NT])
        ps = ctx.enter_context(nc.psum_tensor("psC", [P, 8, 512], F32))

        late_in_psum = sem("late_in_psum")
        late_out = sem("late_out")
        xg_in_psum = sem("xg_in_psum")
        xg_copied = sem("xg_copied")
        vals_in_psum = sem("vals_in_psum")
        prod_ready = sem("prod_ready")
        prod_hi_ready = sem("prod_hi_ready")
        prod_lo_ready = sem("prod_lo_ready")
        contributed = sem("contributed")
        ff_copied = sem("ff_copied")
        ff_in_psum = sem("ff_in_psum")
        resid3_ready = sem("resid3_ready")
        stats_ready = sem("stats3_ready")
        mv_ready = sem("mv3_ready")
        var_ready = sem("var3_ready")
        rstd_ready = sem("rstd3_ready")
        y_ready = sem("y_ready")
        stored = sem("stored")

        def tiles(h):
            return range(h * HT, (h + 1) * HT)

        with nc.Block() as block:

            @block.sync
            def _(sp):
                stack_shares(sp, keep, 1, late_out, len(HIDDEN))
                for h in range(2):
                    sp.wait_ge(y_ready, (h + 1) * HT)
                    sp.dma_start(io["out"].rearrange("b s d -> (b s) d").rearrange("(i p) d -> p i d", p=TT)[:, h * HT:(h + 1) * HT],
                                 y_sb[:, h * HT:(h + 1) * HT]).then_inc(stored, 16)
                sp.wait_ge(stored, 32)

            @block.gpsimd
            def _(pool):
                for n in range(len(UNIT)):
                    pool.wait_ge(prod_hi_ready, n + 1)
                    nc.gpsimd.tensor_tensor(prod_lo[:, n % BUFS], prod[:, n % BUFS], prod_hi[:, n % BUFS].bitcast(F32), ALU.subtract).then_inc(prod_lo_ready, 1)
                    if n == 4:
                        result_on_gpsimd(nc, pool, keep, NT - 1)
                for h in range(2):
                    g = slice(h * HT, (h + 1) * HT)
                    pool.wait_ge(var_ready, h + 1)
                    nc.gpsimd.tensor_tensor(rstd[:, g], var_eps[:, g], keep["minus_half"][:, g], ALU.pow).then_inc(rstd_ready, 1)

            @block.tensor
            def _(pe):
                def dense(h):
                    x2T_hi, x2T_lo = x2T_parts(keep, h)
                    if h == 1:
                        pe.wait_ge(late_out, len(HIDDEN))
                    for m in range(KT):
                        e = slice(m * P, (m + 1) * P)
                        mm = [t for k in range(KT) for t in ((wT_hi[:, k, e], x2T_hi[:, k]), (wT_hi[:, k, e], x2T_lo[:, k]),
                                                             (wT_lo[:, k, e], x2T_hi[:, k]))]
                        for n, (w, x) in enumerate(mm):
                            nc.tensor.matmul(ps[:, 4 + 2 * h + m, 0:HALF], w, x, start=n == 0, stop=False)

                def gather(n):
                    h, j = UNIT[n]
                    if n >= 2:
                        pe.wait_ge(xg_copied, n - 1)
                    if (h, j) == (1, 0):
                        pe.wait_ge(late_out, 1 + HIDDEN.index(("T", 1, 0)))
                    mm = [(pick_c[:, m, j * P:(j + 1) * P], part[:, m]) for m in range(KT) for part in x2T_parts(keep, h)]
                    for k, (w, x) in enumerate(mm):
                        last = nc.tensor.matmul(ps[:, n % 2, 0:HALF], w, x, start=k == 0, stop=k == len(mm) - 1)
                    last.then_inc(xg_in_psum, 1)

                def values(n):
                    h, j = UNIT[n]
                    if n >= 2:
                        pe.wait_ge(prod_ready, n - 1)
                    if j == 0:
                        pe.wait_ge(keep["c_stacked"][h], 32)
                    nc.tensor.matmul(ps[:, 2 + n % 2, 0:HALF], w_stack[:, j * P:(j + 1) * P], shares_stack(keep, h),
                                     start=True, stop=True).then_inc(vals_in_psum, 1)

                def scatter(n):
                    h, j = UNIT[n]
                    pe.wait_ge(prod_lo_ready, n + 1)
                    for m in range(KT):
                        for part in (prod_hi, prod_lo):
                            last = nc.tensor.matmul(ps[:, 4 + 2 * h + m, 0:HALF], pick_r[:, j, m * P:(m + 1) * P], part[:, n % BUFS],
                                                    start=False, stop=j == NST - 1 and part is prod_lo)
                    last.then_inc(contributed, 1)

                def hidden(k):
                    u, h = HIDDEN[k], 1
                    if k >= 2:
                        pe.wait_ge(late_out, k - 1)
                    if u in (("R", 1, 0), ("R", 3, 0), ("L", 0, 0), ("L", 1, 0)):
                        pe.wait_ge(late_out, k)
                    if u == ("R", 2, 0):
                        pe.wait_ge(keep["r_int_ready"], NT)
                    if u == ("T", 0, 0):
                        pe.wait_ge(keep["r_steps"], NT * R_STEPS)
                    if u == ("C", 0, 0):
                        pe.wait_ge(keep["route_steps"], 2 * ROUTE_STEPS)
                    late_unit_on_tensor(nc, keep, u, h, ps[:, 6 + k % 2]).then_inc(late_in_psum, 1)

                def back(h):
                    pe.wait_ge(ff_copied, KT * (h + 1))
                    for j, i in enumerate(tiles(h)):
                        for m in range(KT):
                            last = nc.tensor.transpose(ps[0:TT, 4 + 2 * h + j // 2, (j % 2) * D + m * P:(j % 2) * D + (m + 1) * P],
                                                       ffT[:, m, i * TT:(i + 1) * TT], keep["ident"][:])
                        if j % 2:
                            last.then_inc(ff_in_psum, 1)

                pe.wait_ge(keep["column_steps"], 1 + KT)
                gather(0)
                gather(1)
                dense(0)
                for n, (h, j) in enumerate(UNIT):
                    if n >= 2:
                        gather(n)
                    values(n)
                    if n >= LAG:
                        if n == LAG:
                            pe.wait_ge(keep["row_steps"], 2 + NST)
                        scatter(n - LAG)
                    if n in HIDDEN_AT:
                        hidden(HIDDEN_AT[n])
                    if n == DENSE_AT[1]:
                        dense(1)
                    if (h, j) == (1, 6):
                        back(0)
                for n in range(len(UNIT) - LAG, len(UNIT)):
                    scatter(n)
                back(1)

            @block.scalar
            def _(act):
                def gathered(n):
                    act.wait_ge(xg_in_psum, n + 1)
                    if n >= 2:
                        act.wait_ge(prod_ready, n - 1)
                    nc.scalar.activation(xg_sb[:, n % 2], ps[:, n % 2, 0:HALF], ACT.Copy).then_inc(xg_copied, 1)

                def hidden(k):
                    u = HIDDEN[k]
                    if u[0] in "TC":
                        act.wait_ge(late_in_psum, k + 1)
                        late_unit_on_scalar(nc, keep, u, 1, ps[:, 6 + k % 2])

                gathered(0)
                gathered(1)
                for n, (h, j) in enumerate(UNIT):
                    act.wait_ge(prod_ready, n + 1)
                    if n >= BUFS:
                        act.wait_ge(contributed, n - BUFS + 1)
                    nc.scalar.activation(prod_hi[:, n % BUFS], prod[:, n % BUFS], ACT.Copy).then_inc(prod_hi_ready, 1)
                    if n in HIDDEN_AT:
                        hidden(HIDDEN_AT[n])
                    if n == GAP_AT:
                        gap_on_scalar(nc, act, keep, 1)
                    if n + 2 < len(UNIT):
                        gathered(n + 2)
                    if (h, j) == (1, 3):
                        act.wait_ge(contributed, NST)
                        for m in range(KT):
                            nc.scalar.activation(ffT[:, m, half_of(0)], ps[:, 4 + m, 0:HALF], ACT.Copy).then_inc(ff_copied, 1)
                act.wait_ge(contributed, 2 * NST)
                for m in range(KT):
                    nc.scalar.activation(ffT[:, m, half_of(1)], ps[:, 6 + m, 0:HALF], ACT.Copy).then_inc(ff_copied, 1)

            @block.vector
            def _(dve):
                def normalise(h):
                    for j, i in enumerate(tiles(h)):
                        if j % 2 == 0:
                            dve.wait_ge(ff_in_psum, 2 * h + j // 2 + 1)
                        nc.vector.tensor_tensor(resid3[:, i], ps[0:TT, 4 + 2 * h + j // 2, (j % 2) * D:(j % 2 + 1) * D], x2[:, i], ALU.add).then_inc(resid3_ready, 1)
                    g = slice(h * HT, (h + 1) * HT)
                    for i in tiles(h):
                        dve.wait_ge(resid3_ready, i + 1)
                        nc.vector.bn_stats(stats[:, i], resid3[:, i]).then_inc(stats_ready, 1)
                    for i in tiles(h):
                        dve.wait_ge(stats_ready, i + 1)
                        nc.vector.bn_aggr(mv[:, i], stats[:, i]).then_inc(mv_ready, 1)
                    dve.wait_ge(mv_ready, (h + 1) * HT)
                    nc.vector.tensor_scalar(var_eps[:, g], mv[:, g, 1], LN_EPS, None, ALU.add).then_inc(var_ready, 1)

                def centred(h):
                    dve.wait_ge(rstd_ready, h + 1)
                    for i in tiles(h):
                        nc.vector.tensor_scalar(y_sb[:, i], resid3[:, i], mv[:, i, 0:1], rstd[:, i:i + 1], ALU.subtract, ALU.mult).then_inc(y_ready, 1)

                for n, (h, j) in enumerate(UNIT):
                    dve.wait_ge(xg_copied, n + 1)
                    dve.wait_ge(vals_in_psum, n + 1)
                    if n >= BUFS:
                        dve.wait_ge(prod_lo_ready, n - BUFS + 1)
                    nc.vector.tensor_tensor(prod[:, n % BUFS], ps[:, 2 + n % 2, 0:HALF], xg_sb[:, n % 2], ALU.mult).then_inc(prod_ready, 1)
                    if n in HIDDEN_AT:
                        k = HIDDEN_AT[n]
                        late_unit_on_vector(nc, dve, keep, HIDDEN[k], 1, ps[:, 6 + k % 2], NT - 1, late_in_psum, k + 1, late_out, k + 1)
                    if n == 5:
                        centre(nc, dve, keep, NT - 1)
                    if n == GAP_AT + 1:
                        shares_on_vector(nc, dve, keep, 1)
                    if (h, j) == (1, 12):
                        normalise(0)
                normalise(1)
                for h in range(2):
                    centred(h)


def build_program(nc, io):
    with ExitStack() as ctx:
        keep = kept(nc, ctx)
        self_attention_phase(nc, io, keep)
        keep.update(kept_later(nc, ctx))
        cross_attention_phase(nc, io, keep)
        feed_forward_phase(nc, io, keep)


_INS = ["x", "ctx_2048", "mask_BxSxS2_ff0",
        "L0_attn_Wq", "L0_attn_bq", "L0_attn_Wk", "L0_attn_bk", "L0_attn_Wv", "L0_attn_bv", "L0_attn_Wo", "L0_attn_bo",
        "L0_xattn_wq", "L0_xattn_bq", "L0_xattn_wk", "L0_xattn_bk", "L0_xattn_wv", "L0_xattn_bv", "L0_xattn_wo", "L0_xattn_bo",
        "L0_ffn_gate_w", "L0_ffn_W", "L0_ffn_atoms", "L0_ffn_expert_atom_weights", "L0_ffn_importance", "L0_ffn_mask_idx"]


def kernel(**inputs):
    import numpy as np
    import concourse.bacc as bacc
    from concourse import mybir as mb
    from concourse.bass_utils import run_bass_kernel_spmd

    nc = bacc.Bacc("TRN2", target_bir_lowering=False, num_devices=1)
    arrays, io = {}, {}
    for name in _INS:
        a = np.ascontiguousarray(inputs[name])
        arrays[f"in_{name}"] = a
        io[name] = nc.dram_tensor(f"in_{name}", a.shape, mb.dt.from_np(a.dtype), kind="ExternalInput").ap()
    io["ctx"], io["mask"] = io["ctx_2048"], io["mask_BxSxS2_ff0"]
    io["out"] = nc.dram_tensor("out_0", (B, S, D), F32, kind="ExternalOutput").ap()
    for name in ("q_hi", "q_lo"):
        io[name] = nc.dram_tensor(name, (KT, P, B, PN), F32, kind="Internal").ap()
    io["gate"] = nc.dram_tensor("gate", (E, NS), F32, kind="Internal").ap()
    build_program(nc, io)
    r = run_bass_kernel_spmd(nc, [arrays], core_ids=[0])
    return r.results[0]["out_0"]
```
